# Optimizing a Trainium2 kernel written in Bass

```python
import numpy as np
import jax
import jax.numpy as jnp

def _softmax(x, axis=-1):
    return jax.nn.softmax(x, axis=axis)

def _gelu(x):
    return jax.nn.gelu(x, approximate=True)

def _silu(x):
    return jax.nn.silu(x)

def _sigmoid(x):
    return jax.nn.sigmoid(x)

def _layernorm(x, axis=-1, eps=1e-05):
    m = jnp.mean(x, axis=axis, keepdims=True)
    v = jnp.var(x, axis=axis, keepdims=True)
    return (x - m) / jnp.sqrt(v + eps)

def _scatter_add(tgt, idx, src, axis=0):
    return tgt.at[idx].add(src)

def _segment_sum(src, seg, n):
    return jax.ops.segment_sum(src, seg, n)
kernel_name = 'mk_perceiver_d2_seqx_r4_cfc33b'

def setup_inputs(seed: int=0):
    np.random.seed(seed)
    _w = jnp.asarray

    def _rec_inputs():
        import jax
        import jax.numpy as jnp
        _rk = jax.random.key(seed)
        x = 7.22e-05 + 1 * jax.random.normal(jax.random.fold_in(_rk, 1), (8, 64, 256), jnp.float32)
        _lenS = 64 - jax.random.randint(jax.random.fold_in(_rk, 7), (8,), 0, max(1, 64 // 4) + 1, jnp.int32)
        _lenS2 = 256 - jax.random.randint(jax.random.fold_in(_rk, 8), (8,), 0, max(1, 256 // 4) + 1, jnp.int32)
        _ctx_1024P = jax.random.normal(jax.random.fold_in(_rk, 11), (8, 16, 256), jnp.float32)
        _ctx_1024c = jax.random.dirichlet(jax.random.fold_in(_rk, 511), 0.3 * jnp.ones((16,), jnp.float32), (8, 256))
        _ctx_1024t = jnp.einsum('bsk,bkd->bsd', _ctx_1024c, _ctx_1024P)
        _ctx_1024t = _ctx_1024t * jax.lax.rsqrt(jnp.mean(jnp.square(_ctx_1024t)) + 1e-12) * 0.953939
        ctx_1024 = 2.81802e-05 + 1.00001 * (_ctx_1024t + 0.3 * jax.random.normal(jax.random.fold_in(_rk, 611), (8, 256, 256), jnp.float32))
        _validS = jnp.arange(64)[None, :] < _lenS[:, None]
        _validS2 = jnp.arange(256)[None, :] < _lenS2[:, None]
        _causal = jnp.tril(jnp.ones((64, 64), dtype=bool))
        mask_Bx1xSxS2_ff1 = jnp.where(jnp.ones((8, 1, 64, 256), dtype=bool), 1.0, 0.0).astype(jnp.float32)
        return (x, ctx_1024, mask_Bx1xSxS2_ff1)
    x, ctx_1024, mask_Bx1xSxS2_ff1 = _rec_inputs()

    def _L0_xattn_setup():
        import jax, jax.numpy as jnp
        import numpy as np
        B, NT, NM, C, H, FF = (8, 256, 512, 256, 8, 1024)

        def _ln(x, g, b):
            m = x.mean(-1, keepdims=True)
            v = jnp.mean((x - m) ** 2, axis=-1, keepdims=True)
            return (x - m) / jnp.sqrt(v + 1e-05) * g + b
        key = jax.random.key(seed)
        ks = jax.random.split(key, 8)
        w = lambda k, shape, s=0.02: jax.random.normal(k, shape, dtype=jnp.float32) * s
        return {'tgt': jax.random.normal(ks[0], (B, NT, C), dtype=jnp.float32), 'memory': jax.random.normal(ks[1], (B, NM, C), dtype=jnp.float32), 'qkv_w': w(ks[2], (3 * C, C)), 'qkv_b': jnp.zeros((3 * C,), jnp.float32), 'sa_out_w': w(ks[3], (C, C)), 'sa_out_b': jnp.zeros((C,), jnp.float32), 'in_proj_w': w(ks[4], (3 * C, C)), 'in_proj_b': jnp.zeros((3 * C,), jnp.float32), 'mha_out_w': w(ks[5], (C, C)), 'mha_out_b': jnp.zeros((C,), jnp.float32), 'lin1_w': w(ks[6], (FF, C)), 'lin1_b': jnp.zeros((FF,), jnp.float32), 'lin2_w': w(ks[7], (C, FF)), 'lin2_b': jnp.zeros((C,), jnp.float32), 'ln1_g': jnp.ones((C,), jnp.float32), 'ln1_b': jnp.zeros((C,), jnp.float32), 'ln2_g': jnp.ones((C,), jnp.float32), 'ln2_b': jnp.zeros((C,), jnp.float32), 'ln3_g': jnp.ones((C,), jnp.float32), 'ln3_b': jnp.zeros((C,), jnp.float32)}
    _L0_xattn_all = _L0_xattn_setup()
    _L0_xattn_in = {k: v for k, v in _L0_xattn_all.items() if k in ('qkv_w', 'qkv_b', 'sa_out_w', 'sa_out_b', 'in_proj_w', 'in_proj_b', 'mha_out_w', 'mha_out_b', 'lin1_w', 'lin1_b', 'lin2_w', 'lin2_b', 'ln1_g', 'ln1_b', 'ln2_g', 'ln2_b', 'ln3_g', 'ln3_b')}
    del _L0_xattn_all

    def _L0_attn_setup():
        import jax, jax.numpy as jnp
        import numpy as np
        D_MODEL = 256
        NUM_HEADS = 4
        KEY_DIM = 256
        VALUE_DIM = 512
        HEAD_QK = KEY_DIM // NUM_HEADS
        HEAD_V = VALUE_DIM // NUM_HEADS
        EPS = 1e-05
        CHUNK = 64
        ROPE_BASE = 10000.0

        def apply_rotary(q, k):
            n, d = (q.shape[1], q.shape[-1])
            inv_freq = 1.0 / ROPE_BASE ** (jnp.arange(0, d, 2, dtype=jnp.float32) / d)
            t = jnp.arange(n, dtype=jnp.float32)
            freqs = jnp.outer(t, inv_freq)
            cos = jnp.cos(freqs)[None, :, None, :]
            sin = jnp.sin(freqs)[None, :, None, :]

            def rot(x):
                x1, x2 = jnp.split(x, 2, axis=-1)
                return jnp.concatenate([x1 * cos - x2 * sin, x2 * cos + x1 * sin], axis=-1)
            return (rot(q), rot(k))

        def chunk_retention(q, k, v, gamma, chunk=CHUNK):
            B, H, N, dk = q.shape
            dv = v.shape[-1]
            NC = N // chunk
            qc = jnp.moveaxis(q.reshape(B, H, NC, chunk, dk), 2, 0)
            kc = jnp.moveaxis(k.reshape(B, H, NC, chunk, dk), 2, 0)
            vc = jnp.moveaxis(v.reshape(B, H, NC, chunk, dv), 2, 0)
            idx = jnp.arange(chunk)
            rel = idx[:, None] - idx[None, :]
            D = jnp.where(rel >= 0, gamma[:, None, None] ** rel, 0.0)
            cross_q = (gamma[:, None] ** (idx + 1))[None, :, :, None]
            cross_k = (gamma[:, None] ** (chunk - 1 - idx))[None, :, :, None]
            gC = (gamma ** chunk)[None, :, None, None]

            def step(S, qkv):
                qb, kb, vb = qkv
                attn = jnp.einsum('bhid,bhjd->bhij', qb, kb) * D[None]
                o_intra = jnp.einsum('bhij,bhjd->bhid', attn, vb)
                o_inter = jnp.einsum('bhid,bhde->bhie', qb * cross_q, S)
                S_new = gC * S + jnp.einsum('bhjd,bhje->bhde', kb * cross_k, vb)
                return (S_new, o_intra + o_inter)
            S0 = jnp.zeros((B, H, dk, dv), dtype=q.dtype)
            _, o = jax.lax.scan(step, S0, (qc, kc, vc))
            return jnp.moveaxis(o, 0, 2).reshape(B, H, N, dv)

        def rmsnorm(x, w):
            var = jnp.mean(x * x, axis=-1, keepdims=True)
            return x * jax.lax.rsqrt(var + EPS) * w
        key = jax.random.key(seed)
        ks = jax.random.split(key, 7)
        B, N = (2, 1024)
        s = 0.02
        return {'x': jax.random.normal(ks[0], (B, N, D_MODEL), dtype=jnp.float32), 'Wq': jax.random.normal(ks[1], (D_MODEL, D_MODEL), dtype=jnp.float32) * s, 'Wk': jax.random.normal(ks[2], (D_MODEL, D_MODEL), dtype=jnp.float32) * s, 'Wv': jax.random.normal(ks[3], (D_MODEL, VALUE_DIM), dtype=jnp.float32) * s, 'Wg': jax.random.normal(ks[4], (D_MODEL, VALUE_DIM), dtype=jnp.float32) * s, 'Wo': jax.random.normal(ks[5], (VALUE_DIM, D_MODEL), dtype=jnp.float32) * s, 'gn_weight': jnp.ones((HEAD_V,), dtype=jnp.float32)}
    _L0_attn_all = _L0_attn_setup()
    _L0_attn_in = {k: v for k, v in _L0_attn_all.items() if k in ('Wq', 'Wk', 'Wv', 'Wg', 'Wo', 'gn_weight')}
    del _L0_attn_all

    def _L0_ffn_setup():
        import jax, jax.numpy as jnp
        import numpy as np
        NUM_EXPERTS = 8
        HIDDEN = 256
        D_FF = 1024
        SCALE = 0.8
        SPARSITY = 0.1

        def _perturb_attractive(w, scale=SCALE, sparsity=SPARSITY):
            a = jnp.abs(w)
            flat = a.ravel()
            n = flat.shape[0]
            k = max(1, int(n * sparsity / 2))
            s = jnp.sort(flat)
            thr_bot = s[k - 1]
            thr_top = s[n - k]
            tier = jnp.where(a >= thr_top, -1.0, jnp.where(a <= thr_bot, 1.0, 0.0))
            return w + scale * w * tier

        def _stack_expert_params(w):
            pw = _perturb_attractive(w)
            return jnp.concatenate([w[None], jnp.broadcast_to(pw, (NUM_EXPERTS - 1,) + w.shape)], axis=0)
        key = jax.random.key(seed)
        ks = jax.random.split(key, 6)
        B, S, H, F, E = (2, 512, HIDDEN, D_FF, NUM_EXPERTS)
        return {'x': jax.random.normal(ks[0], (B, S, H), dtype=jnp.float32), 'W1': jax.random.normal(ks[1], (H, F), dtype=jnp.float32) * (1.0 / np.sqrt(H)), 'b1': jax.random.normal(ks[2], (F,), dtype=jnp.float32) * 0.02, 'W2': jax.random.normal(ks[3], (F, H), dtype=jnp.float32) * (1.0 / np.sqrt(F)), 'b2': jax.random.normal(ks[4], (H,), dtype=jnp.float32) * 0.02, 'ln_gamma': jnp.ones((H,), dtype=jnp.float32), 'ln_beta': jnp.zeros((H,), dtype=jnp.float32), 'Wr': jax.random.normal(ks[5], (H, E), dtype=jnp.float32) * (1.0 / np.sqrt(H)), 'br': jnp.zeros((E,), dtype=jnp.float32)}
    _L0_ffn_all = _L0_ffn_setup()
    _L0_ffn_in = {k: v for k, v in _L0_ffn_all.items() if k in ('W1', 'b1', 'W2', 'b2', 'ln_gamma', 'ln_beta', 'Wr', 'br')}
    del _L0_ffn_all

    def _L1_xattn_setup():
        import jax, jax.numpy as jnp
        import numpy as np
        N_HEADS, N_UNITS = (16, 256)
        D_K = N_UNITS // N_HEADS
        B, S = (2, 512)
        key = jax.random.key(seed)
        ks = jax.random.split(key, 12)
        s = 1.0 / np.sqrt(N_UNITS)
        return {'query': jax.random.normal(ks[0], (B, S, N_UNITS), jnp.float32), 'key': jax.random.normal(ks[1], (B, S, N_UNITS), jnp.float32), 'value': jax.random.normal(ks[2], (B, S, N_UNITS), jnp.float32), 'mask': jnp.ones((B, 1, S, S), jnp.float32), 'Wq': jax.random.normal(ks[3], (N_HEADS, N_UNITS, D_K), jnp.float32) * s, 'bq': jax.random.normal(ks[4], (N_HEADS, D_K), jnp.float32) * s, 'Wk': jax.random.normal(ks[5], (N_HEADS, N_UNITS, D_K), jnp.float32) * s, 'bk': jax.random.normal(ks[6], (N_HEADS, D_K), jnp.float32) * s, 'Wv': jax.random.normal(ks[7], (N_HEADS, N_UNITS, D_K), jnp.float32) * s, 'bv': jax.random.normal(ks[8], (N_HEADS, D_K), jnp.float32) * s, 'Wo': jax.random.normal(ks[9], (N_UNITS, N_UNITS), jnp.float32) * s, 'bo': jax.random.normal(ks[10], (N_UNITS,), jnp.float32) * s}
    _L1_xattn_all = _L1_xattn_setup()
    _L1_xattn_in = {k: v for k, v in _L1_xattn_all.items() if k in ('Wq', 'bq', 'Wk', 'bk', 'Wv', 'bv', 'Wo', 'bo')}
    del _L1_xattn_all

    def _L1_attn_setup():
        import math
        import jax, jax.numpy as jnp
        import numpy as np
        NUM_BUCKETS = 32
        MAX_DISTANCE = 128
        B, T, E, H, D = (2, 512, 256, 16, 64)
        INIT_SCALE = 0.1

        def _relative_position_bucket(rel, num_buckets=NUM_BUCKETS, max_distance=MAX_DISTANCE):
            nb = num_buckets // 2
            buckets = (rel > 0).astype(jnp.int32) * nb
            rel_abs = jnp.abs(rel)
            max_exact = nb // 2
            is_small = rel_abs < max_exact
            val_large = max_exact + (jnp.log(jnp.maximum(rel_abs, 1).astype(jnp.float32) / max_exact) / math.log(max_distance / max_exact) * (nb - max_exact)).astype(jnp.int32)
            val_large = jnp.minimum(val_large, nb - 1)
            return buckets + jnp.where(is_small, rel_abs, val_large)
        key = jax.random.key(seed)
        ks = jax.random.split(key, 6)
        x = jax.random.normal(ks[0], (B, T, E), dtype=jnp.float32)
        Wq = jax.random.normal(ks[1], (H * D, E), dtype=jnp.float32) * INIT_SCALE
        Wk = jax.random.normal(ks[2], (H * D, E), dtype=jnp.float32) * INIT_SCALE
        Wv = jax.random.normal(ks[3], (H * D, E), dtype=jnp.float32) * INIT_SCALE
        Wo = jax.random.normal(ks[4], (E, H * D), dtype=jnp.float32) * INIT_SCALE
        rel_emb = jax.random.normal(ks[5], (NUM_BUCKETS, H), dtype=jnp.float32)
        return {'x': x, 'Wq': Wq, 'Wk': Wk, 'Wv': Wv, 'Wo': Wo, 'rel_emb': rel_emb}
    _L1_attn_all = _L1_attn_setup()
    _L1_attn_in = {k: v for k, v in _L1_attn_all.items() if k in ('Wq', 'Wk', 'Wv', 'Wo', 'rel_emb')}
    del _L1_attn_all

    def _L1_ffn_setup():
        import jax, jax.numpy as jnp
        import numpy as np
        B, S, D = (2, 512, 256)
        DFF = 512
        E_FFN = 8
        E_ZERO = 4
        E_TOT = E_FFN + E_ZERO
        TOP_K = 2
        key = jax.random.key(seed)
        k1, k2, k3, k4 = jax.random.split(key, 4)
        x = jax.random.normal(k1, (B, S, D), dtype=jnp.float32)
        gate_w = jax.random.normal(k2, (E_TOT, D), dtype=jnp.float32) * (1.0 / np.sqrt(D))
        expert_bias = jnp.zeros((E_TOT,), dtype=jnp.float32)
        w1 = jax.random.normal(k3, (E_FFN, DFF, D), dtype=jnp.float32) * (1.0 / np.sqrt(D))
        w2 = jax.random.normal(k4, (E_FFN, D, DFF), dtype=jnp.float32) * (1.0 / np.sqrt(DFF))
        return {'x': x, 'gate_w': gate_w, 'expert_bias': expert_bias, 'w1': w1, 'w2': w2}
    _L1_ffn_all = _L1_ffn_setup()
    _L1_ffn_in = {k: v for k, v in _L1_ffn_all.items() if k in ('gate_w', 'expert_bias', 'w1', 'w2')}
    del _L1_ffn_all
    return {'x': x, 'ctx_1024': ctx_1024, 'mask_Bx1xSxS2_ff1': mask_Bx1xSxS2_ff1, 'L0_xattn_qkv_w': _L0_xattn_in['qkv_w'], 'L0_xattn_qkv_b': _L0_xattn_in['qkv_b'], 'L0_xattn_sa_out_w': _L0_xattn_in['sa_out_w'], 'L0_xattn_sa_out_b': _L0_xattn_in['sa_out_b'], 'L0_xattn_in_proj_w': _L0_xattn_in['in_proj_w'], 'L0_xattn_in_proj_b': _L0_xattn_in['in_proj_b'], 'L0_xattn_mha_out_w': _L0_xattn_in['mha_out_w'], 'L0_xattn_mha_out_b': _L0_xattn_in['mha_out_b'], 'L0_xattn_lin1_w': _L0_xattn_in['lin1_w'], 'L0_xattn_lin1_b': _L0_xattn_in['lin1_b'], 'L0_xattn_lin2_w': _L0_xattn_in['lin2_w'], 'L0_xattn_lin2_b': _L0_xattn_in['lin2_b'], 'L0_xattn_ln1_g': _L0_xattn_in['ln1_g'], 'L0_xattn_ln1_b': _L0_xattn_in['ln1_b'], 'L0_xattn_ln2_g': _L0_xattn_in['ln2_g'], 'L0_xattn_ln2_b': _L0_xattn_in['ln2_b'], 'L0_xattn_ln3_g': _L0_xattn_in['ln3_g'], 'L0_xattn_ln3_b': _L0_xattn_in['ln3_b'], 'L0_attn_Wq': _L0_attn_in['Wq'], 'L0_attn_Wk': _L0_attn_in['Wk'], 'L0_attn_Wv': _L0_attn_in['Wv'], 'L0_attn_Wg': _L0_attn_in['Wg'], 'L0_attn_Wo': _L0_attn_in['Wo'], 'L0_attn_gn_weight': _L0_attn_in['gn_weight'], 'L0_ffn_W1': _L0_ffn_in['W1'], 'L0_ffn_b1': _L0_ffn_in['b1'], 'L0_ffn_W2': _L0_ffn_in['W2'], 'L0_ffn_b2': _L0_ffn_in['b2'], 'L0_ffn_ln_gamma': _L0_ffn_in['ln_gamma'], 'L0_ffn_ln_beta': _L0_ffn_in['ln_beta'], 'L0_ffn_Wr': _L0_ffn_in['Wr'], 'L0_ffn_br': _L0_ffn_in['br'], 'L1_xattn_Wq': _L1_xattn_in['Wq'], 'L1_xattn_bq': _L1_xattn_in['bq'], 'L1_xattn_Wk': _L1_xattn_in['Wk'], 'L1_xattn_bk': _L1_xattn_in['bk'], 'L1_xattn_Wv': _L1_xattn_in['Wv'], 'L1_xattn_bv': _L1_xattn_in['bv'], 'L1_xattn_Wo': _L1_xattn_in['Wo'], 'L1_xattn_bo': _L1_xattn_in['bo'], 'L1_attn_Wq': _L1_attn_in['Wq'], 'L1_attn_Wk': _L1_attn_in['Wk'], 'L1_attn_Wv': _L1_attn_in['Wv'], 'L1_attn_Wo': _L1_attn_in['Wo'], 'L1_attn_rel_emb': _L1_attn_in['rel_emb'], 'L1_ffn_gate_w': _L1_ffn_in['gate_w'], 'L1_ffn_expert_bias': _L1_ffn_in['expert_bias'], 'L1_ffn_w1': _L1_ffn_in['w1'], 'L1_ffn_w2': _L1_ffn_in['w2']}

def reference(x, ctx_1024, mask_Bx1xSxS2_ff1, L0_xattn_qkv_w, L0_xattn_qkv_b, L0_xattn_sa_out_w, L0_xattn_sa_out_b, L0_xattn_in_proj_w, L0_xattn_in_proj_b, L0_xattn_mha_out_w, L0_xattn_mha_out_b, L0_xattn_lin1_w, L0_xattn_lin1_b, L0_xattn_lin2_w, L0_xattn_lin2_b, L0_xattn_ln1_g, L0_xattn_ln1_b, L0_xattn_ln2_g, L0_xattn_ln2_b, L0_xattn_ln3_g, L0_xattn_ln3_b, L0_attn_Wq, L0_attn_Wk, L0_attn_Wv, L0_attn_Wg, L0_attn_Wo, L0_attn_gn_weight, L0_ffn_W1, L0_ffn_b1, L0_ffn_W2, L0_ffn_b2, L0_ffn_ln_gamma, L0_ffn_ln_beta, L0_ffn_Wr, L0_ffn_br, L1_xattn_Wq, L1_xattn_bq, L1_xattn_Wk, L1_xattn_bk, L1_xattn_Wv, L1_xattn_bv, L1_xattn_Wo, L1_xattn_bo, L1_attn_Wq, L1_attn_Wk, L1_attn_Wv, L1_attn_Wo, L1_attn_rel_emb, L1_ffn_gate_w, L1_ffn_expert_bias, L1_ffn_w1, L1_ffn_w2):
    import jax
    import jax.numpy as jnp

    def _L0_xattn_ref(tgt, memory, qkv_w, qkv_b, sa_out_w, sa_out_b, in_proj_w, in_proj_b, mha_out_w, mha_out_b, lin1_w, lin1_b, lin2_w, lin2_b, ln1_g, ln1_b, ln2_g, ln2_b, ln3_g, ln3_b):
        import jax, jax.numpy as jnp
        import numpy as np
        B, NT, NM, C, H, FF = (8, 256, 512, 256, 8, 1024)

        def _ln(x, g, b):
            m = x.mean(-1, keepdims=True)
            v = jnp.mean((x - m) ** 2, axis=-1, keepdims=True)
            return (x - m) / jnp.sqrt(v + 1e-05) * g + b
        Bx, N, Cx = tgt.shape
        qkv = tgt @ qkv_w.T + qkv_b
        q, k, v = jnp.split(qkv, 3, axis=-1)
        scores = jnp.einsum('bnc,bmc->bnm', q, k) * jnp.sqrt(jnp.float32(Cx))
        diag = jnp.eye(N, dtype=bool)
        scores = jnp.where(diag[None, :, :], scores, -jnp.inf)
        attn = jax.nn.softmax(scores, axis=-1)
        sa = jnp.einsum('bnm,bmc->bnc', attn, v) @ sa_out_w.T + sa_out_b
        x = _ln(tgt + sa, ln1_g, ln1_b)
        d = Cx // H
        wq, wk, wv = jnp.split(in_proj_w, 3, axis=0)
        bq, bk, bv = jnp.split(in_proj_b, 3, axis=0)
        qh = (x @ wq.T + bq).reshape(Bx, N, H, d).transpose(0, 2, 1, 3)
        kh = (memory @ wk.T + bk).reshape(Bx, -1, H, d).transpose(0, 2, 1, 3)
        vh = (memory @ wv.T + bv).reshape(Bx, -1, H, d).transpose(0, 2, 1, 3)
        a = jax.nn.softmax(jnp.einsum('bhnd,bhmd->bhnm', qh, kh) / jnp.sqrt(jnp.float32(d)), axis=-1)
        ca = jnp.einsum('bhnm,bhmd->bhnd', a, vh).transpose(0, 2, 1, 3).reshape(Bx, N, Cx)
        ca = ca @ mha_out_w.T + mha_out_b
        x = _ln(x + ca, ln2_g, ln2_b)
        ff = jax.nn.relu(x @ lin1_w.T + lin1_b) @ lin2_w.T + lin2_b
        return _ln(x + ff, ln3_g, ln3_b)

    def _L0_attn_ref(x, Wq, Wk, Wv, Wg, Wo, gn_weight):
        import jax, jax.numpy as jnp
        import numpy as np
        D_MODEL = 256
        NUM_HEADS = 4
        KEY_DIM = 256
        VALUE_DIM = 512
        HEAD_QK = KEY_DIM // NUM_HEADS
        HEAD_V = VALUE_DIM // NUM_HEADS
        EPS = 1e-05
        CHUNK = 64
        ROPE_BASE = 10000.0

        def apply_rotary(q, k):
            n, d = (q.shape[1], q.shape[-1])
            inv_freq = 1.0 / ROPE_BASE ** (jnp.arange(0, d, 2, dtype=jnp.float32) / d)
            t = jnp.arange(n, dtype=jnp.float32)
            freqs = jnp.outer(t, inv_freq)
            cos = jnp.cos(freqs)[None, :, None, :]
            sin = jnp.sin(freqs)[None, :, None, :]

            def rot(x):
                x1, x2 = jnp.split(x, 2, axis=-1)
                return jnp.concatenate([x1 * cos - x2 * sin, x2 * cos + x1 * sin], axis=-1)
            return (rot(q), rot(k))

        def chunk_retention(q, k, v, gamma, chunk=CHUNK):
            B, H, N, dk = q.shape
            dv = v.shape[-1]
            NC = N // chunk
            qc = jnp.moveaxis(q.reshape(B, H, NC, chunk, dk), 2, 0)
            kc = jnp.moveaxis(k.reshape(B, H, NC, chunk, dk), 2, 0)
            vc = jnp.moveaxis(v.reshape(B, H, NC, chunk, dv), 2, 0)
            idx = jnp.arange(chunk)
            rel = idx[:, None] - idx[None, :]
            D = jnp.where(rel >= 0, gamma[:, None, None] ** rel, 0.0)
            cross_q = (gamma[:, None] ** (idx + 1))[None, :, :, None]
            cross_k = (gamma[:, None] ** (chunk - 1 - idx))[None, :, :, None]
            gC = (gamma ** chunk)[None, :, None, None]

            def step(S, qkv):
                qb, kb, vb = qkv
                attn = jnp.einsum('bhid,bhjd->bhij', qb, kb) * D[None]
                o_intra = jnp.einsum('bhij,bhjd->bhid', attn, vb)
                o_inter = jnp.einsum('bhid,bhde->bhie', qb * cross_q, S)
                S_new = gC * S + jnp.einsum('bhjd,bhje->bhde', kb * cross_k, vb)
                return (S_new, o_intra + o_inter)
            S0 = jnp.zeros((B, H, dk, dv), dtype=q.dtype)
            _, o = jax.lax.scan(step, S0, (qc, kc, vc))
            return jnp.moveaxis(o, 0, 2).reshape(B, H, N, dv)

        def rmsnorm(x, w):
            var = jnp.mean(x * x, axis=-1, keepdims=True)
            return x * jax.lax.rsqrt(var + EPS) * w
        B, N, _ = x.shape
        H = NUM_HEADS
        q1 = (x @ Wq).reshape(B, N, H, HEAD_QK)
        k1 = (x @ Wk).reshape(B, N, H, HEAD_QK)
        q1, k1 = apply_rotary(q1, k1)
        q = jnp.transpose(q1, (0, 2, 1, 3)) * HEAD_QK ** (-0.5)
        k = jnp.transpose(k1, (0, 2, 1, 3))
        v = jnp.transpose((x @ Wv).reshape(B, N, H, HEAD_V), (0, 2, 1, 3))
        gamma = 1.0 - jnp.exp2(-5.0 - jnp.arange(H, dtype=jnp.float32))
        o = chunk_retention(q, k, v, gamma)
        o = jnp.transpose(o, (0, 2, 1, 3))
        o = rmsnorm(o, gn_weight)
        g = jax.nn.silu(x @ Wg)
        o = o.reshape(B, N, VALUE_DIM) * g
        return o @ Wo

    def _L0_ffn_ref(x, W1, b1, W2, b2, ln_gamma, ln_beta, Wr, br):
        import jax, jax.numpy as jnp
        import numpy as np
        NUM_EXPERTS = 8
        HIDDEN = 256
        D_FF = 1024
        SCALE = 0.8
        SPARSITY = 0.1

        def _perturb_attractive(w, scale=SCALE, sparsity=SPARSITY):
            a = jnp.abs(w)
            flat = a.ravel()
            n = flat.shape[0]
            k = max(1, int(n * sparsity / 2))
            s = jnp.sort(flat)
            thr_bot = s[k - 1]
            thr_top = s[n - k]
            tier = jnp.where(a >= thr_top, -1.0, jnp.where(a <= thr_bot, 1.0, 0.0))
            return w + scale * w * tier

        def _stack_expert_params(w):
            pw = _perturb_attractive(w)
            return jnp.concatenate([w[None], jnp.broadcast_to(pw, (NUM_EXPERTS - 1,) + w.shape)], axis=0)
        mu = jnp.mean(x, axis=-1, keepdims=True)
        var = jnp.mean(jnp.square(x - mu), axis=-1, keepdims=True)
        h = (x - mu) * jax.lax.rsqrt(var + 1e-05) * ln_gamma + ln_beta
        logits = jnp.einsum('bsh,he->bse', h, Wr) + br
        probs = jax.nn.softmax(logits, axis=-1)
        W1s = _stack_expert_params(W1)
        b1s = _stack_expert_params(b1)
        W2s = _stack_expert_params(W2)
        b2s = _stack_expert_params(b2)
        pre = jnp.einsum('bsh,ehf->besf', x, W1s) + b1s[None, :, None, :]
        act = jax.nn.gelu(pre)
        y = jnp.einsum('besf,efh->besh', act, W2s) + b2s[None, :, None, :]
        out = jnp.einsum('bse,besh->bsh', probs, y)
        return out

    def _L1_xattn_ref(query, key, value, mask, Wq, bq, Wk, bk, Wv, bv, Wo, bo):
        import jax, jax.numpy as jnp
        import numpy as np
        N_HEADS, N_UNITS = (16, 256)
        D_K = N_UNITS // N_HEADS
        B, S = (2, 512)
        q = jnp.einsum('bsd,hdk->bhsk', query, Wq) + bq[None, :, None, :]
        k = jnp.einsum('bsd,hdk->bhsk', key, Wk) + bk[None, :, None, :]
        v = jnp.einsum('bsd,hdk->bhsk', value, Wv) + bv[None, :, None, :]
        scores = jnp.einsum('bhqk,bhmk->bhqm', q, k) / jnp.sqrt(jnp.asarray(D_K, q.dtype))
        scores = jnp.where(mask == 0.0, jnp.asarray(-1000000000.0, scores.dtype), scores)
        attn = jax.nn.softmax(scores, axis=-1)
        h = jnp.einsum('bhqm,bhmk->bhqk', attn, v)
        h = h.transpose(0, 2, 1, 3).reshape(query.shape[0], query.shape[1], N_UNITS)
        return h @ Wo + bo

    def _L1_attn_ref(x, Wq, Wk, Wv, Wo, rel_emb):
        import math
        import jax, jax.numpy as jnp
        import numpy as np
        NUM_BUCKETS = 32
        MAX_DISTANCE = 128
        B, T, E, H, D = (2, 512, 256, 16, 64)
        INIT_SCALE = 0.1

        def _relative_position_bucket(rel, num_buckets=NUM_BUCKETS, max_distance=MAX_DISTANCE):
            nb = num_buckets // 2
            buckets = (rel > 0).astype(jnp.int32) * nb
            rel_abs = jnp.abs(rel)
            max_exact = nb // 2
            is_small = rel_abs < max_exact
            val_large = max_exact + (jnp.log(jnp.maximum(rel_abs, 1).astype(jnp.float32) / max_exact) / math.log(max_distance / max_exact) * (nb - max_exact)).astype(jnp.int32)
            val_large = jnp.minimum(val_large, nb - 1)
            return buckets + jnp.where(is_small, rel_abs, val_large)
        b, t, _ = x.shape
        scale = D ** (-0.5)
        q = jnp.einsum('bte,fe->btf', x, Wq).reshape(b, t, H, D).transpose(0, 2, 1, 3)
        k = jnp.einsum('bte,fe->btf', x, Wk).reshape(b, t, H, D).transpose(0, 2, 1, 3)
        v = jnp.einsum('bte,fe->btf', x, Wv).reshape(b, t, H, D).transpose(0, 2, 1, 3)
        attn = jnp.einsum('bhtd,bhsd->bhts', q, k) * scale
        pos = jnp.arange(t)
        rel = pos[:, None] - pos[None, :]
        buckets = _relative_position_bucket(rel)
        bias = rel_emb[buckets]
        attn = attn + bias.transpose(2, 0, 1)[None]
        causal = jnp.triu(jnp.ones((t, t), dtype=bool), k=1)
        attn = jnp.where(causal[None, None], -jnp.inf, attn)
        attn = jax.nn.softmax(attn, axis=-1)
        out = jnp.einsum('bhts,bhsd->bhtd', attn, v).transpose(0, 2, 1, 3).reshape(b, t, H * D)
        return jnp.einsum('btf,ef->bte', out, Wo)

    def _L1_ffn_ref(x, gate_w, expert_bias, w1, w2):
        import jax, jax.numpy as jnp
        import numpy as np
        B, S, D = (2, 512, 256)
        DFF = 512
        E_FFN = 8
        E_ZERO = 4
        E_TOT = E_FFN + E_ZERO
        TOP_K = 2
        logits = jnp.einsum('btd,ed->bte', x, gate_w) + expert_bias
        topk_logits, topk_idx = jax.lax.top_k(logits, TOP_K)
        topk_w = jax.nn.softmax(topk_logits, axis=-1)
        onehot = jax.nn.one_hot(topk_idx, E_TOT, dtype=x.dtype)
        w = jnp.einsum('btk,btke->bte', topk_w, onehot)
        w_ffn = w[..., :E_FFN]
        w_zero = jnp.sum(w[..., E_FFN:], axis=-1)
        h = jax.nn.silu(jnp.einsum('btd,efd->btef', x, w1))
        y = jnp.einsum('btef,edf->bted', h, w2)
        out = jnp.einsum('bte,bted->btd', w_ffn, y) + w_zero[..., None] * x
        return out
    x = x + _L0_xattn_ref(_layernorm(x, axis=-1), ctx_1024, L0_xattn_qkv_w, L0_xattn_qkv_b, L0_xattn_sa_out_w, L0_xattn_sa_out_b, L0_xattn_in_proj_w, L0_xattn_in_proj_b, L0_xattn_mha_out_w, L0_xattn_mha_out_b, L0_xattn_lin1_w, L0_xattn_lin1_b, L0_xattn_lin2_w, L0_xattn_lin2_b, L0_xattn_ln1_g, L0_xattn_ln1_b, L0_xattn_ln2_g, L0_xattn_ln2_b, L0_xattn_ln3_g, L0_xattn_ln3_b)
    x = x + _L0_attn_ref(_layernorm(x, axis=-1), L0_attn_Wq, L0_attn_Wk, L0_attn_Wv, L0_attn_Wg, L0_attn_Wo, L0_attn_gn_weight)
    x = x + _L0_ffn_ref(_layernorm(x, axis=-1), L0_ffn_W1, L0_ffn_b1, L0_ffn_W2, L0_ffn_b2, L0_ffn_ln_gamma, L0_ffn_ln_beta, L0_ffn_Wr, L0_ffn_br)
    x = x + _L1_xattn_ref(_layernorm(x, axis=-1), ctx_1024, ctx_1024, mask_Bx1xSxS2_ff1, L1_xattn_Wq, L1_xattn_bq, L1_xattn_Wk, L1_xattn_bk, L1_xattn_Wv, L1_xattn_bv, L1_xattn_Wo, L1_xattn_bo)
    x = x + _L1_attn_ref(_layernorm(x, axis=-1), L1_attn_Wq, L1_attn_Wk, L1_attn_Wv, L1_attn_Wo, L1_attn_rel_emb)
    x = x + _L1_ffn_ref(_layernorm(x, axis=-1), L1_ffn_gate_w, L1_ffn_expert_bias, L1_ffn_w1, L1_ffn_w2)
    return x

_drawn_inputs = setup_inputs


def setup_inputs(seed=0):
    import zlib

    import numpy as np

    out = dict(_drawn_inputs(seed))
    spreads = {'L0_xattn_qkv_b': (0.0, 0.283),
     'L0_xattn_sa_out_b': (0.0, 0.1),
     'L0_xattn_in_proj_b': (0.0, 0.1),
     'L0_xattn_mha_out_b': (0.0, 0.1),
     'L0_xattn_lin1_b': (0.0, 0.1),
     'L0_xattn_lin2_b': (0.0, 0.1),
     'L0_xattn_ln1_g': (1.0, 0.2),
     'L0_xattn_ln1_b': (0.0, 0.1),
     'L0_xattn_ln2_g': (1.0, 0.2),
     'L0_xattn_ln2_b': (0.0, 0.1),
     'L0_xattn_ln3_g': (1.0, 0.2),
     'L0_xattn_ln3_b': (0.0, 0.1),
     'L0_attn_gn_weight': (1.0, 0.6),
     'L0_ffn_ln_gamma': (1.0, 0.6),
     'L0_ffn_ln_beta': (0.0, 0.8),
     'L0_ffn_br': (0.0, 2.0),
     'L1_ffn_expert_bias': (0.0, 0.268)}
    factors = {'L0_ffn_b1': 5.289, 'L0_ffn_b2': 3.475, 'L1_xattn_bq': 4.145, 'L1_xattn_bk': 64.0}
    for name, (base, spread) in spreads.items():
        noise = np.random.default_rng([zlib.crc32(name.encode()), seed]).standard_normal(out[name].shape)
        drawn = base * np.exp(spread * noise) if base else spread * noise
        out[name] = jnp.asarray(drawn.astype(out[name].dtype))
    for name, factor in factors.items():
        out[name] = (out[name] * factor).astype(out[name].dtype)
    return out
```

```python
from contextlib import ExitStack

import numpy as np

import concourse.bass as bass
from concourse import mybir

F32 = mybir.dt.float32
BF16 = mybir.dt.bfloat16
U16 = mybir.dt.uint16
I32 = mybir.dt.int32
U32 = mybir.dt.uint32
ALU = mybir.AluOpType
ACT = mybir.ActivationFunctionType
AX = mybir.AxisListType

P = 128
NB, SQ, SK, D = 8, 64, 256, 256
T = NB * SQ
NT = T // P
NH = 2
HT = T // NH
EPS = 1e-5
NE = 8
NSTEP1, NSTEP2 = 15, 16
LIN, DFF = 1024, 512
NEG = -1.0e9
CAUSAL_NEG = -1.0e30

COLS = ["v_b", "q_b", "k_b", "cv_b", "lin1_b", "ffn_b1", "ffn_b2", "xq_b", "xk_b", "xv_b"]
COL_N = {"v_b": 2, "q_b": 2, "k_b": 2, "cv_b": 2, "lin1_b": 8, "ffn_b1": 8, "ffn_b2": 2, "xq_b": 2,
         "xk_b": 2, "xv_b": 2}
COL_AT = {n: sum(COL_N[m] for m in COLS[:i]) for i, n in enumerate(COLS)}
NCOL = sum(COL_N.values())
ROWS = ["so_b", "ln1_g", "ln1_b", "mo_b", "ln2_g", "ln2_b", "lin2_b", "ln3_g", "ln3_b", "gn", "f_g",
        "f_b", "ffn_b2", "xo_b", "br", "eb"]
ROW_N = {n: D for n in ROWS} | {"gn": 128, "br": 8, "eb": 12}
ROW_AT = {n: sum(ROW_N[m] for m in ROWS[:i]) for i, n in enumerate(ROWS)}
NROW = sum(ROW_N.values())


def job_order(upto):
    H = range(NH)
    out = []

    def search(s):
        if s < NSTEP1 + NSTEP2 + 1:
            out.extend([("cnt", s), ("tot", s)])

    def attention(p, n_s, steps):
        for i in range(NB + 1):
            if i < NB:
                out.extend([(p + "K", i), (p + "V", i)])
                for s in range(n_s):
                    out.append((p + "S", i, s))
                    if i > 0:
                        out.append((p + "PT", i - 1, s))
            else:
                out.extend([(p + "PT", i - 1, s) for s in range(n_s)])
            if i > 0:
                out.append((p + "O", i - 1))
            if i < NB:
                for s in range(steps):
                    search(i * steps + s)

    def ffn(one, two, n_e, n_f):
        seq = [(e, h) for e in range(n_e) for h in H]
        for i in range(len(seq) + 1):
            if i < len(seq):
                out.extend([(one, *seq[i], f) for f in range(n_f)])
            if i > 0:
                out.append((two, *seq[i - 1]))

    for n in ("aT0", "av", "aso", "aT1", "aq"):
        out.extend([(n, h) for h in H])
    attention("a", 2, 4)
    for n in ("aOT", "amo", "aT2"):
        out.extend([(n, h) for h in H])
    ffn("af1", "af2", 1, 4)
    if upto >= 2:
        out.extend([("bT", h) for h in H])
        for h in H:
            out.extend([(n, h) for n in ("bq", "bqs", "bk", "bks")])
        for t in range(NT):
            out.extend([("bv", t), ("bg", t)])
        for t in range(NT + 1):
            if t < NT:
                out.extend([("bS", t, 0), ("bS", t, 1)])
            if t > 0:
                out.extend([("bO", t - 1, 0), ("bO", t - 1, 1)])
        out.extend([("bOT", t) for t in range(NT)])
        out.extend([("bwo", h) for h in H])
    if upto >= 3:
        out.extend([("cT", h) for h in H])
        out.extend([("cT2", h) for h in H])
        out.extend([("cr", h) for h in H])
        ffn("c1", "c2", 2, 4)
    if upto >= 4:
        out.extend([("dT", h) for h in H])
        out.extend([("dq", h) for h in H])
        attention("d", 4, 0)
        for n in ("dOT", "dmo"):
            out.extend([(n, h) for h in H])
    if upto >= 5:
        out.extend([("eT", h) for h in H])
        for h in H:
            out.extend([("eq", h, c) for c in range(4)])
            out.extend([("ek", h, c) for c in range(4)])
            for t in (2 * h, 2 * h + 1):
                out.extend([("ev", t, 0), ("ev", t, 1)])
            for t in (2 * h, 2 * h + 1):
                for bp in range(2):
                    for hp in range(2):
                        out.append(("eS", t, bp, hp))
            for t in (2 * h, 2 * h + 1):
                out.extend([("ePT", t, 0), ("ePT", t, 1)])
                for bp in range(2):
                    for n in range(2):
                        out.append(("eO", t, bp, n))
            for t in (2 * h, 2 * h + 1):
                out.extend([("eOT", t, 0), ("eOT", t, 1)])
            out.append(("ewo", h))
    if upto >= 6:
        out.extend([("fT", h) for h in H])
        out.extend([("fg", h) for h in H])
        ffn("f1", "f2", NE, 2)
    return out


def build(nc, A, out, upto=6):
    with ExitStack() as ctx:
        _build(nc, A, out, upto, ctx)


def _build(nc, A, out, upto, ctx):
    def sb(name, shape, dt=F32):
        return ctx.enter_context(nc.sbuf_tensor(name, shape, dt))

    sems = {}

    def S(name):
        if name not in sems:
            sems[name] = ctx.enter_context(nc.semaphore(name))
        return sems[name]

    JOBS = {name: (i % 8, i // 8) for i, name in enumerate(job_order(upto))}
    psum = ctx.enter_context(nc.psum_tensor("psum", [P, 8, 512], F32))
    full = [S(f"bank{b}_full") for b in range(8)]
    free = [S(f"bank{b}_free") for b in range(8)]

    X = sb("X", [P, NT, D])
    Z = sb("Z", [P, NT, D])
    Y = sb("Y", [P, NT, D])
    FT = sb("FT", [P, 2, T])
    FV = sb("FV", [P, 2, T])
    FK = sb("FK", [P, 2, T])
    BIG = sb("BIG", [P, 8192])
    RA = sb("RA", [P, 7168])
    RB = sb("RB", [P, 5120])
    RC = sb("RC", [P, 8192])
    CTX = sb("CTX", [P, 2, NB * SK])
    KT = sb("KT", [P, 2, 2, SK])
    VB = sb("VB", [P, 2, 2, D])
    QD = sb("QD", [P, 2, 2, 8, SQ])
    PR = sb("PR", [P, 4, 512])
    PT = sb("PT", [P, 4, 512])
    rows = sb("rows", [P, NROW])
    cols = sb("cols", [P, NCOL])
    ident = sb("ident", [P, P])
    hmask = sb("hmask", [P, 12])
    rot = sb("rot", [P, 2, SQ])
    decay = sb("decay", [P, 4, SQ])
    iota12 = sb("iota12", [P, 12])
    Wr = sb("Wr", [P, 2, 8])
    gw = sb("gw", [P, 2, 12])
    kwant = sb("kwant", [P, 8])
    onesb = sb("onesb", [P, 1], BF16)
    onesf = sb("onesf", [P, P])
    st = sb("st", [P, NT, 6])
    mv = sb("mv", [P, NT, 2])
    lnv = sb("lnv", [P, NT])
    rstd = sb("rstd", [P, NT])
    nmx = sb("nmx", [P, 2, 8])
    sums = sb("sums", [P, 2, 8])
    rinv = sb("rinv", [P, 2, 8])
    rmx = sb("rmx", [P, 2, 8])
    ms = sb("ms", [P, NT, 4])
    eps = sb("eps", [P, 1])
    sm = sb("sm", [P, 256])
    cnt = sb("cnt", [P, 8])
    cur = sb("cur", [P, 8])
    cand = sb("cand", [P, 8])
    kleft = sb("kleft", [P, 8])
    thr = sb("thr", [P, 2, 8])
    bkey = sb("bkey", [P, 40], U16)
    lgt = sb("lgt", [P, 4, 12])
    m8 = sb("m8", [P, 4, 8])
    i8 = sb("i8", [P, 4, 8], U32)
    i8f = sb("i8f", [P, 4, 8])
    wgt = sb("wgt", [P, 4, 12])
    rany = sb("rany", [P, NB])
    bp_row = sb("bp_row", [P, D])
    bp_col = sb("bp_col", [P, 8])

    def part(region, at, *shape):
        n = int(np.prod(shape))
        v = region[:, at:at + n]
        if len(shape) == 2:
            v = v.rearrange("p (a b) -> p a b", a=shape[0])
        if len(shape) == 3:
            v = v.rearrange("p (a b c) -> p a b c", a=shape[0], b=shape[1])
        return v

    a_wv, a_so, a_wq, a_wk, a_wcv, a_mo = (part(RA, 512 * i, 2, 256) for i in range(6))
    a_l1 = part(RA, 3072, 2, 1024)
    a_l2 = part(RA, 5120, 8, 256)
    b_wq, b_wqs, b_wk, b_wks = (part(RB, 512 * i, 2, 256) for i in range(4))
    b_wv, b_wg = part(RB, 2048, 2, 512), part(RB, 3072, 2, 512)
    b_wo = part(RB, 4096, 4, 256)
    c_w1 = [part(RC, 0, 2, 1024), part(RC, 4096, 2, 1024)]
    c_w2 = [part(RC, 2048, 8, 256), part(RC, 6144, 8, 256)]
    d_wq, d_wk, d_wv, d_wo = (part(RA, 512 * i, 2, 256) for i in range(4))
    d_mask = part(RB, 0, NB, SK)
    e_wq, e_wk, e_wv = (part(RC, 2048 * i, 2, 1024) for i in range(3))
    e_wo = part(RC, 6144, 8, 256)
    e_bias = part(RB, 2048, 8, SQ)
    e_causal = part(RB, 2560, SQ)
    f_w1 = [part(RA, 2048 + 2048 * i, 2, 512) for i in range(2)]
    f_w2 = [part(RA, 3072 + 2048 * i, 4, 256) for i in range(2)]
    a_hid = part(BIG, 0, 8, T)
    b_v, b_g = part(BIG, 0, NT, 512), part(BIG, 2048, NT, 512)
    b_o, b_ot = part(BIG, 4096, NT, 512), part(BIG, 6144, 4, T)
    c_hid = [part(BIG, 0, 8, T), part(BIG, 4096, 8, T)]
    e_q, e_k = part(BIG, 0, 8, HT), part(BIG, 2048, 8, HT)
    e_v, e_o = part(BIG, 4096, 2, 1024), part(BIG, 6144, 2, 1024)
    f_hid = [part(BIG, 0, 4, T), part(BIG, 2048, 4, T)]
    KEY = BIG[:, 4096:8192].bitcast(U16).rearrange("p (q n) -> p q n", q=4)
    smask = RC[:, 4096:8192].bitcast(BF16).rearrange("p (q n) -> p q n", q=4)

    def row(name, n=None):
        return rows[:, ROW_AT[name]:ROW_AT[name] + (n or ROW_N[name])]

    def col(name, i):
        return cols[:, COL_AT[name] + i:COL_AT[name] + i + 1]

    def bank(name):
        return psum[:, JOBS[name][0], :]

    def over(ap, n):
        return ap.unsqueeze(1).to_broadcast([ap.shape[0], n, ap.shape[1]])

    def each(ap, n):
        return ap.unsqueeze(2).to_broadcast([ap.shape[0], ap.shape[1], n])

    block = ctx.enter_context(nc.Block())

    def claim(pe, name):
        b, u = JOBS[name]
        if u:
            pe.wait_ge(free[b], u)
        return psum[:, b, :]

    def filled(name):
        return full[JOBS[name][0]]

    def taken(name):
        return free[JOBS[name][0]]

    def finished(eng, name):
        b, u = JOBS[name]
        eng.wait_ge(full[b], u + 1)
        return psum[:, b, :]

    def written(eng, name):
        b, u = JOBS[name]
        eng.wait_ge(free[b], u + 1)

    half = [slice(h * HT, (h + 1) * HT) for h in range(NH)]
    tiles = [slice(2 * h, 2 * h + 2) for h in range(NH)]
    N_SEARCH = NSTEP1 + NSTEP2 + 1

    @block.sync
    def _(sp):
        def load(dst, name, src=None):
            sp.dma_start(dst, A[name] if src is None else src).then_inc(S("ld_" + name), 16)

        for t in range(NT):
            sp.dma_start(X[:, t, :], A["x"][t * P:(t + 1) * P, :]).then_inc(S(f"ld_x{t // 2}"), 16)
        load(ident[:], "ident")
        load(cols[:], "cols")
        load(a_wv, "v_w")
        load(rows[:], "rows", A["rows"].to_broadcast([P, NROW]))
        load(a_so, "so_w")
        load(a_wq, "q_w")
        load(a_wk, "k_w")
        load(CTX[:], "ctx")
        load(a_wcv, "cv_w")
        load(hmask[:], "hmask")
        load(c_w1[0], "ffn_w1")
        load(c_w2[0], "ffn_w2")
        load(kwant[:], "kwant")
        load(a_mo, "mo_w")
        load(a_l1, "lin1_w")
        load(a_l2, "lin2_w")
        if upto >= 2:
            load(b_wq, "rq_w")
            load(b_wqs, "rqs_w")
            load(b_wk, "rk_w")
            load(b_wks, "rks_w")
            load(b_wv, "rv_w")
            load(b_wg, "rg_w")
            load(b_wo, "ro_w")
            load(rot[:], "rot")
            load(decay[:], "decay")
        if upto >= 3:
            load(Wr[:], "Wr")
            load(gw[:], "gw")
            load(iota12[:], "iota12")
        if upto >= 4:
            finished(sp, ("af2", 0, 1))
            load(d_wq, "xq_w")
            load(d_wk, "xk_w")
            load(d_wv, "xv_w")
            load(d_wo, "xo_w")
            finished(sp, ("bwo", 1))
            for hp in range(2):
                sp.dma_start(d_mask[hp * 64:hp * 64 + 64], A["mask"]).then_inc(S("ld_mask"), 16)
            load(e_bias, "rbias")
            load(e_causal, "causal")
        if upto >= 5:
            finished(sp, ("c2", 1, 1))
            load(e_wq, "eq_w")
            load(e_wk, "ek_w")
            load(e_wv, "ev_w")
            load(e_wo, "eo_w")
        if upto >= 6:
            for e in range(NE):
                if e >= 2:
                    finished(sp, ("f2", e - 2, 1))
                sp.dma_start(f_w1[e % 2], A["fw1"][e]).then_inc(S(f"ld_f{e % 2}"), 16)
                sp.dma_start(f_w2[e % 2], A["fw2"][e]).then_inc(S(f"ld_f{e % 2}"), 16)
        for h in range(NH):
            if upto == 1:
                sp.wait_ge(S("x_final"), h + 1)
            else:
                written(sp, {2: ("bwo", h), 3: ("c2", 1, h), 4: ("dmo", h), 5: ("ewo", h), 6: ("f2", NE - 1, h)}[upto])
            for t in (2 * h, 2 * h + 1):
                sp.dma_start(out[t * P:(t + 1) * P, :], X[:, t, :]).then_inc(S("stored"), 16)
        sp.wait_ge(S("stored"), 16 * NT)

    @block.tensor
    def _(pe):
        def loaded(*names):
            for n in names:
                pe.wait_ge(S("ld_" + n), 16)

        def to_fm(name, h, src, nk=2):
            ps = claim(pe, (name, h)).rearrange("p (c n) -> p c n", c=2)
            for t in (2 * h, 2 * h + 1):
                for c in range(2):
                    ins = pe.transpose(ps[:, c, (t % 2) * P:(t % 2 + 1) * P], src[:, t, c * P:(c + 1) * P],
                                       ident[:])
            ins.then_inc(filled((name, h)), 1)

        def fm(name, w, c0, src, tok):
            ps = claim(pe, name).rearrange("p (c n) -> p c n", c=2)
            for c in range(2):
                for k in range(2):
                    ins = pe.matmul(ps[:, c, :], w[:, k, (c0 + c) * P:(c0 + c + 1) * P], src[:, k, tok],
                                    start=(k == 0), stop=(k == 1))
            ins.then_inc(filled(name), 1)

        def tm(name, src, h, w, nk, n=256, t0=None):
            ps = claim(pe, name).rearrange("p (c n) -> p c n", c=2)
            for j in range(2):
                at = ((2 * h + j) if t0 is None else j) * P
                for k in range(nk):
                    ins = pe.matmul(ps[:, j, :n], src[:, k, at:at + P], w[:, k, :n],
                                    start=(k == 0), stop=(k == nk - 1))
            ins.then_inc(filled(name), 1)

        def search(s):
            if s >= N_SEARCH:
                return
            ps = claim(pe, ("cnt", s))
            for q in range(4):
                pe.wait_ge(S("smask_ready"), 4 * s + q + 1)
                for i in range(16):
                    ins = pe.matmul(ps[:, q:q + 1], smask[:, q, i * P:(i + 1) * P], onesb[:],
                                    start=(i == 0), stop=(i == 15))
            ins.then_inc(filled(("cnt", s)), 1)
            ps = claim(pe, ("tot", s))
            written(pe, ("cnt", s))
            pe.matmul(ps[:, 0:8], onesf[:], cnt[:], start=True, stop=True).then_inc(filled(("tot", s)), 1)

        def attention(p, wk, wv, n_s, steps):
            w = D // (4 * n_s) * 2
            per = 2 if n_s == 2 else 4

            def p_ready(p, b, s):
                if p == "a":
                    written(pe, ("aS", b, s))
                else:
                    pe.wait_ge(S("d_p"), n_s * b + s + 1)

            def pv(b):
                ps = claim(pe, (p + "O", b))
                for s in range(n_s):
                    for pr in range(2):
                        j = 2 * s + pr
                        for kc in range(2):
                            ins = pe.matmul(ps[:, j * w:(j + 1) * w],
                                            PT[:, (n_s * b + s) % 4, pr * 256 + kc * P:pr * 256 + (kc + 1) * P],
                                            VB[:, b % 2, kc, j * w:(j + 1) * w], start=(kc == 0), stop=(kc == 1))
                ins.then_inc(filled((p + "O", b)), 1)

            def p_transpose(b, s):
                ps = claim(pe, (p + "PT", b, s))
                p_ready(p, b, s)
                for pr in range(2):
                    for kc in range(2):
                        at = pr * 256 + kc * P
                        ins = pe.transpose(ps[:, at:at + P], PR[:, (n_s * b + s) % 4, at:at + P], ident[:])
                ins.then_inc(filled((p + "PT", b, s)), 1)

            for i in range(NB + 1):
                if i < NB:
                    fm((p + "K", i), wk, 0, CTX, slice(i * SK, (i + 1) * SK))
                    ps = claim(pe, (p + "V", i)).rearrange("p (c n) -> p c n", c=2)
                    for kt in range(2):
                        for k in range(2):
                            at = i * SK + kt * P
                            ins = pe.matmul(ps[:, kt, :], CTX[:, k, at:at + P], wv[:, k, :],
                                            start=(k == 0), stop=(k == 1))
                    ins.then_inc(filled((p + "V", i)), 1)
                    pe.wait_ge(S(p + "_qd_ready"), i + 1)
                    written(pe, (p + "K", i))
                    for s in range(n_s):
                        ps = claim(pe, (p + "S", i, s))
                        for pr in range(2):
                            j = 2 * s + pr
                            c, jj = j // per, j % per
                            ins = pe.matmul(ps[:, pr * 256:(pr + 1) * 256], QD[:, i % 2, c, 2 * jj:2 * jj + 2, :],
                                            KT[:, i % 2, c, :], start=True, stop=True)
                        ins.then_inc(filled((p + "S", i, s)), 1)
                        if i > 0:
                            p_transpose(i - 1, s)
                else:
                    for s in range(n_s):
                        p_transpose(i - 1, s)
                if i > 0:
                    for s in range(n_s):
                        written(pe, (p + "PT", i - 1, s))
                    written(pe, (p + "V", i - 1))
                    pv(i - 1)
                if i < NB:
                    for s in range(steps):
                        search(i * steps + s)

        def ffn(one, two, n_e, n_f, hid, w1, w2, before):
            seq = [(e, h) for e in range(n_e) for h in range(NH)]
            for i in range(len(seq) + 1):
                if i < len(seq):
                    e, h = seq[i]
                    before(e, h)
                    for f in range(n_f):
                        fm((one, e, h, f), w1[e % 2], 2 * f, FT, half[h])
                if i > 0:
                    e, h = seq[i - 1]
                    for f in range(n_f):
                        written(pe, (one, e, h, f))
                    tm((two, e, h), hid[e % 2], h, w2[e % 2], 2 * n_f)

        loaded("ident", "v_w")
        for h in range(NH):
            pe.wait_ge(S("a_z0"), h + 1)
            to_fm("aT0", h, Z)
        for h in range(NH):
            written(pe, ("aT0", h))
            fm(("av", h), a_wv, 0, FT, half[h])
        loaded("so_w")
        for h in range(NH):
            written(pe, ("av", h))
            tm(("aso", h), FV, h, a_so, 2)
        for h in range(NH):
            pe.wait_ge(S("a_z1"), h + 1)
            to_fm("aT1", h, Z)
        loaded("q_w")
        for h in range(NH):
            written(pe, ("aT1", h))
            fm(("aq", h), a_wq, 0, FT, half[h])
        loaded("k_w", "cv_w", "ctx")
        pe.wait_ge(S("ones_ready"), 2)
        attention("a", a_wk, a_wcv, 2, 4)
        for h in range(NH):
            written(pe, ("aO", 4 * h + 3))
            to_fm("aOT", h, Y)
        loaded("mo_w")
        for h in range(NH):
            written(pe, ("aOT", h))
            tm(("amo", h), FT, h, a_mo, 2)
        for h in range(NH):
            pe.wait_ge(S("a_z2"), h + 1)
            to_fm("aT2", h, Z)
        loaded("lin1_w", "lin2_w")
        ffn("af1", "af2", 1, 4, [a_hid], [a_l1], [a_l2],
            lambda e, h: written(pe, ("aT2", h)))

        if upto >= 2:
            for h in range(NH):
                pe.wait_ge(S("b_z"), h + 1)
                to_fm("bT", h, Z)
            loaded("rq_w", "rqs_w", "rk_w", "rks_w")
            for h in range(NH):
                written(pe, ("bT", h))
                for n, w in (("bq", b_wq), ("bqs", b_wqs), ("bk", b_wk), ("bks", b_wks)):
                    fm((n, h), w, 0, FT, half[h])
            loaded("rv_w", "rg_w")
            for t in range(NT):
                for n, w in (("bv", b_wv), ("bg", b_wg)):
                    ps = claim(pe, (n, t))
                    for k in range(2):
                        ins = pe.matmul(ps, FT[:, k, t * P:(t + 1) * P], w[:, k, :], start=(k == 0), stop=(k == 1))
                    ins.then_inc(filled((n, t)), 1)
            for t in range(NT + 1):
                if t < NT:
                    if t % 2 == 0:
                        pe.wait_ge(S("b_qk"), 2 * (t // 2 + 1))
                    for hp in range(2):
                        ps = claim(pe, ("bS", t, hp)).rearrange("p (c n) -> p c n", n=SQ)
                        for bp in range(2):
                            tok = slice(t * P + bp * 64, t * P + bp * 64 + 64)
                            for c in range(2):
                                ins = pe.matmul(ps[bp * 64:bp * 64 + 64, c, :], FK[hp * 64:hp * 64 + 64, c, tok],
                                                FV[hp * 64:hp * 64 + 64, c, tok], start=True, stop=True)
                        ins.then_inc(filled(("bS", t, hp)), 1)
                if t > 0:
                    for hp in range(2):
                        written(pe, ("bS", t - 1, hp))
                    written(pe, ("bv", t - 1))
                    for bp in range(2):
                        ps = claim(pe, ("bO", t - 1, bp))
                        for hd in range(4):
                            at = slice(bp * 64, bp * 64 + 64)
                            ins = pe.matmul(ps[at, hd * P:(hd + 1) * P], PR[at, t - 1, hd * SQ:(hd + 1) * SQ],
                                            b_v[at, t - 1, hd * P:(hd + 1) * P], start=True, stop=True)
                        ins.then_inc(filled(("bO", t - 1, bp)), 1)
            for t in range(NT):
                ps = claim(pe, ("bOT", t))
                pe.wait_ge(S("b_gated"), t + 1)
                for c in range(4):
                    ins = pe.transpose(ps[:, c * P:(c + 1) * P], b_o[:, t, c * P:(c + 1) * P], ident[:])
                ins.then_inc(filled(("bOT", t)), 1)
            loaded("ro_w")
            for h in range(NH):
                for t in (2 * h, 2 * h + 1):
                    written(pe, ("bOT", t))
                tm(("bwo", h), b_ot, h, b_wo, 4)

        if upto >= 3:
            for h in range(NH):
                pe.wait_ge(S("c_z"), h + 1)
                to_fm("cT", h, Z)
            for h in range(NH):
                pe.wait_ge(S("c_y"), h + 1)
                to_fm("cT2", h, Y)
            loaded("Wr", "ffn_w1", "ffn_w2")
            for h in range(NH):
                written(pe, ("cT2", h))
                tm(("cr", h), FV, h, Wr, 2, 8)

            def c_before(e, h):
                written(pe, ("cT", h))
                if e == 1:
                    pe.wait_ge(S("perturbed"), 2)
            ffn("c1", "c2", 2, 4, c_hid, c_w1, c_w2, c_before)

        if upto >= 4:
            for h in range(NH):
                pe.wait_ge(S("d_z"), h + 1)
                to_fm("dT", h, Z)
            loaded("xq_w", "xk_w", "xv_w")
            for h in range(NH):
                written(pe, ("dT", h))
                fm(("dq", h), d_wq, 0, FT, half[h])
            attention("d", d_wk, d_wv, 4, 0)
            loaded("xo_w")
            for h in range(NH):
                written(pe, ("dO", 4 * h + 3))
                to_fm("dOT", h, Y)
            for h in range(NH):
                written(pe, ("dOT", h))
                tm(("dmo", h), FT, h, d_wo, 2)

        if upto >= 5:
            for h in range(NH):
                pe.wait_ge(S("e_z"), h + 1)
                to_fm("eT", h, Z)
            loaded("eq_w", "ek_w", "ev_w", "eo_w")
            for h in range(NH):
                written(pe, ("eT", h))
                for n, w in (("eq", e_wq), ("ek", e_wk)):
                    for c in range(4):
                        fm((n, h, c), w, 2 * c, FT, half[h])
                for t in (2 * h, 2 * h + 1):
                    for n in range(2):
                        ps = claim(pe, ("ev", t, n))
                        for k in range(2):
                            ins = pe.matmul(ps, FT[:, k, t * P:(t + 1) * P], e_wv[:, k, n * 512:(n + 1) * 512],
                                            start=(k == 0), stop=(k == 1))
                        ins.then_inc(filled(("ev", t, n)), 1)
                for c in range(4):
                    written(pe, ("eq", h, c))
                    written(pe, ("ek", h, c))
                for t in (2 * h, 2 * h + 1):
                    for bp in range(2):
                        tok = slice((t % 2) * P + bp * 64, (t % 2) * P + bp * 64 + 64)
                        for hp in range(2):
                            ps = claim(pe, ("eS", t, bp, hp)).rearrange("p (c n) -> p c n", n=SQ)
                            at = slice(hp * 64, hp * 64 + 64)
                            for pr in range(8):
                                ins = pe.matmul(ps[at, pr, :], e_q[at, pr, tok], e_k[at, pr, tok],
                                                start=True, stop=True)
                            ins.then_inc(filled(("eS", t, bp, hp)), 1)
                for t in (2 * h, 2 * h + 1):
                    pe.wait_ge(S("e_p"), t + 1)
                    for s in range(2):
                        ps = claim(pe, ("ePT", t, s))
                        for i in range(4):
                            pr = 4 * s + i
                            src = PR[:, 2 * (t % 2):2 * (t % 2) + 2, :].rearrange("p a n -> p (a n)")
                            ins = pe.transpose(ps[:, i * P:(i + 1) * P], src[:, pr * P:(pr + 1) * P], ident[:])
                        ins.then_inc(filled(("ePT", t, s)), 1)
                    for n in range(2):
                        written(pe, ("ev", t, n))
                        written(pe, ("ePT", t, n))
                    for bp in range(2):
                        at = slice(bp * 64, bp * 64 + 64)
                        for n in range(2):
                            ps = claim(pe, ("eO", t, bp, n))
                            for i in range(8):
                                hd = 8 * n + i
                                pr, hp = hd // 2, hd % 2
                                ins = pe.matmul(ps[at, i * SQ:(i + 1) * SQ],
                                                PT[at, 2 * (t % 2) + pr // 4, (pr % 4) * P + hp * 64:(pr % 4) * P + hp * 64 + 64],
                                                e_v[at, t % 2, hd * SQ:(hd + 1) * SQ], start=True, stop=True)
                            ins.then_inc(filled(("eO", t, bp, n)), 1)
                for t in (2 * h, 2 * h + 1):
                    for bp in range(2):
                        for n in range(2):
                            written(pe, ("eO", t, bp, n))
                    for s in range(2):
                        ps = claim(pe, ("eOT", t, s))
                        for i in range(4):
                            c = 4 * s + i
                            ins = pe.transpose(ps[:, i * P:(i + 1) * P], e_o[:, t % 2, c * P:(c + 1) * P], ident[:])
                        ins.then_inc(filled(("eOT", t, s)), 1)
                for t in (2 * h, 2 * h + 1):
                    for s in range(2):
                        written(pe, ("eOT", t, s))
                tm(("ewo", h), e_q, h, e_wo, 8, t0=0)

        if upto >= 6:
            for h in range(NH):
                pe.wait_ge(S("f_z"), h + 1)
                to_fm("fT", h, Z)
            loaded("gw")
            for h in range(NH):
                written(pe, ("fT", h))
                tm(("fg", h), FT, h, gw, 2, 12)
            ffn("f1", "f2", NE, 2, f_hid, f_w1, f_w2,
                lambda e, h: pe.wait_ge(S(f"ld_f{e % 2}"), 32 * (e // 2 + 1)))

    @block.scalar
    def _(act):
        chain = [0]
        norms = [0]

        def link(ins):
            chain[0] += 1
            ins.then_inc(S("act_chain"), 1)
            act.wait_ge(S("act_chain"), chain[0])

        def norm():
            n = norms[0]
            norms[0] += 1
            act.wait_ge(S("var_ready"), n + 1)
            t = tiles[n % 2]
            link(act.activation(lnv[:, t], mv[:, t, 1], ACT.Ln, bias=eps[:]))
            act.activation(rstd[:, t], lnv[:, t], ACT.Exp, scale=-0.5).then_inc(S("rstd_ready"), 1)

        def copy_fm(name, dst, bias=None, scale=1.0, func=ACT.Identity):
            ps = finished(act, name).rearrange("p (c n) -> p c n", c=2)
            if bias is None:
                act.activation(dst, ps, ACT.Copy, scale=scale).then_inc(taken(name), 1)
                return
            for c in range(2):
                ins = act.activation(dst[:, c, :], ps[:, c, :], func, bias=bias[c])
            ins.then_inc(taken(name), 1)

        def bias2(name, at=0):
            return [col(name, at), col(name, at + 1)]

        def attention(p, n_s, kb):
            for b in range(NB):
                if b >= 2:
                    finished(act, (p + "S", b - 2, n_s - 1))
                copy_fm((p + "K", b), KT[:, b % 2], bias2(kb))
                if b >= 2:
                    finished(act, (p + "O", b - 2))
                copy_fm((p + "V", b), VB[:, b % 2])
                for s in range(n_s):
                    n = n_s * b + s
                    r = n % 4
                    act.wait_ge(S(p + "_max"), n + 1)
                    if b >= 2:
                        written(act, (p + "O", b - 2))
                    if p == "a":
                        ps = finished(act, ("aS", b, s))
                        if n >= 4:
                            finished(act, ("aPT", *divmod(n - 4, n_s)))
                    else:
                        ps = PR[:, r, :]
                    for pr in range(2):
                        j = 2 * s + pr
                        ins = act.activation(PR[:, r, pr * 256:(pr + 1) * 256], ps[:, pr * 256:(pr + 1) * 256],
                                             ACT.Exp, bias=nmx[:, b % 2, j:j + 1],
                                             accum_out=sums[:, b % 2, j:j + 1])
                    ins.then_inc(taken(("aS", b, s)) if p == "a" else S("d_p"), 1)

        def ffn(one, n_e, n_f, hid, func, biases, before):
            for e in range(n_e):
                for h in range(NH):
                    before(e, h)
                    for f in range(n_f):
                        name = (one, e, h, f)
                        dst = hid[e % 2][:, 2 * f:2 * f + 2, half[h]]
                        if biases is None:
                            ps = finished(act, name).rearrange("p (c n) -> p c n", c=2)
                            act.activation(dst, ps, func).then_inc(taken(name), 1)
                        else:
                            copy_fm(name, dst, biases(e, f), func=func)

        TABLE = "natural_log_exp_and_others"
        act.preload_act_table_set(TABLE)
        act.wait_ge(S("eps_ready"), 1)
        act.wait_ge(S("ld_cols"), 16)
        norm()
        norm()
        for h in range(NH):
            copy_fm(("aT0", h), FT[:, :, half[h]])
        for h in range(NH):
            copy_fm(("av", h), FV[:, :, half[h]], bias2("v_b"))
        norm()
        norm()
        for h in range(NH):
            copy_fm(("aT1", h), FT[:, :, half[h]])
        attention("a", 2, "k_b")
        for h in range(NH):
            copy_fm(("aOT", h), FT[:, :, half[h]], bias2("cv_b"))
        norm()
        norm()
        for h in range(NH):
            copy_fm(("aT2", h), FT[:, :, half[h]])
        ffn("af1", 1, 4, [a_hid], ACT.Relu, lambda e, f: bias2("lin1_b", 2 * f), lambda e, h: None)
        norm()
        norm()

        if upto >= 2:
            norm()
            norm()
            for h in range(NH):
                copy_fm(("bT", h), FT[:, :, half[h]])
            for t in range(NT):
                act.activation(b_v[:, t, :], finished(act, ("bv", t)), ACT.Copy).then_inc(taken(("bv", t)), 1)
                act.activation(b_g[:, t, :], finished(act, ("bg", t)), ACT.Silu).then_inc(taken(("bg", t)), 1)
            act.preload_act_table_set(TABLE)
            for t in range(NT):
                for bp in range(2):
                    at = slice(bp * 64, bp * 64 + 64)
                    ps = finished(act, ("bO", t, bp))
                    act.activation(b_o[at, t, :], ps[at, :], ACT.Copy).then_inc(taken(("bO", t, bp)), 1)
                act.wait_ge(S("b_ms"), t + 1)
                link(act.activation(ms[:, t, :], ms[:, t, :], ACT.Ln, bias=eps[:], scale=1.0 / 128))
                act.activation(ms[:, t, :], ms[:, t, :], ACT.Exp, scale=-0.5).then_inc(S("b_rms"), 1)
            for t in range(NT):
                ps = finished(act, ("bOT", t)).rearrange("p (c n) -> p c n", c=4)
                act.activation(b_ot[:, :, t * P:(t + 1) * P], ps, ACT.Copy).then_inc(taken(("bOT", t)), 1)

        if upto >= 3:
            norm()
            norm()
            for h in range(NH):
                copy_fm(("cT", h), FT[:, :, half[h]])
            norm()
            norm()
            for h in range(NH):
                copy_fm(("cT2", h), FV[:, :, half[h]])
            act.wait_ge(S("c_shifted"), 1)
            act.activation(lgt[:, :, 0:8], lgt[:, :, 0:8], ACT.Exp).then_inc(S("c_exp"), 1)

            def c_before(e, h):
                if e == 1:
                    act.wait_ge(S("perturbed"), 4)
            ffn("c1", 2, 4, c_hid, ACT.Gelu_apprx_tanh,
                lambda e, f: (bias2("ffn_b1", 2 * f) if e == 0 else
                              [bp_col[:, 2 * f:2 * f + 1], bp_col[:, 2 * f + 1:2 * f + 2]]), c_before)
            act.preload_act_table_set(TABLE)

        if upto >= 4:
            norm()
            norm()
            for h in range(NH):
                copy_fm(("dT", h), FT[:, :, half[h]])
            attention("d", 4, "xk_b")
            for h in range(NH):
                copy_fm(("dOT", h), FT[:, :, half[h]], bias2("xv_b"))

        if upto >= 5:
            norm()
            norm()
            for h in range(NH):
                copy_fm(("eT", h), FT[:, :, half[h]])
            for h in range(NH):
                if h:
                    finished(act, ("ewo", h - 1))
                for c in range(4):
                    copy_fm(("eq", h, c), e_q[:, 2 * c:2 * c + 2, :], scale=0.125)
                for c in range(4):
                    copy_fm(("ek", h, c), e_k[:, 2 * c:2 * c + 2, :])
                for t in (2 * h, 2 * h + 1):
                    for n in range(2):
                        ps = finished(act, ("ev", t, n))
                        act.activation(e_v[:, t % 2, n * 512:(n + 1) * 512], ps, ACT.Copy)\
                           .then_inc(taken(("ev", t, n)), 1)
                for t in (2 * h, 2 * h + 1):
                    act.wait_ge(S("e_shifted"), t + 1)
                    p2 = PR[:, 2 * (t % 2):2 * (t % 2) + 2, :]
                    act.activation(p2, p2, ACT.Exp).then_inc(S("e_exp"), 1)
                for t in (2 * h, 2 * h + 1):
                    for bp in range(2):
                        at = slice(bp * 64, bp * 64 + 64)
                        for n in range(2):
                            ps = finished(act, ("eO", t, bp, n))
                            act.activation(e_o[at, t % 2, n * 512:(n + 1) * 512], ps[at, :], ACT.Copy)\
                               .then_inc(taken(("eO", t, bp, n)), 1)
                for t in (2 * h, 2 * h + 1):
                    for s in range(2):
                        ps = finished(act, ("eOT", t, s)).rearrange("p (c n) -> p c n", c=4)
                        act.activation(e_q[:, 4 * s:4 * s + 4, (t % 2) * P:(t % 2 + 1) * P], ps, ACT.Copy)\
                           .then_inc(taken(("eOT", t, s)), 1)

        if upto >= 6:
            norm()
            norm()
            for h in range(NH):
                copy_fm(("fT", h), FT[:, :, half[h]])
            act.wait_ge(S("f_gap"), 1)
            act.activation(sm[:, 0:4], sm[:, 0:4], ACT.Exp).then_inc(S("f_exp"), 1)

            def f_before(e, h):
                if e >= 2:
                    finished(act, ("f2", e - 2, h))
            ffn("f1", NE, 2, f_hid, ACT.Silu, None, f_before)

    @block.vector
    def _(dve):
        chain = [0]
        norms = [0]

        def link(ins):
            chain[0] += 1
            ins.then_inc(S("dve_chain"), 1)
            dve.wait_ge(S("dve_chain"), chain[0])

        def statistics(h, src):
            for t in (2 * h, 2 * h + 1):
                ins = dve.bn_stats(st[:, t, :], src[:, t, :])
            link(ins)
            for t in (2 * h, 2 * h + 1):
                ins = dve.bn_aggr(mv[:, t, :], st[:, t, :])
            norms[0] += 1
            ins.then_inc(S("var_ready"), 1)

        def normalise(h, src, dst, n, signal, gain=None, shift=None):
            dve.wait_ge(S("rstd_ready"), n)
            for t in (2 * h, 2 * h + 1):
                if gain is None:
                    ins = dve.tensor_scalar(dst[:, t, :], src[:, t, :], mv[:, t, 0:1], rstd[:, t:t + 1],
                                            ALU.subtract, ALU.mult)
                else:
                    link(dve.scalar_tensor_tensor(out=Y[:, t, :], in0=src[:, t, :], scalar=mv[:, t, 0:1],
                                                  in1=row(gain), op0=ALU.subtract, op1=ALU.mult))
                    ins = dve.scalar_tensor_tensor(out=dst[:, t, :], in0=Y[:, t, :], scalar=rstd[:, t:t + 1],
                                                   in1=row(shift), op0=ALU.mult, op1=ALU.add)
            if signal is None:
                link(ins)
            else:
                ins.then_inc(S(signal), 1)

        def plain_norm(signal, src=X, dst=Z, gain=None, shift=None):
            for h in range(NH):
                statistics(h, src)
            for h in range(NH):
                normalise(h, src, dst, norms[0] - 1 + h, signal, gain, shift)

        def add_norm(name, bias, signal, gain, shift, between=None):
            for h in range(NH):
                job = (*name, h)
                ps = finished(dve, job).rearrange("p (c n) -> p c n", c=2)
                dve.tensor_tensor(Y[:, tiles[h], :], ps, Z[:, tiles[h], :], ALU.add).then_inc(taken(job), 1)
                written(dve, job)
                link(dve.tensor_tensor(Y[:, tiles[h], :], Y[:, tiles[h], :], over(row(bias), 2), ALU.add))
                statistics(h, Y)
            for h in range(NH):
                normalise(h, Y, Z, norms[0] - 1 + h, signal, gain, shift)

        w1f, w2f = RC[:, 0:2048], RC[:, 2048:4096]
        b1c = cols[:, COL_AT["ffn_b1"]:COL_AT["ffn_b1"] + 8]
        b2c = cols[:, COL_AT["ffn_b2"]:COL_AT["ffn_b2"] + 2]
        srcs = [w1f, w2f, w1f, w2f, b1c, b2c, b1c, b2c]
        small = {4: bkey[:, 0:8], 5: bkey[:, 8:10], 6: bkey[:, 10:18], 7: bkey[:, 18:20]}

        def key(q, phase):
            if q >= 4:
                return small[q]
            return KEY[:, q if phase else q % 2, :]

        def keys_high():
            for n in ("ffn_w1", "ffn_w2", "kwant"):
                dve.wait_ge(S("ld_" + n), 16)
            dve.wait_ge(S("ld_cols"), 16)
            for q in (0, 1, 4, 5, 6, 7):
                ins = dve.tensor_scalar(key(q, 0), srcs[q].bitcast(U16)[:, 1::2], 0x7FFF, None, ALU.bitwise_and)
            link(ins)

        def keys_low():
            link(dve.tensor_copy(thr[:, 0, :], cur[:]))
            for q in (2, 3, 0, 1, 4, 5, 6, 7):
                link(dve.tensor_scalar(key(q, 1), key(q, 0), cur[:, q:q + 1], 65535.0, ALU.not_equal, ALU.mult))
                link(dve.tensor_tensor(key(q, 1), key(q, 1), srcs[q].bitcast(U16)[:, 0::2], ALU.max))
            link(dve.memset(cur[:], 0.0))

        def search(s):
            if s >= N_SEARCH:
                return
            if s == 0:
                keys_high()
                dve.memset(cur[:], 0.0)
                link(dve.tensor_copy(kleft[:], kwant[:]))
            if s == NSTEP1 + 1:
                keys_low()
            phase = int(s > NSTEP1)
            bit = 0.0 if s == NSTEP1 else float(1 << (14 - s if s < NSTEP1 else 31 - s))
            link(dve.tensor_scalar(cand[:], cur[:], bit, None, ALU.add))
            if s:
                finished(dve, ("tot", s - 1))
            for q in range(4):
                dve.tensor_scalar(smask[:, q, :], key(q, phase), cand[:, q:q + 1], None, ALU.is_lt)\
                   .then_inc(S("smask_ready"), 1)
            for q in range(4, 8):
                k = key(q, phase)
                dve.tensor_scalar(sm[:, 64 + 16 * q:64 + 16 * q + k.shape[1]], k, cand[:, q:q + 1], None, ALU.is_lt, ALU.add,
                                  accum_out=cnt[:, q:q + 1])
            ps = finished(dve, ("cnt", s))
            dve.tensor_copy(cnt[:, 0:4], ps[:, 0:4]).then_inc(taken(("cnt", s)), 1)
            ps = finished(dve, ("tot", s))
            if s == NSTEP1:
                dve.tensor_tensor(kleft[:], kleft[:], ps[:, 0:8], ALU.subtract).then_inc(taken(("tot", s)), 1)
                written(dve, ("tot", s))
                return
            dve.tensor_tensor(sm[:, 192:200], ps[:, 0:8], kleft[:], ALU.is_lt).then_inc(taken(("tot", s)), 1)
            written(dve, ("tot", s))
            link(dve.scalar_tensor_tensor(out=cur[:], in0=sm[:, 192:200], scalar=bit, in1=cur[:],
                                          op0=ALU.mult, op1=ALU.add))

        def perturb():
            link(dve.tensor_copy(thr[:, 1, :], cur[:]))
            hi, lo = sm[:, 0:8].bitcast(I32), sm[:, 8:16].bitcast(I32)
            dve.tensor_copy(hi, thr[:, 0, :])
            link(dve.tensor_copy(lo, thr[:, 1, :]))
            link(dve.tensor_scalar(hi, hi, 16, None, ALU.logical_shift_left))
            link(dve.tensor_tensor(hi, hi, lo, ALU.bitwise_or))
            bound = sm[:, 0:8]
            tmp = [KEY[:, 0:2, :].rearrange("p a n -> p (a n)").bitcast(F32),
                   KEY[:, 2:4, :].rearrange("p a n -> p (a n)").bitcast(F32)]
            dve.wait_ge(S("ld_rows"), 16)
            perturbed = 0
            for src, dst, q in ((w1f, RC[:, 4096:6144], 0), (w2f, RC[:, 6144:8192], 1), (b1c, bp_col[:], 4),
                                (row("ffn_b2"), bp_row[:], 5)):
                n = src.shape[1]
                t1, t2 = tmp[0][:, 0:n], tmp[1][:, 0:n]
                link(dve.tensor_scalar(t1.bitcast(I32), src.bitcast(I32), 0x7FFFFFFF, None, ALU.bitwise_and))
                link(dve.tensor_scalar(t2, t1, bound[:, q + 2:q + 3], None, ALU.is_le))
                link(dve.tensor_scalar(t1, t1, bound[:, q:q + 1], None, ALU.is_ge))
                link(dve.scalar_tensor_tensor(out=t1, in0=t2, scalar=1.0, in1=t1, op0=ALU.add, op1=ALU.mult))
                link(dve.tensor_tensor(t2, t2, t1, ALU.subtract))
                link(dve.scalar_tensor_tensor(out=t1, in0=src, scalar=0.8, in1=t2, op0=ALU.mult, op1=ALU.mult))
                dve.tensor_tensor(dst, src, t1, ALU.add).then_inc(S("perturbed"), 1)
                perturbed += 1
                dve.wait_ge(S("perturbed"), perturbed)

        def attention(p, n_s, dk, steps):
            w = 2 * dk

            def transposed(b, s):
                n = n_s * b + s
                ps = finished(dve, (p + "PT", b, s))
                if n >= 4:
                    finished(dve, (p + "O", (n - 4) // n_s))
                dve.tensor_copy(PT[:, n % 4, :], ps).then_inc(taken((p + "PT", b, s)), 1)

            for i in range(NB + 1):
                for s in range(n_s):
                    if i < NB:
                        n = n_s * i + s
                        ps = finished(dve, (p + "S", i, s)).rearrange("p (c n) -> p c n", c=2)
                        if p == "a":
                            if i >= 2:
                                written(dve, ("aS", i - 2, n_s - 1))
                            dve.tensor_reduce(nmx[:, i % 2, 2 * s:2 * s + 2], ps, AX.X, ALU.max, negate=True)\
                               .then_inc(S("a_max"), 1)
                        else:
                            if n >= 4:
                                finished(dve, ("dPT", *divmod(n - 4, n_s)))
                            for pr in range(2):
                                j = 2 * s + pr
                                ins = dve.tensor_tensor_reduce(
                                    PR[:, n % 4, pr * 256:(pr + 1) * 256], ps[:, pr, :], d_mask[:, i, :],
                                    rany[:, i:i + 1], -3.0e38, ALU.add, ALU.max, rmx[:, i % 2, j:j + 1])
                            ins.then_inc(taken(("dS", i, s)), 1)
                            written(dve, ("dS", i, s))
                            dve.tensor_scalar(nmx[:, i % 2, 2 * s:2 * s + 2], rmx[:, i % 2, 2 * s:2 * s + 2], -1.0,
                                              None, ALU.mult).then_inc(S("d_max"), 1)
                    if i > 0:
                        transposed(i - 1, s)
                if i > 0:
                    b = i - 1
                    if p == "a":
                        written(dve, ("aS", b, n_s - 1))
                    else:
                        dve.wait_ge(S("d_p"), n_s * i)
                    link(dve.reciprocal(rinv[:, b % 2, 0:2 * n_s], sums[:, b % 2, 0:2 * n_s]))
                    ps = finished(dve, (p + "O", b))[:, 0:2 * n_s * w].rearrange("p (j n) -> p j n", n=w)
                    at = slice((b % 2) * 64, (b % 2) * 64 + 64)
                    for hp in range(2):
                        f = slice(hp * 64, hp * 64 + 64)
                        dst = Y[at, b // 2, :].rearrange("p (j n) -> p j n", n=w)[:, :, hp * dk:(hp + 1) * dk]
                        ins = dve.tensor_tensor(dst, ps[f, :, hp * dk:(hp + 1) * dk],
                                                each(rinv[f, b % 2, 0:2 * n_s], dk), ALU.mult)
                    ins.then_inc(taken((p + "O", b)), 1)
                if i < NB:
                    for s in range(steps):
                        search(i * steps + s)

        dve.memset(eps[:], EPS).then_inc(S("eps_ready"), 1)
        dve.memset(onesb[:], 1.0).then_inc(S("ones_ready"), 1)
        dve.memset(onesf[:], 1.0).then_inc(S("ones_ready"), 1)

        for h in range(NH):
            dve.wait_ge(S(f"ld_x{h}"), 32)
            statistics(h, X)
        for h in range(NH):
            normalise(h, X, Z, norms[0] - 1 + h, "a_z0")
        dve.wait_ge(S("a_z0"), 2)
        dve.wait_ge(S("ld_rows"), 16)
        add_norm(("aso",), "so_b", "a_z1", "ln1_g", "ln1_b")
        dve.wait_ge(S("ld_cols"), 16)
        for h in range(NH):
            ps = finished(dve, ("aq", h)).rearrange("p (c n) -> p c n", c=2)
            for c in range(2):
                ins = dve.tensor_scalar(FV[:, c, half[h]], ps[:, c, :], col("q_b", c), 32.0 ** -0.5, ALU.add, ALU.mult)
            ins.then_inc(taken(("aq", h)), 1)
        attention("a", 2, 32, 4)
        dve.wait_ge(S("a_z1"), 2)
        for h in range(NH):
            finished(dve, ("aOT", h))
        add_norm(("amo",), "mo_b", "a_z2", "ln2_g", "ln2_b")
        perturb()
        dve.wait_ge(S("a_z2"), 2)
        add_norm(("af2", 0), "lin2_b", None, "ln3_g", "ln3_b")
        for h in range(NH):
            ins = dve.tensor_tensor(X[:, tiles[h], :], X[:, tiles[h], :], Z[:, tiles[h], :], ALU.add)
            if upto == 1:
                ins.then_inc(S("x_final"), 1)
            else:
                link(ins)

        if upto >= 2:
            plain_norm("b_z")
            for n in ("rot", "decay"):
                dve.wait_ge(S("ld_" + n), 16)
            for h in range(NH):
                for a, b, dst in (("bq", "bqs", FV), ("bk", "bks", FK)):
                    ps = finished(dve, (a, h)).rearrange("p (c m s) -> p c m s", c=2, s=SQ)
                    for c in range(2):
                        ins = dve.tensor_tensor(dst[:, c, half[h]].rearrange("p (m s) -> p m s", s=SQ), ps[:, c],
                                                over(rot[:, 0, :], 4), ALU.mult)
                    ins.then_inc(taken((a, h)), 1)
                    ps = finished(dve, (b, h)).rearrange("p (m s) -> p m s", s=SQ)
                    y = Y[:, tiles[h], :].rearrange("p t (m s) -> p (t m) s", s=SQ)
                    dve.tensor_tensor(y, ps, over(rot[:, 1, :], 8), ALU.mult).then_inc(taken((b, h)), 1)
                    written(dve, (b, h))
                    d = dst[:, :, half[h]]
                    dve.tensor_tensor(d, d, Y[:, tiles[h], :], ALU.add).then_inc(S("b_qk"), 1)
                    dve.wait_ge(S("b_qk"), 2 * h + (1 if dst is FV else 2))
            for t in range(NT):
                for hp in range(2):
                    ps = finished(dve, ("bS", t, hp)).rearrange("p (c n) -> p c n", n=SQ)
                    dst = PR[:, t, 0:256].rearrange("p (c g n) -> p c g n", c=2, g=2)[:, :, hp, :]
                    dec = decay[:].rearrange("p (c g) n -> p c g n", g=2)[:, :, hp, :]
                    dve.tensor_tensor(dst, ps[:, 0:2, :], dec, ALU.mult).then_inc(taken(("bS", t, hp)), 1)
            sq = QD[:, 0].rearrange("p c h n -> p (c h n)")[:, 0:512]
            for t in range(NT):
                for bp in range(2):
                    written(dve, ("bO", t, bp))
                link(dve.tensor_tensor(sq, b_o[:, t, :], b_o[:, t, :], ALU.mult))
                dve.tensor_reduce(ms[:, t, :], sq.rearrange("p (a n) -> p a n", a=4), AX.X, ALU.add)\
                   .then_inc(S("b_ms"), 1)
                o4 = b_o[:, t, :].rearrange("p (a n) -> p a n", a=4)
                dve.wait_ge(S("b_rms"), t + 1)
                link(dve.tensor_tensor(o4, o4, each(ms[:, t, :], 128), ALU.mult))
                dve.wait_ge(S("b_gain"), t + 1)
                dve.tensor_tensor(b_o[:, t, :], b_o[:, t, :], b_g[:, t, :], ALU.mult).then_inc(S("b_gated"), 1)
            for h in range(NH):
                ps = finished(dve, ("bwo", h)).rearrange("p (c n) -> p c n", c=2)
                dve.tensor_tensor(X[:, tiles[h], :], X[:, tiles[h], :], ps, ALU.add).then_inc(taken(("bwo", h)), 1)
                written(dve, ("bwo", h))

        if upto >= 3:
            plain_norm("c_z")
            dve.wait_ge(S("c_z"), 2)
            plain_norm("c_y", Z, Y, "f_g", "f_b")
            for h in range(NH):
                ps = finished(dve, ("cr", h)).rearrange("p (c n) -> p c n", c=2)
                dve.tensor_tensor(lgt[:, tiles[h], 0:8], ps[:, :, 0:8], over(row("br"), 2), ALU.add)\
                   .then_inc(taken(("cr", h)), 1)
                written(dve, ("cr", h))
            lg = lgt[:, :, 0:8]
            link(dve.tensor_reduce(sm[:, 16:20], lg, AX.X, ALU.max))
            dve.tensor_tensor(lg, lg, each(sm[:, 16:20], 8), ALU.subtract).then_inc(S("c_shifted"), 1)
            dve.wait_ge(S("c_exp"), 1)
            dve.tensor_reduce(sm[:, 20:24], lg, AX.X, ALU.add)
            link(dve.tensor_reduce(sm[:, 24:28], lgt[:, :, 1:8], AX.X, ALU.add))
            link(dve.reciprocal(sm[:, 20:24], sm[:, 20:24]))
            pe0, pe1 = sm[:, 32:36], sm[:, 36:40]
            dve.tensor_tensor(pe0, lgt[:, :, 0], sm[:, 20:24], ALU.mult)
            link(dve.tensor_tensor(pe1, sm[:, 24:28], sm[:, 20:24], ALU.mult))
            dve.wait_ge(S("perturbed"), 4)
            for pe_, b2 in ((pe0, row("ffn_b2")), (pe1, bp_row[:])):
                for t in range(NT):
                    ins = dve.scalar_tensor_tensor(out=X[:, t, :], in0=b2, scalar=pe_[:, t:t + 1], in1=X[:, t, :],
                                                   op0=ALU.mult, op1=ALU.add)
                link(ins)
            for e in range(2):
                for h in range(NH):
                    ps = finished(dve, ("c2", e, h)).rearrange("p (c n) -> p c n", c=2)
                    for t in (2 * h, 2 * h + 1):
                        ins = dve.scalar_tensor_tensor(out=X[:, t, :], in0=ps[:, t % 2, :],
                                                       scalar=(pe0, pe1)[e][:, t:t + 1],
                                                       in1=X[:, t, :], op0=ALU.mult, op1=ALU.add)
                    ins.then_inc(taken(("c2", e, h)), 1)
                    written(dve, ("c2", e, h))

        if upto >= 4:
            plain_norm("d_z")
            dve.wait_ge(S("d_z"), 2)
            link(dve.tensor_tensor(X[:], X[:], over(row("xo_b"), 4), ALU.add))
            dve.wait_ge(S("ld_mask"), 32)
            link(dve.tensor_scalar(d_mask, d_mask, 0.0, NEG, ALU.is_equal, ALU.mult))
            link(dve.tensor_reduce(rany[:], d_mask, AX.X, ALU.max))
            link(dve.tensor_scalar(rany[:], rany[:], 0.0, None, ALU.is_ge))
            for h in range(NH):
                ps = finished(dve, ("dq", h)).rearrange("p (c n) -> p c n", c=2)
                for c in range(2):
                    ins = dve.tensor_scalar(FV[:, c, half[h]], ps[:, c, :], col("xq_b", c), 0.25, ALU.add, ALU.mult)
                ins.then_inc(taken(("dq", h)), 1)
            attention("d", 4, 16, 0)
            for h in range(NH):
                ps = finished(dve, ("dmo", h)).rearrange("p (c n) -> p c n", c=2)
                xs = X[:, tiles[h], :]
                dve.tensor_tensor(xs, xs, ps, ALU.add).then_inc(taken(("dmo", h)), 1)
                written(dve, ("dmo", h))

        if upto >= 5:
            plain_norm("e_z")
            dve.wait_ge(S("ld_rbias"), 16)
            dve.wait_ge(S("ld_causal"), 16)
            link(dve.tensor_tensor(e_bias, e_bias, over(e_causal, 8), ALU.add))
            for h in range(NH):
                for t in (2 * h, 2 * h + 1):
                    p2 = PR[:, 2 * (t % 2):2 * (t % 2) + 2, :].rearrange("p a n -> p (a n)")
                    if t >= 2:
                        finished(dve, ("ePT", t - 2, 1))
                    for bp in range(2):
                        for hp in range(2):
                            at = slice(hp * 64, hp * 64 + 64)
                            ps = finished(dve, ("eS", t, bp, hp)).rearrange("p (c n) -> p c n", n=SQ)
                            dst = p2.rearrange("p (c g n) -> p c g n", c=8, g=2)[at, :, bp, :]
                            dve.tensor_tensor(dst, ps[at], e_bias[at], ALU.add).then_inc(taken(("eS", t, bp, hp)), 1)
                            written(dve, ("eS", t, bp, hp))
                    pv = p2.rearrange("p (c n) -> p c n", n=SQ)
                    mx = sm[:, 64 + 16 * (t % 2):80 + 16 * (t % 2)]
                    link(dve.tensor_reduce(mx, pv, AX.X, ALU.max))
                    dve.tensor_tensor(pv, pv, each(mx, SQ), ALU.subtract).then_inc(S("e_shifted"), 1)
                for t in (2 * h, 2 * h + 1):
                    p2 = PR[:, 2 * (t % 2):2 * (t % 2) + 2, :].rearrange("p a n -> p (a n)")
                    pv = p2.rearrange("p (c n) -> p c n", n=SQ)
                    mx = sm[:, 64 + 16 * (t % 2):80 + 16 * (t % 2)]
                    dve.wait_ge(S("e_exp"), t + 1)
                    link(dve.tensor_reduce(mx, pv, AX.X, ALU.add))
                    link(dve.reciprocal(mx, mx))
                    dve.tensor_tensor(pv, pv, each(mx, SQ), ALU.mult).then_inc(S("e_p"), 1)
                for t in (2 * h, 2 * h + 1):
                    for s in range(2):
                        ps = finished(dve, ("ePT", t, s))
                        if t >= 2:
                            finished(dve, ("eO", t - 2, 1, 1))
                        dve.tensor_copy(PT[:, 2 * (t % 2) + s, :], ps).then_inc(taken(("ePT", t, s)), 1)
                ps = finished(dve, ("ewo", h)).rearrange("p (c n) -> p c n", c=2)
                dve.tensor_tensor(X[:, tiles[h], :], X[:, tiles[h], :], ps, ALU.add).then_inc(taken(("ewo", h)), 1)
                written(dve, ("ewo", h))

        if upto >= 6:
            plain_norm("f_z")
            dve.wait_ge(S("f_z"), 2)
            dve.wait_ge(S("ld_iota12"), 16)
            for h in range(NH):
                ps = finished(dve, ("fg", h)).rearrange("p (c n) -> p c n", c=2)
                dve.tensor_tensor(lgt[:, tiles[h], :], ps[:, :, 0:12], over(row("eb"), 2), ALU.add)\
                   .then_inc(taken(("fg", h)), 1)
                written(dve, ("fg", h))
            for t in range(NT):
                link(dve.max(m8[:, t, :], lgt[:, t, :]))
                link(dve.max_index(i8[:, t, :], m8[:, t, :], lgt[:, t, :]))
            dve.tensor_tensor(sm[:, 0:4], m8[:, :, 1], m8[:, :, 0], ALU.subtract).then_inc(S("f_gap"), 1)
            link(dve.tensor_copy(i8f[:, :, 0:2], i8[:, :, 0:2]))
            dve.wait_ge(S("f_exp"), 1)
            link(dve.tensor_scalar(sm[:, 4:8], sm[:, 0:4], 1.0, None, ALU.add))
            link(dve.reciprocal(sm[:, 8:12], sm[:, 4:8]))
            link(dve.tensor_tensor(sm[:, 12:16], sm[:, 0:4], sm[:, 8:12], ALU.mult))
            for t in range(NT):
                dve.tensor_scalar(wgt[:, t, :], iota12[:], i8f[:, t, 0:1], sm[:, 8 + t:9 + t], ALU.is_equal, ALU.mult)
                link(dve.tensor_scalar(lgt[:, t, :], iota12[:], i8f[:, t, 1:2], sm[:, 12 + t:13 + t], ALU.is_equal,
                                       ALU.mult))
            link(dve.tensor_tensor(wgt[:], wgt[:], lgt[:], ALU.add))
            link(dve.tensor_reduce(sm[:, 16:20], wgt[:, :, 8:12], AX.X, ALU.add))
            for t in range(NT):
                ins = dve.scalar_tensor_tensor(out=X[:, t, :], in0=Z[:, t, :], scalar=sm[:, 16 + t:17 + t],
                                               in1=X[:, t, :], op0=ALU.mult, op1=ALU.add)
            link(ins)
            for e in range(NE):
                for h in range(NH):
                    name = ("f2", e, h)
                    ps = finished(dve, name).rearrange("p (c n) -> p c n", c=2)
                    for t in (2 * h, 2 * h + 1):
                        ins = dve.scalar_tensor_tensor(out=X[:, t, :], in0=ps[:, t % 2, :], scalar=wgt[:, t, e:e + 1],
                                                       in1=X[:, t, :], op0=ALU.mult, op1=ALU.add)
                    ins.then_inc(taken(name), 1)
                    written(dve, name)

    @block.gpsimd
    def _(pool):
        def block_diagonal(p, n_h, n_s, m0):
            for b in range(NB):
                if b >= 2:
                    finished(pool, (p + "S", b - 2, n_s - 1))
                if b % 4 == 0:
                    written(pool, (p + "q", b // 4))
                tok = slice(b * SQ, (b + 1) * SQ)
                for c in range(2):
                    ins = pool.tensor_tensor(QD[:, b % 2, c, 0:n_h, :], over(FV[:, c, tok], n_h),
                                             each(hmask[:, m0:m0 + n_h], SQ), ALU.mult)
                ins.then_inc(S(p + "_qd_ready"), 1)

        pool.wait_ge(S("ld_hmask"), 16)
        block_diagonal("a", 4, 2, 0)
        if upto >= 2:
            pool.wait_ge(S("ld_rows"), 16)
            for t in range(NT):
                written(pool, ("bg", t))
                g4 = b_g[:, t, :].rearrange("p (a n) -> p a n", a=4)
                pool.tensor_tensor(g4, g4, over(row("gn"), 4), ALU.mult).then_inc(S("b_gain"), 1)
        if upto >= 4:
            block_diagonal("d", 8, 4, 4)


def _bucket(rel, num_buckets=32, max_distance=128):
    nb = num_buckets // 2
    buckets = (rel > 0).astype(np.int32) * nb
    rel_abs = np.abs(rel)
    max_exact = nb // 2
    large = max_exact + (np.log(np.maximum(rel_abs, 1).astype(np.float32) / np.float32(max_exact))
                         / np.float32(np.log(max_distance / max_exact)) * (nb - max_exact)).astype(np.int32)
    return buckets + np.where(rel_abs < max_exact, rel_abs, np.minimum(large, nb - 1))


def kernel(**inputs):
    import concourse.bacc as _bacc
    from concourse.bass_utils import run_bass_kernel_spmd as _run

    I = {k: np.asarray(v) for k, v in inputs.items()}
    f32 = np.float32

    def kmajor(w):
        k, n = w.shape
        return np.ascontiguousarray(w.reshape(k // P, P, n).transpose(1, 0, 2))

    a = {}
    a["x"] = np.ascontiguousarray(I["x"].reshape(T, D))
    a["ctx"] = kmajor(I["ctx_1024"].reshape(NB * SK, D).T)
    a["mask"] = np.ascontiguousarray(I["mask_Bx1xSxS2_ff1"][:, 0].transpose(1, 0, 2))
    qkv, inp = I["L0_xattn_qkv_w"], I["L0_xattn_in_proj_w"]
    a["v_w"] = kmajor(qkv[512:].T)
    a["so_w"] = kmajor(I["L0_xattn_sa_out_w"].T)
    a["q_w"], a["k_w"], a["cv_w"] = (kmajor(inp[256 * i:256 * i + 256].T) for i in range(3))
    a["mo_w"] = kmajor(I["L0_xattn_mha_out_w"].T)
    a["lin1_w"] = kmajor(I["L0_xattn_lin1_w"].T)
    a["lin2_w"] = kmajor(I["L0_xattn_lin2_w"].T)
    swap = (np.arange(256) // 64) * 64 + (np.arange(256) % 64 + 32) % 64
    a["rq_w"], a["rk_w"] = kmajor(I["L0_attn_Wq"]), kmajor(I["L0_attn_Wk"])
    a["rqs_w"], a["rks_w"] = kmajor(I["L0_attn_Wq"][:, swap]), kmajor(I["L0_attn_Wk"][:, swap])
    a["rv_w"], a["rg_w"], a["ro_w"] = (kmajor(I["L0_attn_W" + n]) for n in "vgo")
    a["ffn_w1"], a["ffn_w2"] = kmajor(I["L0_ffn_W1"]), kmajor(I["L0_ffn_W2"])
    a["Wr"] = kmajor(I["L0_ffn_Wr"])
    for n in "qkv":
        a[f"x{n}_w"] = kmajor(I["L1_xattn_W" + n].transpose(1, 0, 2).reshape(D, D))
        a[f"e{n}_w"] = kmajor(I["L1_attn_W" + n].T)
    a["xo_w"] = kmajor(I["L1_xattn_Wo"])
    a["eo_w"] = kmajor(I["L1_attn_Wo"].T)
    a["gw"] = kmajor(I["L1_ffn_gate_w"].T)
    a["fw1"] = np.ascontiguousarray(I["L1_ffn_w1"].transpose(0, 2, 1).reshape(NE, 2, P, DFF).transpose(0, 2, 1, 3))
    a["fw2"] = np.ascontiguousarray(I["L1_ffn_w2"].transpose(0, 2, 1).reshape(NE, 4, P, D).transpose(0, 2, 1, 3))
    colv = {"v_b": I["L0_xattn_qkv_b"][512:], "q_b": I["L0_xattn_in_proj_b"][:256],
            "k_b": I["L0_xattn_in_proj_b"][256:512], "cv_b": I["L0_xattn_in_proj_b"][512:],
            "lin1_b": I["L0_xattn_lin1_b"], "ffn_b1": I["L0_ffn_b1"], "ffn_b2": I["L0_ffn_b2"],
            "xq_b": I["L1_xattn_bq"].reshape(-1), "xk_b": I["L1_xattn_bk"].reshape(-1),
            "xv_b": I["L1_xattn_bv"].reshape(-1)}
    a["cols"] = np.ascontiguousarray(np.concatenate([colv[n].reshape(-1, P).T for n in COLS], axis=1))
    rowv = {"so_b": I["L0_xattn_sa_out_b"], "ln1_g": I["L0_xattn_ln1_g"], "ln1_b": I["L0_xattn_ln1_b"],
            "mo_b": I["L0_xattn_mha_out_b"], "ln2_g": I["L0_xattn_ln2_g"], "ln2_b": I["L0_xattn_ln2_b"],
            "lin2_b": I["L0_xattn_lin2_b"], "ln3_g": I["L0_xattn_ln3_g"], "ln3_b": I["L0_xattn_ln3_b"],
            "gn": I["L0_attn_gn_weight"], "f_g": I["L0_ffn_ln_gamma"], "f_b": I["L0_ffn_ln_beta"],
            "ffn_b2": I["L0_ffn_b2"], "xo_b": I["L1_xattn_bo"], "br": I["L0_ffn_br"],
            "eb": I["L1_ffn_expert_bias"]}
    a["rows"] = np.ascontiguousarray(np.concatenate([rowv[n] for n in ROWS])[None, :])
    p = np.arange(P)
    a["ident"] = np.eye(P, dtype=f32)
    a["hmask"] = np.concatenate([p[:, None] // 32 == np.arange(4), p[:, None] // 16 == np.arange(8)], 1).astype(f32)
    inv_freq = f32(1.0) / np.power(f32(10000.0), np.arange(0, 64, 2, dtype=f32) / f32(64))
    ang = (np.arange(SQ, dtype=f32)[None, :] * inv_freq[p % 32][:, None]).astype(f32)
    sign = np.where(p % 64 < 32, -1.0, 1.0).astype(f32)[:, None]
    a["rot"] = np.ascontiguousarray(np.stack([np.cos(ang), np.sin(ang) * sign], 1).astype(f32))
    gamma = 1.0 - np.exp2(-5.0 - np.arange(4))
    j, i = (p % 64)[:, None, None], np.arange(SQ)[None, None, :]
    a["decay"] = np.where(i >= j, gamma[None, :, None] ** np.maximum(i - j, 0) / 8.0, 0.0).astype(f32)
    a["iota12"] = np.tile(np.arange(12, dtype=f32), (P, 1))
    ranks = []
    for size in (LIN * D, LIN * D, LIN, D):
        k = max(1, int(size * 0.1 / 2))
        ranks.append((size - k + 1, k))
    want = [ranks[0][0], ranks[1][0], ranks[0][1], ranks[1][1], ranks[2][0], ranks[3][0], ranks[2][1], ranks[3][1]]
    a["kwant"] = np.tile(np.array(want, f32), (P, 1))
    rel = np.arange(SQ)[:, None] - np.arange(SQ)[None, :]
    e = I["L1_attn_rel_emb"][_bucket(rel)]
    a["rbias"] = np.ascontiguousarray(e.reshape(SQ, SQ, 8, 2).transpose(3, 0, 2, 1).reshape(P, 8, SQ))
    a["causal"] = np.where(rel[p % 64] < 0, CAUSAL_NEG, 0.0).astype(f32)

    nc = _bacc.Bacc("TRN2", target_bir_lowering=False, num_devices=1)
    A = {n: nc.dram_tensor(f"in_{n}", v.shape, mybir.dt.from_np(v.dtype), kind="ExternalInput").ap()
         for n, v in a.items()}
    out = nc.dram_tensor("out_x", (T, D), F32, kind="ExternalOutput").ap()
    build(nc, A, out, UPTO)
    r = _run(nc, [{f"in_{n}": v for n, v in a.items()}], core_ids=[0])
    return r.results[0]["out_x"].reshape(NB, SQ, D)


UPTO = 6
```

```python
from contextlib import ExitStack

import numpy as np

import concourse.bass as bass
from concourse import mybir

F32 = mybir.dt.float32
BF16 = mybir.dt.bfloat16
U16 = mybir.dt.uint16
I32 = mybir.dt.int32
U32 = mybir.dt.uint32
ALU = mybir.AluOpType
ACT = mybir.ActivationFunctionType
AX = mybir.AxisListType

P = 128
NB, SQ, SK, D = 8, 64, 256, 256
T = NB * SQ
NT = T // P
NH = 2
HT = T // NH
EPS = 1e-5
NE = 8
NSTEP1, NSTEP2 = 15, 16
N_SEARCH = NSTEP1 + 1 + NSTEP2
LIN, DFF = 1024, 512
NEG = -1.0e9
CAUSAL_NEG = -1.0e30

COLS = ["v_b", "q_b", "k_b", "cv_b", "lin1_b", "ffn_b1", "ffn_b2", "xq_b", "xk_b", "xv_b"]
COL_N = {"v_b": 2, "q_b": 2, "k_b": 2, "cv_b": 2, "lin1_b": 8, "ffn_b1": 8, "ffn_b2": 2, "xq_b": 2,
         "xk_b": 2, "xv_b": 2}
COL_AT = {n: sum(COL_N[m] for m in COLS[:i]) for i, n in enumerate(COLS)}
NCOL = sum(COL_N.values())
ROWS = ["so_b", "ln1_g", "ln1_b", "mo_b", "ln2_g", "ln2_b", "lin2_b", "ln3_g", "ln3_b", "gn", "f_g",
        "f_b", "ffn_b2", "xo_b", "br", "eb"]
ROW_N = {n: D for n in ROWS} | {"gn": 128, "br": 8, "eb": 12}
ROW_AT = {n: sum(ROW_N[m] for m in ROWS[:i]) for i, n in enumerate(ROWS)}
NROW = sum(ROW_N.values())


def job_order(upto):
    H = range(NH)
    out = []
    parts = [0]

    def search(n=1):
        for _ in range(n):
            s, summing = divmod(parts[0], 2)
            parts[0] += 1
            out.append(("tot" if summing else "cnt", s))

    def attention(p, n_s, steps):
        out.extend([(p + "K", 0), (p + "V", 0)])
        for i in range(NB + 1):
            for s in range(n_s):
                if i < NB:
                    out.append((p + "S", i, s))
                if i > 0:
                    out.append((p + "PT", i - 1, s))
                if i < NB and s < 2:
                    search(steps)
            if i + 1 < NB:
                out.extend([(p + "K", i + 1), (p + "V", i + 1)])
            if i < NB:
                search(steps)
            if i > 0:
                out.append((p + "O", i - 1))
            if i < NB:
                search(steps)

    for n in ("aT0", "av", "aso", "aT1", "aq"):
        out.extend([(n, h) for h in H])
        if n != "aT0":
            search()
    attention("a", 2, 1)
    for n in ("aOT", "amo", "aT2"):
        out.extend([(n, h) for h in H])
        search()
    for h in H:
        out.extend([("af1", 0, h, f) for f in range(4)])
        search()
    out.extend([("af2", 0, 0)])
    search()
    out.extend([("af2", 0, 1)])
    if upto >= 2:
        out.extend([("bT", h) for h in H])
        for h in H:
            for a in ("bq", "bk"):
                out.extend([(a, h), (a + "s", h)])
                search()
        for t in range(NT):
            out.extend([("bv", t), ("bg", t)])
            search()
        for t in range(NT + 1):
            if t < NT:
                out.extend([("bS", t, 0), ("bS", t, 1)])
            if t > 0:
                out.extend([("bO", t - 1, 0), ("bO", t - 1, 1)])
            if t < NT:
                search()
        out.extend([("bOT", t) for t in range(NT)])
        search()
        out.extend([("bwo", h) for h in H])
    if upto >= 3:
        for n in ("cT", "cT2", "cr"):
            out.extend([(n, h) for h in H])
            search()
        for e in range(2):
            for h in H:
                for f in range(4):
                    out.append(("c1", e, h, f))
                    if e == 0 and (h, f) < (1, 2):
                        search()
            out.extend([("c2", e, h) for h in H])
    if upto >= 4:
        out.extend([("dT", h) for h in H])
        out.extend([("dq", h) for h in H])
        attention("d", 4, 0)
        for n in ("dOT", "dmo"):
            out.extend([(n, h) for h in H])
    if upto >= 5:
        out.extend([("eT", h) for h in H])
        for h in H:
            out.extend([("eq", h, c) for c in range(4)])
            out.extend([("ek", h, c) for c in range(4)])
            for t in (2 * h, 2 * h + 1):
                out.extend([("ev", t, 0), ("ev", t, 1)])
            for t in (2 * h, 2 * h + 1):
                for bp in range(2):
                    for hp in range(2):
                        out.append(("eS", t, bp, hp))
            for t in (2 * h, 2 * h + 1):
                out.extend([("ePT", t, 0), ("ePT", t, 1)])
                for bp in range(2):
                    for n in range(2):
                        out.append(("eO", t, bp, n))
            for t in (2 * h, 2 * h + 1):
                out.extend([("eOT", t, 0), ("eOT", t, 1)])
            out.append(("ewo", h))
    if upto >= 6:
        out.extend([("fT", h) for h in H])
        out.extend([("fg", h) for h in H])
        seq = [(e, h) for e in range(NE) for h in H]
        for i in range(len(seq) + 1):
            if i < len(seq):
                out.extend([("f1", *seq[i], f) for f in range(2)])
            if i > 0:
                out.append(("f2", *seq[i - 1]))
    assert upto < 3 or parts[0] == 2 * N_SEARCH, parts
    return out


def build(nc, A, out, upto=6):
    with ExitStack() as ctx:
        _build(nc, A, out, upto, ctx)


def _build(nc, A, out, upto, ctx):
    def sb(name, shape, dt=F32):
        return ctx.enter_context(nc.sbuf_tensor(name, shape, dt))

    sems = {}

    def S(name):
        if name not in sems:
            sems[name] = ctx.enter_context(nc.semaphore(name))
        return sems[name]

    JOBS = {name: (i % 8, i // 8) for i, name in enumerate(job_order(upto))}
    psum = ctx.enter_context(nc.psum_tensor("psum", [P, 8, 512], F32))
    full = [S(f"bank{b}_full") for b in range(8)]
    free = [S(f"bank{b}_free") for b in range(8)]

    X = sb("X", [P, NT, D])
    Z = sb("Z", [P, NT, D])
    Y = sb("Y", [P, NT, D])
    FT = sb("FT", [P, 2, T])
    FV = sb("FV", [P, 2, T])
    FK = sb("FK", [P, 2, T])
    BIG = sb("BIG", [P, 8192])
    RA = sb("RA", [P, 7168])
    RB = sb("RB", [P, 5120])
    RC = sb("RC", [P, 8192])
    CTX = sb("CTX", [P, 2, NB * SK])
    KT = sb("KT", [P, 2, 2, SK])
    VB = sb("VB", [P, 2, 2, D])
    QD = sb("QD", [P, 2, 2, 8, SQ])
    PR = sb("PR", [P, 4, 512])
    PT = sb("PT", [P, 4, 512])
    rows = sb("rows", [P, NROW])
    cols = sb("cols", [P, NCOL])
    ident = sb("ident", [P, P])
    hmask = sb("hmask", [P, 12])
    rot = sb("rot", [P, 2, SQ])
    decay = sb("decay", [P, 4, SQ])
    iota12 = sb("iota12", [P, 12])
    Wr = sb("Wr", [P, 2, 8])
    gw = sb("gw", [P, 2, 12])
    kwant = sb("kwant", [P, 8])
    onesb = sb("onesb", [P, 1], BF16)
    onesf = sb("onesf", [P, P])
    st = sb("st", [P, NT, 6])
    mv = sb("mv", [P, NT, 2])
    lnv = sb("lnv", [P, NT])
    rstd = sb("rstd", [P, NT])
    nmx = sb("nmx", [P, 2, 8])
    sums = sb("sums", [P, 2, 8])
    rinv = sb("rinv", [P, 2, 8])
    rmx = sb("rmx", [P, 2, 8])
    ms = sb("ms", [P, NT, 4])
    eps = sb("eps", [P, 1])
    sm = sb("sm", [P, 256])
    cnt = sb("cnt", [P, 8])
    cur = sb("cur", [P, 8])
    cand = sb("cand", [P, 8])
    kleft = sb("kleft", [P, 8])
    thr = sb("thr", [P, 2, 8])
    bkey = sb("bkey", [P, 4, 8], U16)
    below = sb("below", [P, 4, 8])
    nbias = sb("nbias", [P, 1])
    signs = sb("signs", [P, 1])
    bound = sb("bound", [P, 8])
    lgt = sb("lgt", [P, 4, 12])
    m8 = sb("m8", [P, 4, 8])
    i8 = sb("i8", [P, 4, 8], U32)
    i8f = sb("i8f", [P, 4, 8])
    wgt = sb("wgt", [P, 4, 12])
    rany = sb("rany", [P, NB])
    bp_row = sb("bp_row", [P, D])
    bp_col = sb("bp_col", [P, 8])

    def part(region, at, *shape):
        n = int(np.prod(shape))
        v = region[:, at:at + n]
        if len(shape) == 2:
            v = v.rearrange("p (a b) -> p a b", a=shape[0])
        if len(shape) == 3:
            v = v.rearrange("p (a b c) -> p a b c", a=shape[0], b=shape[1])
        return v

    a_wv, a_so, a_wq, a_wk, a_wcv, a_mo = (part(RA, 512 * i, 2, 256) for i in range(6))
    a_l1 = part(RA, 3072, 2, 1024)
    a_l2 = part(RA, 5120, 8, 256)
    b_wq, b_wqs, b_wk, b_wks = (part(RB, 512 * i, 2, 256) for i in range(4))
    b_wv, b_wg = part(RB, 2048, 2, 512), part(RB, 3072, 2, 512)
    b_wo = part(RB, 4096, 4, 256)
    c_w1 = [part(RC, 0, 2, 1024), part(RC, 4096, 2, 1024)]
    c_w2 = [part(RC, 2048, 8, 256), part(RC, 6144, 8, 256)]
    d_wq, d_wk, d_wv, d_wo = (part(RA, 512 * i, 2, 256) for i in range(4))
    d_mask = part(RB, 0, NB, SK)
    e_wq, e_wk, e_wv = (part(RC, 2048 * i, 2, 1024) for i in range(3))
    e_wo = part(RC, 6144, 8, 256)
    e_bias = part(RB, 2048, 8, SQ)
    e_causal = part(RB, 2560, SQ)
    f_w1 = [part(RA, 2048 + 2048 * i, 2, 512) for i in range(2)]
    f_w2 = [part(RA, 3072 + 2048 * i, 4, 256) for i in range(2)]
    a_hid = part(BIG, 0, 8, T)
    b_v, b_g = part(BIG, 0, NT, 512), part(BIG, 2048, NT, 512)
    b_o, b_ot = part(RA, 2048, NT, 512), part(RA, 4608, 4, T)
    c_hid = [part(BIG, 0, 8, T), part(BIG, 4096, 8, T)]
    e_q, e_k = part(BIG, 0, 8, HT), part(BIG, 2048, 8, HT)
    e_v, e_o = part(BIG, 4096, 2, 1024), part(BIG, 6144, 2, 1024)
    f_hid = [part(BIG, 0, 4, T), part(BIG, 2048, 4, T)]
    KEY = BIG[:, 4096:8192].bitcast(U16).rearrange("p (q n) -> p q n", q=4)
    smask = RC[:, 4096:8192].bitcast(BF16).rearrange("p (q n) -> p q n", q=4)

    def row(name, n=None):
        return rows[:, ROW_AT[name]:ROW_AT[name] + (n or ROW_N[name])]

    def col(name, i):
        return cols[:, COL_AT[name] + i:COL_AT[name] + i + 1]

    def bank(name):
        return psum[:, JOBS[name][0], :]

    def over(ap, n):
        return ap.unsqueeze(1).to_broadcast([ap.shape[0], n, ap.shape[1]])

    def each(ap, n):
        return ap.unsqueeze(2).to_broadcast([ap.shape[0], ap.shape[1], n])

    block = ctx.enter_context(nc.Block())

    def claim(pe, name):
        b, u = JOBS[name]
        if u:
            pe.wait_ge(free[b], u)
        return psum[:, b, :]

    def filled(name):
        return full[JOBS[name][0]]

    def taken(name):
        return free[JOBS[name][0]]

    def finished(eng, name):
        b, u = JOBS[name]
        eng.wait_ge(full[b], u + 1)
        return psum[:, b, :]

    def written(eng, name):
        b, u = JOBS[name]
        eng.wait_ge(free[b], u + 1)

    half = [slice(h * HT, (h + 1) * HT) for h in range(NH)]
    tiles = [slice(2 * h, 2 * h + 2) for h in range(NH)]

    @block.sync
    def _(sp):
        def load(dst, name, src=None):
            sp.dma_start(dst, A[name] if src is None else src).then_inc(S("ld_" + name), 16)

        for t in range(NT):
            sp.dma_start(X[:, t, :], A["x"][t * P:(t + 1) * P, :]).then_inc(S(f"ld_x{t // 2}"), 16)
        load(ident[:], "ident")
        load(cols[:], "cols")
        load(a_wv, "v_w")
        load(rows[:], "rows", A["rows"].to_broadcast([P, NROW]))
        load(a_so, "so_w")
        load(c_w1[0], "ffn_w1")
        load(c_w2[0], "ffn_w2")
        load(kwant[:], "kwant")
        load(a_wq, "q_w")
        load(a_wk, "k_w")
        load(CTX[:], "ctx")
        load(a_wcv, "cv_w")
        load(hmask[:], "hmask")
        load(a_mo, "mo_w")
        load(a_l1, "lin1_w")
        load(a_l2, "lin2_w")
        if upto >= 2:
            load(b_wq, "rq_w")
            load(b_wqs, "rqs_w")
            load(b_wk, "rk_w")
            load(b_wks, "rks_w")
            load(b_wv, "rv_w")
            load(b_wg, "rg_w")
            load(b_wo, "ro_w")
            load(rot[:], "rot")
            load(decay[:], "decay")
        if upto >= 3:
            load(Wr[:], "Wr")
            load(gw[:], "gw")
            load(iota12[:], "iota12")
        if upto >= 4:
            finished(sp, ("af2", 0, 1))
            load(d_wq, "xq_w")
            load(d_wk, "xk_w")
            load(d_wv, "xv_w")
            load(d_wo, "xo_w")
            finished(sp, ("bwo", 1))
            for hp in range(2):
                sp.dma_start(d_mask[hp * 64:hp * 64 + 64], A["mask"]).then_inc(S("ld_mask"), 16)
            load(e_bias, "rbias")
            load(e_causal, "causal")
        if upto >= 5:
            finished(sp, ("c2", 1, 1))
            load(e_wq, "eq_w")
            load(e_wk, "ek_w")
            load(e_wv, "ev_w")
            load(e_wo, "eo_w")
        if upto >= 6:
            for e in range(NE):
                if e >= 2:
                    finished(sp, ("f2", e - 2, 1))
                sp.dma_start(f_w1[e % 2], A["fw1"][e]).then_inc(S(f"ld_f{e % 2}"), 16)
                sp.dma_start(f_w2[e % 2], A["fw2"][e]).then_inc(S(f"ld_f{e % 2}"), 16)
        for h in range(NH):
            if upto == 1:
                sp.wait_ge(S("x_final"), h + 1)
            else:
                written(sp, {2: ("bwo", h), 3: ("c2", 1, h), 4: ("dmo", h), 5: ("ewo", h), 6: ("f2", NE - 1, h)}[upto])
            for t in (2 * h, 2 * h + 1):
                sp.dma_start(out[t * P:(t + 1) * P, :], X[:, t, :]).then_inc(S("stored"), 16)
        sp.wait_ge(S("stored"), 16 * NT)

    @block.tensor
    def _(pe):
        parts = [0]

        def loaded(*names):
            for n in names:
                pe.wait_ge(S("ld_" + n), 16)

        def to_fm(name, h, src, nk=2):
            ps = claim(pe, (name, h)).rearrange("p (c n) -> p c n", c=2)
            for t in (2 * h, 2 * h + 1):
                for c in range(2):
                    ins = pe.transpose(ps[:, c, (t % 2) * P:(t % 2 + 1) * P], src[:, t, c * P:(c + 1) * P],
                                       ident[:])
            ins.then_inc(filled((name, h)), 1)

        def fm(name, w, c0, src, tok):
            ps = claim(pe, name).rearrange("p (c n) -> p c n", c=2)
            for c in range(2):
                for k in range(2):
                    ins = pe.matmul(ps[:, c, :], w[:, k, (c0 + c) * P:(c0 + c + 1) * P], src[:, k, tok],
                                    start=(k == 0), stop=(k == 1))
            ins.then_inc(filled(name), 1)

        def tm(name, src, h, w, nk, n=256, t0=None):
            ps = claim(pe, name).rearrange("p (c n) -> p c n", c=2)
            for j in range(2):
                at = ((2 * h + j) if t0 is None else j) * P
                for k in range(nk):
                    ins = pe.matmul(ps[:, j, :n], src[:, k, at:at + P], w[:, k, :n],
                                    start=(k == 0), stop=(k == nk - 1))
            ins.then_inc(filled(name), 1)

        def search():
            s, summing = divmod(parts[0], 2)
            parts[0] += 1
            if not summing:
                ps = claim(pe, ("cnt", s))
                for q in range(1, 4):
                    pe.wait_ge(S("smask_ready"), 3 * s + q)
                    for i in range(16):
                        ins = pe.matmul(ps[:, q:q + 1], smask[:, q, i * P:(i + 1) * P], onesb[:],
                                        start=(i == 0), stop=(i == 15))
                ins.then_inc(filled(("cnt", s)), 1)
            else:
                ps = claim(pe, ("tot", s))
                written(pe, ("cnt", s))
                pe.matmul(ps[:, 0:8], onesf[:], cnt[:], start=True, stop=True).then_inc(filled(("tot", s)), 1)

        def attention(p, wk, wv, n_s, steps):
            w = D // (4 * n_s) * 2
            per = 2 if n_s == 2 else 4

            def p_ready(p, b, s):
                if p == "a":
                    written(pe, ("aS", b, s))
                else:
                    pe.wait_ge(S("d_p"), n_s * b + s + 1)

            def pv(b):
                ps = claim(pe, (p + "O", b))
                for s in range(n_s):
                    for pr in range(2):
                        j = 2 * s + pr
                        for kc in range(2):
                            ins = pe.matmul(ps[:, j * w:(j + 1) * w],
                                            PT[:, (n_s * b + s) % 4, pr * 256 + kc * P:pr * 256 + (kc + 1) * P],
                                            VB[:, b % 2, kc, j * w:(j + 1) * w], start=(kc == 0), stop=(kc == 1))
                ins.then_inc(filled((p + "O", b)), 1)

            def p_transpose(b, s):
                ps = claim(pe, (p + "PT", b, s))
                p_ready(p, b, s)
                for pr in range(2):
                    for kc in range(2):
                        at = pr * 256 + kc * P
                        ins = pe.transpose(ps[:, at:at + P], PR[:, (n_s * b + s) % 4, at:at + P], ident[:])
                ins.then_inc(filled((p + "PT", b, s)), 1)

            def keys_values(i):
                fm((p + "K", i), wk, 0, CTX, slice(i * SK, (i + 1) * SK))
                ps = claim(pe, (p + "V", i)).rearrange("p (c n) -> p c n", c=2)
                for kt in range(2):
                    for k in range(2):
                        at = i * SK + kt * P
                        ins = pe.matmul(ps[:, kt, :], CTX[:, k, at:at + P], wv[:, k, :],
                                        start=(k == 0), stop=(k == 1))
                ins.then_inc(filled((p + "V", i)), 1)

            keys_values(0)
            for i in range(NB + 1):
                if i < NB:
                    pe.wait_ge(S(p + "_qd_ready"), i + 1)
                    written(pe, (p + "K", i))
                for s in range(n_s):
                    if i < NB:
                        ps = claim(pe, (p + "S", i, s))
                        for pr in range(2):
                            j = 2 * s + pr
                            c, jj = j // per, j % per
                            ins = pe.matmul(ps[:, pr * 256:(pr + 1) * 256], QD[:, i % 2, c, 2 * jj:2 * jj + 2, :],
                                            KT[:, i % 2, c, :], start=True, stop=True)
                        ins.then_inc(filled((p + "S", i, s)), 1)
                    if i > 0:
                        p_transpose(i - 1, s)
                    if steps and i < NB and s < 2:
                        search()
                if i + 1 < NB:
                    keys_values(i + 1)
                if steps and i < NB:
                    search()
                if i > 0:
                    for s in range(n_s):
                        written(pe, (p + "PT", i - 1, s))
                    written(pe, (p + "V", i - 1))
                    pv(i - 1)
                if steps and i < NB:
                    search()

        def ffn_in(name, w1, h):
            fm(name, w1, 2 * name[-1], FT, half[h])

        def ffn_out(one, two, e, h, n_f, hid, w2):
            for f in range(n_f):
                written(pe, (one, e, h, f))
            tm((two, e, h), hid, h, w2, 2 * n_f)

        loaded("ident", "v_w")
        pe.wait_ge(S("ones_ready"), 2)
        for h in range(NH):
            pe.wait_ge(S("a_z0"), h + 1)
            to_fm("aT0", h, Z)
        for h in range(NH):
            written(pe, ("aT0", h))
            fm(("av", h), a_wv, 0, FT, half[h])
        search()
        loaded("so_w")
        for h in range(NH):
            written(pe, ("av", h))
            tm(("aso", h), FV, h, a_so, 2)
        search()
        for h in range(NH):
            pe.wait_ge(S("a_z1"), h + 1)
            to_fm("aT1", h, Z)
        search()
        loaded("q_w")
        for h in range(NH):
            written(pe, ("aT1", h))
            fm(("aq", h), a_wq, 0, FT, half[h])
        search()
        loaded("k_w", "cv_w", "ctx")
        attention("a", a_wk, a_wcv, 2, 1)
        for h in range(NH):
            written(pe, ("aO", 4 * h + 3))
            to_fm("aOT", h, Y)
        search()
        loaded("mo_w")
        for h in range(NH):
            written(pe, ("aOT", h))
            tm(("amo", h), FT, h, a_mo, 2)
        search()
        for h in range(NH):
            pe.wait_ge(S("a_z2"), h + 1)
            to_fm("aT2", h, Z)
        search()
        loaded("lin1_w", "lin2_w")
        for h in range(NH):
            written(pe, ("aT2", h))
            for f in range(4):
                ffn_in(("af1", 0, h, f), a_l1, h)
            search()
        ffn_out("af1", "af2", 0, 0, 4, a_hid, a_l2)
        search()
        ffn_out("af1", "af2", 0, 1, 4, a_hid, a_l2)

        if upto >= 2:
            for h in range(NH):
                pe.wait_ge(S("b_z"), h + 1)
                to_fm("bT", h, Z)
            loaded("rq_w", "rqs_w", "rk_w", "rks_w")
            for h in range(NH):
                written(pe, ("bT", h))
                for n, w, n2, w2 in (("bq", b_wq, "bqs", b_wqs), ("bk", b_wk, "bks", b_wks)):
                    fm((n, h), w, 0, FT, half[h])
                    fm((n2, h), w2, 0, FT, half[h])
                    search()
            loaded("rv_w", "rg_w")
            for t in range(NT):
                for n, w in (("bv", b_wv), ("bg", b_wg)):
                    ps = claim(pe, (n, t))
                    for k in range(2):
                        ins = pe.matmul(ps, FT[:, k, t * P:(t + 1) * P], w[:, k, :], start=(k == 0), stop=(k == 1))
                    ins.then_inc(filled((n, t)), 1)
                search()
            for t in range(NT + 1):
                if t < NT:
                    if t % 2 == 0:
                        pe.wait_ge(S("b_qk"), 2 * (t // 2 + 1))
                    for hp in range(2):
                        ps = claim(pe, ("bS", t, hp)).rearrange("p (c n) -> p c n", n=SQ)
                        for bp in range(2):
                            tok = slice(t * P + bp * 64, t * P + bp * 64 + 64)
                            for c in range(2):
                                ins = pe.matmul(ps[bp * 64:bp * 64 + 64, c, :], FK[hp * 64:hp * 64 + 64, c, tok],
                                                FV[hp * 64:hp * 64 + 64, c, tok], start=True, stop=True)
                        ins.then_inc(filled(("bS", t, hp)), 1)
                if t > 0:
                    for hp in range(2):
                        written(pe, ("bS", t - 1, hp))
                    written(pe, ("bv", t - 1))
                    for bp in range(2):
                        ps = claim(pe, ("bO", t - 1, bp))
                        for hd in range(4):
                            at = slice(bp * 64, bp * 64 + 64)
                            ins = pe.matmul(ps[at, hd * P:(hd + 1) * P], PR[at, t - 1, hd * SQ:(hd + 1) * SQ],
                                            b_v[at, t - 1, hd * P:(hd + 1) * P], start=True, stop=True)
                        ins.then_inc(filled(("bO", t - 1, bp)), 1)
                if t < NT:
                    search()
            for t in range(NT):
                ps = claim(pe, ("bOT", t))
                pe.wait_ge(S("b_gated"), t + 1)
                for c in range(4):
                    ins = pe.transpose(ps[:, c * P:(c + 1) * P], b_o[:, t, c * P:(c + 1) * P], ident[:])
                ins.then_inc(filled(("bOT", t)), 1)
            search()
            loaded("ro_w")
            for h in range(NH):
                for t in (2 * h, 2 * h + 1):
                    written(pe, ("bOT", t))
                tm(("bwo", h), b_ot, h, b_wo, 4)

        if upto >= 3:
            for h in range(NH):
                pe.wait_ge(S("c_z"), h + 1)
                to_fm("cT", h, Z)
            search()
            for h in range(NH):
                pe.wait_ge(S("c_y"), h + 1)
                to_fm("cT2", h, Y)
            search()
            loaded("Wr", "ffn_w1", "ffn_w2")
            for h in range(NH):
                written(pe, ("cT2", h))
                tm(("cr", h), FV, h, Wr, 2, 8)
            search()
            for h in range(NH):
                written(pe, ("cT", h))
            for e in range(2):
                if e == 1:
                    pe.wait_ge(S("perturbed"), 3)
                for h in range(NH):
                    for f in range(4):
                        ffn_in(("c1", e, h, f), c_w1[e], h)
                        if e == 0 and (h, f) < (1, 2):
                            search()
                if e == 1:
                    pe.wait_ge(S("perturbed"), 4)
                for h in range(NH):
                    ffn_out("c1", "c2", e, h, 4, c_hid[e], c_w2[e])

        if upto >= 4:
            for h in range(NH):
                pe.wait_ge(S("d_z"), h + 1)
                to_fm("dT", h, Z)
            loaded("xq_w", "xk_w", "xv_w")
            for h in range(NH):
                written(pe, ("dT", h))
                fm(("dq", h), d_wq, 0, FT, half[h])
            attention("d", d_wk, d_wv, 4, 0)
            loaded("xo_w")
            for h in range(NH):
                written(pe, ("dO", 4 * h + 3))
                to_fm("dOT", h, Y)
            for h in range(NH):
                written(pe, ("dOT", h))
                tm(("dmo", h), FT, h, d_wo, 2)

        if upto >= 5:
            for h in range(NH):
                pe.wait_ge(S("e_z"), h + 1)
                to_fm("eT", h, Z)
            loaded("eq_w", "ek_w", "ev_w", "eo_w")
            for h in range(NH):
                written(pe, ("eT", h))
                for n, w in (("eq", e_wq), ("ek", e_wk)):
                    for c in range(4):
                        fm((n, h, c), w, 2 * c, FT, half[h])
                for t in (2 * h, 2 * h + 1):
                    for n in range(2):
                        ps = claim(pe, ("ev", t, n))
                        for k in range(2):
                            ins = pe.matmul(ps, FT[:, k, t * P:(t + 1) * P], e_wv[:, k, n * 512:(n + 1) * 512],
                                            start=(k == 0), stop=(k == 1))
                        ins.then_inc(filled(("ev", t, n)), 1)
                for c in range(4):
                    written(pe, ("eq", h, c))
                    written(pe, ("ek", h, c))
                for t in (2 * h, 2 * h + 1):
                    for bp in range(2):
                        tok = slice((t % 2) * P + bp * 64, (t % 2) * P + bp * 64 + 64)
                        for hp in range(2):
                            ps = claim(pe, ("eS", t, bp, hp)).rearrange("p (c n) -> p c n", n=SQ)
                            at = slice(hp * 64, hp * 64 + 64)
                            for pr in range(8):
                                ins = pe.matmul(ps[at, pr, :], e_q[at, pr, tok], e_k[at, pr, tok],
                                                start=True, stop=True)
                            ins.then_inc(filled(("eS", t, bp, hp)), 1)
                for t in (2 * h, 2 * h + 1):
                    pe.wait_ge(S("e_p"), t + 1)
                    for s in range(2):
                        ps = claim(pe, ("ePT", t, s))
                        for i in range(4):
                            pr = 4 * s + i
                            src = PR[:, 2 * (t % 2):2 * (t % 2) + 2, :].rearrange("p a n -> p (a n)")
                            ins = pe.transpose(ps[:, i * P:(i + 1) * P], src[:, pr * P:(pr + 1) * P], ident[:])
                        ins.then_inc(filled(("ePT", t, s)), 1)
                    for n in range(2):
                        written(pe, ("ev", t, n))
                        written(pe, ("ePT", t, n))
                    for bp in range(2):
                        at = slice(bp * 64, bp * 64 + 64)
                        for n in range(2):
                            ps = claim(pe, ("eO", t, bp, n))
                            for i in range(8):
                                hd = 8 * n + i
                                pr, hp = hd // 2, hd % 2
                                ins = pe.matmul(ps[at, i * SQ:(i + 1) * SQ],
                                                PT[at, 2 * (t % 2) + pr // 4, (pr % 4) * P + hp * 64:(pr % 4) * P + hp * 64 + 64],
                                                e_v[at, t % 2, hd * SQ:(hd + 1) * SQ], start=True, stop=True)
                            ins.then_inc(filled(("eO", t, bp, n)), 1)
                for t in (2 * h, 2 * h + 1):
                    for bp in range(2):
                        for n in range(2):
                            written(pe, ("eO", t, bp, n))
                    for s in range(2):
                        ps = claim(pe, ("eOT", t, s))
                        for i in range(4):
                            c = 4 * s + i
                            ins = pe.transpose(ps[:, i * P:(i + 1) * P], e_o[:, t % 2, c * P:(c + 1) * P], ident[:])
                        ins.then_inc(filled(("eOT", t, s)), 1)
                for t in (2 * h, 2 * h + 1):
                    for s in range(2):
                        written(pe, ("eOT", t, s))
                tm(("ewo", h), e_q, h, e_wo, 8, t0=0)

        if upto >= 6:
            for h in range(NH):
                pe.wait_ge(S("f_z"), h + 1)
                to_fm("fT", h, Z)
            loaded("gw")
            for h in range(NH):
                written(pe, ("fT", h))
                tm(("fg", h), FT, h, gw, 2, 12)
            seq = [(e, h) for e in range(NE) for h in range(NH)]
            for i in range(len(seq) + 1):
                if i < len(seq):
                    e, h = seq[i]
                    pe.wait_ge(S(f"ld_f{e % 2}"), 32 * (e // 2 + 1))
                    for f in range(2):
                        ffn_in(("f1", e, h, f), f_w1[e % 2], h)
                if i > 0:
                    e, h = seq[i - 1]
                    ffn_out("f1", "f2", e, h, 2, f_hid[e % 2], f_w2[e % 2])

    @block.scalar
    def _(act):
        chain = [0]
        steps_done = [0]
        norms = [0]

        def link(ins):
            chain[0] += 1
            ins.then_inc(S("act_chain"), 1)
            act.wait_ge(S("act_chain"), chain[0])

        def norm():
            n = norms[0]
            norms[0] += 1
            act.wait_ge(S("var_ready"), n + 1)
            t = tiles[n % 2]
            link(act.activation(lnv[:, t], mv[:, t, 1], ACT.Ln, bias=eps[:]))
            act.activation(rstd[:, t], lnv[:, t], ACT.Exp, scale=-0.5).then_inc(S("rstd_ready"), 1)

        def copy_fm(name, dst, bias=None, scale=1.0, func=ACT.Identity):
            ps = finished(act, name).rearrange("p (c n) -> p c n", c=2)
            if bias is None:
                act.activation(dst, ps, ACT.Copy, scale=scale).then_inc(taken(name), 1)
                return
            for c in range(2):
                ins = act.activation(dst[:, c, :], ps[:, c, :], func, bias=bias[c])
            ins.then_inc(taken(name), 1)

        def search():
            s = steps_done[0]
            steps_done[0] += 1
            act.wait_ge(S("cand_ready"), s + 1)
            act.activation(smask[:, 0, :], KEY[:, 0, :], ACT.Sign, bias=nbias[:], accum_out=signs[:])\
               .then_inc(S("signs_ready"), 1)

        def bias2(name, at=0):
            return [col(name, at), col(name, at + 1)]

        def attention(p, n_s, kb):
            def keys_values(b):
                if b >= 2:
                    finished(act, (p + "S", b - 2, n_s - 1))
                copy_fm((p + "K", b), KT[:, b % 2], bias2(kb))
                if p == "a" and b:
                    search()
                if b >= 2:
                    finished(act, (p + "O", b - 2))
                copy_fm((p + "V", b), VB[:, b % 2])

            keys_values(0)
            for b in range(NB):
                for s in range(n_s):
                    n = n_s * b + s
                    r = n % 4
                    if p == "a" and s == 0:
                        search()
                    act.wait_ge(S(p + "_max"), n + 1)
                    if b >= 2:
                        written(act, (p + "O", b - 2))
                    if p == "a":
                        ps = finished(act, ("aS", b, s))
                        if n >= 4:
                            finished(act, ("aPT", *divmod(n - 4, n_s)))
                    else:
                        ps = PR[:, r, :]
                    for pr in range(2):
                        j = 2 * s + pr
                        ins = act.activation(PR[:, r, pr * 256:(pr + 1) * 256], ps[:, pr * 256:(pr + 1) * 256],
                                             ACT.Exp, bias=nmx[:, b % 2, j:j + 1],
                                             accum_out=sums[:, b % 2, j:j + 1])
                    ins.then_inc(taken(("aS", b, s)) if p == "a" else S("d_p"), 1)
                if b + 1 < NB:
                    keys_values(b + 1)
                elif p == "a":
                    search()

        def ffn(one, n_e, n_f, hid, func, biases, before, searching=()):
            for e in range(n_e):
                for h in range(NH):
                    before(e, h)
                    for f in range(n_f):
                        name = (one, e, h, f)
                        dst = hid[e % 2][:, 2 * f:2 * f + 2, half[h]]
                        if biases is None:
                            ps = finished(act, name).rearrange("p (c n) -> p c n", c=2)
                            act.activation(dst, ps, func).then_inc(taken(name), 1)
                        else:
                            copy_fm(name, dst, biases(e, f), func=func)
                        if (e, h, f) in searching:
                            search()

        TABLE = "natural_log_exp_and_others"
        act.preload_act_table_set(TABLE)
        act.wait_ge(S("eps_ready"), 1)
        act.wait_ge(S("ld_cols"), 16)
        norm()
        norm()
        for h in range(NH):
            copy_fm(("aT0", h), FT[:, :, half[h]])
        for h in range(NH):
            copy_fm(("av", h), FV[:, :, half[h]], bias2("v_b"))
        search()
        norm()
        norm()
        for h in range(NH):
            copy_fm(("aT1", h), FT[:, :, half[h]])
        search()
        attention("a", 2, "k_b")
        for h in range(NH):
            copy_fm(("aOT", h), FT[:, :, half[h]], bias2("cv_b"))
        search()
        norm()
        norm()
        for h in range(NH):
            copy_fm(("aT2", h), FT[:, :, half[h]])
        search()
        ffn("af1", 1, 4, [a_hid], ACT.Relu, lambda e, f: bias2("lin1_b", 2 * f), lambda e, h: None, [(0, 1, 3)])
        norm()
        norm()

        if upto >= 2:
            norm()
            norm()
            for h in range(NH):
                copy_fm(("bT", h), FT[:, :, half[h]])
            search()
            search()
            for t in range(NT):
                act.activation(b_v[:, t, :], finished(act, ("bv", t)), ACT.Copy).then_inc(taken(("bv", t)), 1)
                act.activation(b_g[:, t, :], finished(act, ("bg", t)), ACT.Silu).then_inc(taken(("bg", t)), 1)
                if t % 2 == 0:
                    search()
            act.preload_act_table_set(TABLE)
            search()
            search()
            for t in range(NT):
                for bp in range(2):
                    at = slice(bp * 64, bp * 64 + 64)
                    ps = finished(act, ("bO", t, bp))
                    act.activation(b_o[at, t, :], ps[at, :], ACT.Copy).then_inc(taken(("bO", t, bp)), 1)
                act.wait_ge(S("b_ms"), t + 1)
                link(act.activation(ms[:, t, :], ms[:, t, :], ACT.Ln, bias=eps[:], scale=1.0 / 128))
                act.activation(ms[:, t, :], ms[:, t, :], ACT.Exp, scale=-0.5).then_inc(S("b_rms"), 1)
            for t in range(NT):
                ps = finished(act, ("bOT", t)).rearrange("p (c n) -> p c n", c=4)
                act.activation(b_ot[:, :, t * P:(t + 1) * P], ps, ACT.Copy).then_inc(taken(("bOT", t)), 1)
            search()

        if upto >= 3:
            norm()
            norm()
            for h in range(NH):
                copy_fm(("cT", h), FT[:, :, half[h]])
            norm()
            norm()
            for h in range(NH):
                copy_fm(("cT2", h), FV[:, :, half[h]])
            search()
            act.wait_ge(S("c_shifted"), 1)
            act.activation(lgt[:, :, 0:8], lgt[:, :, 0:8], ACT.Exp).then_inc(S("c_exp"), 1)

            def c_before(e, h):
                if e == 1:
                    act.wait_ge(S("perturbed"), 3)
            ffn("c1", 2, 4, c_hid, ACT.Gelu_apprx_tanh,
                lambda e, f: (bias2("ffn_b1", 2 * f) if e == 0 else
                              [bp_col[:, 2 * f:2 * f + 1], bp_col[:, 2 * f + 1:2 * f + 2]]), c_before,
                [(0, 0, 0), (0, 0, 2), (0, 1, 0)])
            act.preload_act_table_set(TABLE)

        if upto >= 4:
            norm()
            norm()
            for h in range(NH):
                copy_fm(("dT", h), FT[:, :, half[h]])
            attention("d", 4, "xk_b")
            for h in range(NH):
                copy_fm(("dOT", h), FT[:, :, half[h]], bias2("xv_b"))

        if upto >= 5:
            norm()
            norm()
            for h in range(NH):
                copy_fm(("eT", h), FT[:, :, half[h]])
            for h in range(NH):
                if h:
                    finished(act, ("ewo", h - 1))
                for c in range(4):
                    copy_fm(("eq", h, c), e_q[:, 2 * c:2 * c + 2, :], scale=0.125)
                for c in range(4):
                    copy_fm(("ek", h, c), e_k[:, 2 * c:2 * c + 2, :])
                for t in (2 * h, 2 * h + 1):
                    for n in range(2):
                        ps = finished(act, ("ev", t, n))
                        act.activation(e_v[:, t % 2, n * 512:(n + 1) * 512], ps, ACT.Copy)\
                           .then_inc(taken(("ev", t, n)), 1)
                for t in (2 * h, 2 * h + 1):
                    act.wait_ge(S("e_shifted"), t + 1)
                    p2 = PR[:, 2 * (t % 2):2 * (t % 2) + 2, :]
                    act.activation(p2, p2, ACT.Exp).then_inc(S("e_exp"), 1)
                for t in (2 * h, 2 * h + 1):
                    for bp in range(2):
                        at = slice(bp * 64, bp * 64 + 64)
                        for n in range(2):
                            ps = finished(act, ("eO", t, bp, n))
                            act.activation(e_o[at, t % 2, n * 512:(n + 1) * 512], ps[at, :], ACT.Copy)\
                               .then_inc(taken(("eO", t, bp, n)), 1)
                for t in (2 * h, 2 * h + 1):
                    for s in range(2):
                        ps = finished(act, ("eOT", t, s)).rearrange("p (c n) -> p c n", c=4)
                        act.activation(e_q[:, 4 * s:4 * s + 4, (t % 2) * P:(t % 2 + 1) * P], ps, ACT.Copy)\
                           .then_inc(taken(("eOT", t, s)), 1)

        if upto >= 6:
            norm()
            norm()
            for h in range(NH):
                copy_fm(("fT", h), FT[:, :, half[h]])
            act.wait_ge(S("f_gap"), 1)
            act.activation(sm[:, 0:4], sm[:, 0:4], ACT.Exp).then_inc(S("f_exp"), 1)

            def f_before(e, h):
                if e >= 2:
                    finished(act, ("f2", e - 2, h))
            ffn("f1", NE, 2, f_hid, ACT.Silu, None, f_before)

    @block.vector
    def _(dve):
        chain = [0]
        norms = [0]
        parts = [0]
        perturbed = [0]
        scratch = [QD[:].rearrange("p a c h n -> p (a c h n)"), PT[:].rearrange("p a n -> p (a n)")]

        def link(ins):
            chain[0] += 1
            ins.then_inc(S("dve_chain"), 1)
            dve.wait_ge(S("dve_chain"), chain[0])

        def statistics(h, src):
            for t in (2 * h, 2 * h + 1):
                ins = dve.bn_stats(st[:, t, :], src[:, t, :])
            link(ins)
            for t in (2 * h, 2 * h + 1):
                ins = dve.bn_aggr(mv[:, t, :], st[:, t, :])
            norms[0] += 1
            ins.then_inc(S("var_ready"), 1)

        def normalise(h, src, dst, n, signal, gain=None, shift=None):
            dve.wait_ge(S("rstd_ready"), n)
            for t in (2 * h, 2 * h + 1):
                if gain is None:
                    ins = dve.tensor_scalar(dst[:, t, :], src[:, t, :], mv[:, t, 0:1], rstd[:, t:t + 1],
                                            ALU.subtract, ALU.mult)
                else:
                    link(dve.scalar_tensor_tensor(out=Y[:, t, :], in0=src[:, t, :], scalar=mv[:, t, 0:1],
                                                  in1=row(gain), op0=ALU.subtract, op1=ALU.mult))
                    ins = dve.scalar_tensor_tensor(out=dst[:, t, :], in0=Y[:, t, :], scalar=rstd[:, t:t + 1],
                                                   in1=row(shift), op0=ALU.mult, op1=ALU.add)
            if signal is None:
                link(ins)
            else:
                ins.then_inc(S(signal), 1)

        def plain_norm(signal, src=X, dst=Z, gain=None, shift=None):
            for h in range(NH):
                statistics(h, src)
            for h in range(NH):
                normalise(h, src, dst, norms[0] - 1 + h, signal, gain, shift)

        def add_norm(name, bias, signal, gain, shift, between=None):
            for h in range(NH):
                job = (*name, h)
                ps = finished(dve, job).rearrange("p (c n) -> p c n", c=2)
                dve.tensor_tensor(Y[:, tiles[h], :], ps, Z[:, tiles[h], :], ALU.add).then_inc(taken(job), 1)
                written(dve, job)
                link(dve.tensor_tensor(Y[:, tiles[h], :], Y[:, tiles[h], :], over(row(bias), 2), ALU.add))
                statistics(h, Y)
            for h in range(NH):
                normalise(h, Y, Z, norms[0] - 1 + h, signal, gain, shift)

        w1f, w2f = RC[:, 0:2048], RC[:, 2048:4096]
        b1c = cols[:, COL_AT["ffn_b1"]:COL_AT["ffn_b1"] + 8]
        b2c = cols[:, COL_AT["ffn_b2"]:COL_AT["ffn_b2"] + 2]
        srcs = [w1f, w2f, w1f, w2f, b1c, b2c, b1c, b2c]

        def key(q, phase):
            if q >= 4:
                return bkey[:, q - 4, 0:srcs[q].shape[1]]
            return KEY[:, q if phase else q % 2, :]

        def keys_high():
            for n in ("ffn_w1", "ffn_w2", "kwant"):
                dve.wait_ge(S("ld_" + n), 16)
            dve.wait_ge(S("ld_cols"), 16)
            link(dve.memset(bkey[:], 65535))
            for q in (0, 1, 4, 5, 6, 7):
                ins = dve.tensor_scalar(key(q, 0), srcs[q].bitcast(U16)[:, 1::2], 0x7FFF, None, ALU.bitwise_and)
            link(ins)
            dve.memset(cur[:], 0.0)
            link(dve.tensor_copy(kleft[:], kwant[:]))

        def keys_low():
            link(dve.tensor_copy(thr[:, 0, :], cur[:]))
            for q in (2, 3, 0, 1, 4, 5, 6, 7):
                link(dve.tensor_scalar(key(q, 1), key(q, 0), cur[:, q:q + 1], 65535.0, ALU.not_equal, ALU.mult))
                link(dve.tensor_tensor(key(q, 1), key(q, 1), srcs[q].bitcast(U16)[:, 0::2], ALU.max))
            link(dve.memset(cur[:], 0.0))

        def bit(s):
            return 0.0 if s == NSTEP1 else float(1 << (14 - s if s < NSTEP1 else 31 - s))

        def compare(s):
            if s == 0:
                keys_high()
            if s == NSTEP1 + 1:
                keys_low()
            phase = int(s > NSTEP1)
            dve.tensor_scalar(cand[:], cur[:], bit(s), None, ALU.add)
            dve.tensor_scalar(nbias[:], cur[:, 0:1], -1.0, 0.5 - bit(s), ALU.mult, ALU.add).then_inc(S("cand_ready"), 1)
            dve.wait_ge(S("cand_ready"), s + 1)
            for q in range(1, 4):
                dve.tensor_scalar(smask[:, q, :], key(q, phase), cand[:, q:q + 1], None, ALU.is_lt)\
                   .then_inc(S("smask_ready"), 1)
            link(dve.tensor_tensor(below[:], bkey[:], each(cand[:, 4:8], 8), ALU.is_lt))
            dve.tensor_reduce(cnt[:, 4:8], below[:], AX.X, ALU.add)

        def search():
            s, summing = divmod(parts[0], 2)
            parts[0] += 1
            if not summing:
                dve.wait_ge(S("signs_ready"), s + 1)
                dve.tensor_scalar(cnt[:, 0:1], signs[:], -0.5, LIN * D / P / 2, ALU.mult, ALU.add)
                ps = finished(dve, ("cnt", s))
                dve.tensor_copy(cnt[:, 1:4], ps[:, 1:4]).then_inc(taken(("cnt", s)), 1)
                return
            ps = finished(dve, ("tot", s))
            if s == NSTEP1:
                dve.tensor_tensor(kleft[:], kleft[:], ps[:, 0:8], ALU.subtract).then_inc(taken(("tot", s)), 1)
                written(dve, ("tot", s))
            else:
                dve.tensor_tensor(sm[:, 192:200], ps[:, 0:8], kleft[:], ALU.is_lt).then_inc(taken(("tot", s)), 1)
                written(dve, ("tot", s))
                link(dve.scalar_tensor_tensor(out=cur[:], in0=sm[:, 192:200], scalar=bit(s), in1=cur[:],
                                              op0=ALU.mult, op1=ALU.add))
            if s + 1 < N_SEARCH:
                compare(s + 1)

        def bounds():
            link(dve.tensor_copy(thr[:, 1, :], cur[:]))
            hi, lo = bound[:].bitcast(I32), sm[:, 208:216].bitcast(I32)
            dve.tensor_copy(hi, thr[:, 0, :])
            link(dve.tensor_copy(lo, thr[:, 1, :]))
            link(dve.tensor_scalar(hi, hi, 16, None, ALU.logical_shift_left))
            link(dve.tensor_tensor(hi, hi, lo, ALU.bitwise_or))
            for a in (0, 4):
                low, apart = bound[:, a + 2:a + 4], sm[:, 216:218]
                link(dve.tensor_tensor(apart, bound[:, a:a + 2], low, ALU.is_gt))
                link(dve.tensor_tensor(low, low, apart, ALU.mult))
                link(dve.scalar_tensor_tensor(out=low, in0=apart, scalar=-1.0, in1=low, op0=ALU.add, op1=ALU.add))

        def perturb(src, dst, q):
            n = src.shape[1]
            t1, t2 = scratch[0][:, 0:n], scratch[1][:, 0:n]
            link(dve.tensor_scalar(t1.bitcast(I32), src.bitcast(I32), 0x7FFFFFFF, None, ALU.bitwise_and))
            link(dve.tensor_scalar(t2, t1, bound[:, q:q + 1], None, ALU.is_ge))
            link(dve.scalar_tensor_tensor(out=t2, in0=t1, scalar=bound[:, q + 2:q + 3], in1=t2,
                                          op0=ALU.is_le, op1=ALU.subtract))
            link(dve.scalar_tensor_tensor(out=t2, in0=t2, scalar=0.8, in1=src, op0=ALU.mult, op1=ALU.mult))
            dve.tensor_tensor(dst, src, t2, ALU.add).then_inc(S("perturbed"), 1)
            perturbed[0] += 1
            dve.wait_ge(S("perturbed"), perturbed[0])

        def attention(p, n_s, dk):
            w = 2 * dk

            def transposed(b, s):
                n = n_s * b + s
                ps = finished(dve, (p + "PT", b, s))
                if n >= 4:
                    finished(dve, (p + "O", (n - 4) // n_s))
                dve.tensor_copy(PT[:, n % 4, :], ps).then_inc(taken((p + "PT", b, s)), 1)

            for i in range(NB + 1):
                for s in range(n_s):
                    if i < NB:
                        n = n_s * i + s
                        ps = finished(dve, (p + "S", i, s)).rearrange("p (c n) -> p c n", c=2)
                        if p == "a":
                            if i >= 2:
                                written(dve, ("aS", i - 2, n_s - 1))
                            dve.tensor_reduce(nmx[:, i % 2, 2 * s:2 * s + 2], ps, AX.X, ALU.max, negate=True)\
                               .then_inc(S("a_max"), 1)
                        else:
                            if n >= 4:
                                finished(dve, ("dPT", *divmod(n - 4, n_s)))
                            for pr in range(2):
                                j = 2 * s + pr
                                ins = dve.tensor_tensor_reduce(
                                    PR[:, n % 4, pr * 256:(pr + 1) * 256], ps[:, pr, :], d_mask[:, i, :],
                                    rany[:, i:i + 1], -3.0e38, ALU.add, ALU.max, rmx[:, i % 2, j:j + 1])
                            ins.then_inc(taken(("dS", i, s)), 1)
                            written(dve, ("dS", i, s))
                            dve.tensor_scalar(nmx[:, i % 2, 2 * s:2 * s + 2], rmx[:, i % 2, 2 * s:2 * s + 2], -1.0,
                                              None, ALU.mult).then_inc(S("d_max"), 1)
                    if i > 0:
                        transposed(i - 1, s)
                    if p == "a" and i < NB:
                        search()
                if p == "a" and i < NB:
                    search()
                if i > 0:
                    b = i - 1
                    if p == "a":
                        written(dve, ("aS", b, n_s - 1))
                    else:
                        dve.wait_ge(S("d_p"), n_s * i)
                    link(dve.reciprocal(rinv[:, b % 2, 0:2 * n_s], sums[:, b % 2, 0:2 * n_s]))
                    ps = finished(dve, (p + "O", b))[:, 0:2 * n_s * w].rearrange("p (j n) -> p j n", n=w)
                    at = slice((b % 2) * 64, (b % 2) * 64 + 64)
                    for hp in range(2):
                        f = slice(hp * 64, hp * 64 + 64)
                        dst = Y[at, b // 2, :].rearrange("p (j n) -> p j n", n=w)[:, :, hp * dk:(hp + 1) * dk]
                        ins = dve.tensor_tensor(dst, ps[f, :, hp * dk:(hp + 1) * dk],
                                                each(rinv[f, b % 2, 0:2 * n_s], dk), ALU.mult)
                    ins.then_inc(taken((p + "O", b)), 1)
                if p == "a" and i < NB:
                    search()

        dve.memset(eps[:], EPS).then_inc(S("eps_ready"), 1)
        dve.memset(onesb[:], 1.0).then_inc(S("ones_ready"), 1)
        dve.memset(onesf[:], 1.0).then_inc(S("ones_ready"), 1)

        for h in range(NH):
            dve.wait_ge(S(f"ld_x{h}"), 32)
            statistics(h, X)
        for h in range(NH):
            normalise(h, X, Z, norms[0] - 1 + h, "a_z0")
        dve.wait_ge(S("a_z0"), 2)
        compare(0)
        search()
        dve.wait_ge(S("ld_rows"), 16)
        add_norm(("aso",), "so_b", "a_z1", "ln1_g", "ln1_b")
        search()
        search()
        dve.wait_ge(S("ld_cols"), 16)
        for h in range(NH):
            ps = finished(dve, ("aq", h)).rearrange("p (c n) -> p c n", c=2)
            for c in range(2):
                ins = dve.tensor_scalar(FV[:, c, half[h]], ps[:, c, :], col("q_b", c), 32.0 ** -0.5, ALU.add, ALU.mult)
            ins.then_inc(taken(("aq", h)), 1)
        search()
        attention("a", 2, 32)
        dve.wait_ge(S("a_z1"), 2)
        search()
        for h in range(NH):
            finished(dve, ("aOT", h))
        add_norm(("amo",), "mo_b", "a_z2", "ln2_g", "ln2_b")
        dve.wait_ge(S("a_z2"), 2)
        for _ in range(5):
            search()
        add_norm(("af2", 0), "lin2_b", None, "ln3_g", "ln3_b")
        for h in range(NH):
            ins = dve.tensor_tensor(X[:, tiles[h], :], X[:, tiles[h], :], Z[:, tiles[h], :], ALU.add)
            if upto == 1:
                ins.then_inc(S("x_final"), 1)
            else:
                link(ins)

        if upto >= 2:
            plain_norm("b_z")
            for n in ("rot", "decay"):
                dve.wait_ge(S("ld_" + n), 16)
            for h in range(NH):
                for a, b, dst in (("bq", "bqs", FV), ("bk", "bks", FK)):
                    ps = finished(dve, (a, h)).rearrange("p (c m s) -> p c m s", c=2, s=SQ)
                    for c in range(2):
                        ins = dve.tensor_tensor(dst[:, c, half[h]].rearrange("p (m s) -> p m s", s=SQ), ps[:, c],
                                                over(rot[:, 0, :], 4), ALU.mult)
                    ins.then_inc(taken((a, h)), 1)
                    ps = finished(dve, (b, h)).rearrange("p (m s) -> p m s", s=SQ)
                    y = Y[:, tiles[h], :].rearrange("p t (m s) -> p (t m) s", s=SQ)
                    dve.tensor_tensor(y, ps, over(rot[:, 1, :], 8), ALU.mult).then_inc(taken((b, h)), 1)
                    written(dve, (b, h))
                    d = dst[:, :, half[h]]
                    dve.tensor_tensor(d, d, Y[:, tiles[h], :], ALU.add).then_inc(S("b_qk"), 1)
                    dve.wait_ge(S("b_qk"), 2 * h + (1 if dst is FV else 2))
                    search()
            for t in range(NT):
                search()
            for t in range(NT):
                for hp in range(2):
                    ps = finished(dve, ("bS", t, hp)).rearrange("p (c n) -> p c n", n=SQ)
                    dst = PR[:, t, 0:256].rearrange("p (c g n) -> p c g n", c=2, g=2)[:, :, hp, :]
                    dec = decay[:].rearrange("p (c g) n -> p c g n", g=2)[:, :, hp, :]
                    dve.tensor_tensor(dst, ps[:, 0:2, :], dec, ALU.mult).then_inc(taken(("bS", t, hp)), 1)
                search()
            sq = QD[:, 0].rearrange("p c h n -> p (c h n)")[:, 0:512]
            for t in range(NT):
                for bp in range(2):
                    written(dve, ("bO", t, bp))
                link(dve.tensor_tensor(sq, b_o[:, t, :], b_o[:, t, :], ALU.mult))
                dve.tensor_reduce(ms[:, t, :], sq.rearrange("p (a n) -> p a n", a=4), AX.X, ALU.add)\
                   .then_inc(S("b_ms"), 1)
                o4 = b_o[:, t, :].rearrange("p (a n) -> p a n", a=4)
                dve.wait_ge(S("b_rms"), t + 1)
                link(dve.tensor_tensor(o4, o4, each(ms[:, t, :], 128), ALU.mult))
                dve.wait_ge(S("b_gain"), t + 1)
                dve.tensor_tensor(b_o[:, t, :], b_o[:, t, :], b_g[:, t, :], ALU.mult).then_inc(S("b_gated"), 1)
            search()
            for h in range(NH):
                ps = finished(dve, ("bwo", h)).rearrange("p (c n) -> p c n", c=2)
                dve.tensor_tensor(X[:, tiles[h], :], X[:, tiles[h], :], ps, ALU.add).then_inc(taken(("bwo", h)), 1)
                written(dve, ("bwo", h))

        if upto >= 3:
            plain_norm("c_z")
            dve.wait_ge(S("c_z"), 2)
            search()
            plain_norm("c_y", Z, Y, "f_g", "f_b")
            search()
            for h in range(NH):
                ps = finished(dve, ("cr", h)).rearrange("p (c n) -> p c n", c=2)
                dve.tensor_tensor(lgt[:, tiles[h], 0:8], ps[:, :, 0:8], over(row("br"), 2), ALU.add)\
                   .then_inc(taken(("cr", h)), 1)
                written(dve, ("cr", h))
            lg = lgt[:, :, 0:8]
            link(dve.tensor_reduce(sm[:, 16:20], lg, AX.X, ALU.max))
            dve.tensor_tensor(lg, lg, each(sm[:, 16:20], 8), ALU.subtract).then_inc(S("c_shifted"), 1)
            search()
            dve.wait_ge(S("c_exp"), 1)
            dve.tensor_reduce(sm[:, 20:24], lg, AX.X, ALU.add)
            link(dve.tensor_reduce(sm[:, 24:28], lgt[:, :, 1:8], AX.X, ALU.add))
            link(dve.reciprocal(sm[:, 20:24], sm[:, 20:24]))
            w_clean, w_others = sm[:, 32:36], sm[:, 36:40]
            dve.tensor_tensor(w_clean, lgt[:, :, 0], sm[:, 20:24], ALU.mult)
            link(dve.tensor_tensor(w_others, sm[:, 24:28], sm[:, 20:24], ALU.mult))
            for _ in range(6):
                search()
            bounds()
            perturb(b1c, bp_col[:], 4)
            perturb(row("ffn_b2"), bp_row[:], 5)
            perturb(w1f, RC[:, 4096:6144], 0)

            def add_expert(e, weight, b2):
                for t in range(NT):
                    ins = dve.scalar_tensor_tensor(out=X[:, t, :], in0=b2, scalar=weight[:, t:t + 1], in1=X[:, t, :],
                                                   op0=ALU.mult, op1=ALU.add)
                link(ins)
                for h in range(NH):
                    ps = finished(dve, ("c2", e, h)).rearrange("p (c n) -> p c n", c=2)
                    for t in (2 * h, 2 * h + 1):
                        ins = dve.scalar_tensor_tensor(out=X[:, t, :], in0=ps[:, t % 2, :],
                                                       scalar=weight[:, t:t + 1],
                                                       in1=X[:, t, :], op0=ALU.mult, op1=ALU.add)
                    ins.then_inc(taken(("c2", e, h)), 1)
                    written(dve, ("c2", e, h))

            add_expert(0, w_clean, row("ffn_b2"))
            perturb(w2f, RC[:, 6144:8192], 1)
            add_expert(1, w_others, bp_row[:])

        if upto >= 4:
            plain_norm("d_z")
            dve.wait_ge(S("d_z"), 2)
            link(dve.tensor_tensor(X[:], X[:], over(row("xo_b"), 4), ALU.add))
            dve.wait_ge(S("ld_mask"), 32)
            link(dve.tensor_scalar(d_mask, d_mask, 0.0, NEG, ALU.is_equal, ALU.mult))
            link(dve.tensor_reduce(rany[:], d_mask, AX.X, ALU.max))
            link(dve.tensor_scalar(rany[:], rany[:], 0.0, None, ALU.is_ge))
            for h in range(NH):
                ps = finished(dve, ("dq", h)).rearrange("p (c n) -> p c n", c=2)
                for c in range(2):
                    ins = dve.tensor_scalar(FV[:, c, half[h]], ps[:, c, :], col("xq_b", c), 0.25, ALU.add, ALU.mult)
                ins.then_inc(taken(("dq", h)), 1)
            attention("d", 4, 16)
            for h in range(NH):
                ps = finished(dve, ("dmo", h)).rearrange("p (c n) -> p c n", c=2)
                xs = X[:, tiles[h], :]
                dve.tensor_tensor(xs, xs, ps, ALU.add).then_inc(taken(("dmo", h)), 1)
                written(dve, ("dmo", h))

        if upto >= 5:
            plain_norm("e_z")
            dve.wait_ge(S("ld_rbias"), 16)
            dve.wait_ge(S("ld_causal"), 16)
            link(dve.tensor_tensor(e_bias, e_bias, over(e_causal, 8), ALU.add))
            for h in range(NH):
                for t in (2 * h, 2 * h + 1):
                    p2 = PR[:, 2 * (t % 2):2 * (t % 2) + 2, :].rearrange("p a n -> p (a n)")
                    if t >= 2:
                        finished(dve, ("ePT", t - 2, 1))
                    for bp in range(2):
                        for hp in range(2):
                            at = slice(hp * 64, hp * 64 + 64)
                            ps = finished(dve, ("eS", t, bp, hp)).rearrange("p (c n) -> p c n", n=SQ)
                            dst = p2.rearrange("p (c g n) -> p c g n", c=8, g=2)[at, :, bp, :]
                            dve.tensor_tensor(dst, ps[at], e_bias[at], ALU.add).then_inc(taken(("eS", t, bp, hp)), 1)
                            written(dve, ("eS", t, bp, hp))
                    pv = p2.rearrange("p (c n) -> p c n", n=SQ)
                    mx = sm[:, 64 + 16 * (t % 2):80 + 16 * (t % 2)]
                    link(dve.tensor_reduce(mx, pv, AX.X, ALU.max))
                    dve.tensor_tensor(pv, pv, each(mx, SQ), ALU.subtract).then_inc(S("e_shifted"), 1)
                for t in (2 * h, 2 * h + 1):
                    p2 = PR[:, 2 * (t % 2):2 * (t % 2) + 2, :].rearrange("p a n -> p (a n)")
                    pv = p2.rearrange("p (c n) -> p c n", n=SQ)
                    mx = sm[:, 64 + 16 * (t % 2):80 + 16 * (t % 2)]
                    dve.wait_ge(S("e_exp"), t + 1)
                    link(dve.tensor_reduce(mx, pv, AX.X, ALU.add))
                    link(dve.reciprocal(mx, mx))
                    dve.tensor_tensor(pv, pv, each(mx, SQ), ALU.mult).then_inc(S("e_p"), 1)
                for t in (2 * h, 2 * h + 1):
                    for s in range(2):
                        ps = finished(dve, ("ePT", t, s))
                        if t >= 2:
                            finished(dve, ("eO", t - 2, 1, 1))
                        dve.tensor_copy(PT[:, 2 * (t % 2) + s, :], ps).then_inc(taken(("ePT", t, s)), 1)
                ps = finished(dve, ("ewo", h)).rearrange("p (c n) -> p c n", c=2)
                dve.tensor_tensor(X[:, tiles[h], :], X[:, tiles[h], :], ps, ALU.add).then_inc(taken(("ewo", h)), 1)
                written(dve, ("ewo", h))

        if upto >= 6:
            plain_norm("f_z")
            dve.wait_ge(S("f_z"), 2)
            dve.wait_ge(S("ld_iota12"), 16)
            for h in range(NH):
                ps = finished(dve, ("fg", h)).rearrange("p (c n) -> p c n", c=2)
                dve.tensor_tensor(lgt[:, tiles[h], :], ps[:, :, 0:12], over(row("eb"), 2), ALU.add)\
                   .then_inc(taken(("fg", h)), 1)
                written(dve, ("fg", h))
            for t in range(NT):
                link(dve.max(m8[:, t, :], lgt[:, t, :]))
                link(dve.max_index(i8[:, t, :], m8[:, t, :], lgt[:, t, :]))
            dve.tensor_tensor(sm[:, 0:4], m8[:, :, 1], m8[:, :, 0], ALU.subtract).then_inc(S("f_gap"), 1)
            link(dve.tensor_copy(i8f[:, :, 0:2], i8[:, :, 0:2]))
            dve.wait_ge(S("f_exp"), 1)
            link(dve.tensor_scalar(sm[:, 4:8], sm[:, 0:4], 1.0, None, ALU.add))
            link(dve.reciprocal(sm[:, 8:12], sm[:, 4:8]))
            link(dve.tensor_tensor(sm[:, 12:16], sm[:, 0:4], sm[:, 8:12], ALU.mult))
            for t in range(NT):
                dve.tensor_scalar(wgt[:, t, :], iota12[:], i8f[:, t, 0:1], sm[:, 8 + t:9 + t], ALU.is_equal, ALU.mult)
                link(dve.tensor_scalar(lgt[:, t, :], iota12[:], i8f[:, t, 1:2], sm[:, 12 + t:13 + t], ALU.is_equal,
                                       ALU.mult))
            link(dve.tensor_tensor(wgt[:], wgt[:], lgt[:], ALU.add))
            link(dve.tensor_reduce(sm[:, 16:20], wgt[:, :, 8:12], AX.X, ALU.add))
            for t in range(NT):
                ins = dve.scalar_tensor_tensor(out=X[:, t, :], in0=Z[:, t, :], scalar=sm[:, 16 + t:17 + t],
                                               in1=X[:, t, :], op0=ALU.mult, op1=ALU.add)
            link(ins)
            for e in range(NE):
                for h in range(NH):
                    name = ("f2", e, h)
                    ps = finished(dve, name).rearrange("p (c n) -> p c n", c=2)
                    for t in (2 * h, 2 * h + 1):
                        ins = dve.scalar_tensor_tensor(out=X[:, t, :], in0=ps[:, t % 2, :], scalar=wgt[:, t, e:e + 1],
                                                       in1=X[:, t, :], op0=ALU.mult, op1=ALU.add)
                    ins.then_inc(taken(name), 1)
                    written(dve, name)

    @block.gpsimd
    def _(pool):
        def block_diagonal(p, n_h, n_s, m0):
            for b in range(NB):
                if b >= 2:
                    finished(pool, (p + "S", b - 2, n_s - 1))
                if b % 4 == 0:
                    written(pool, (p + "q", b // 4))
                tok = slice(b * SQ, (b + 1) * SQ)
                for c in range(2):
                    ins = pool.tensor_tensor(QD[:, b % 2, c, 0:n_h, :], over(FV[:, c, tok], n_h),
                                             each(hmask[:, m0:m0 + n_h], SQ), ALU.mult)
                ins.then_inc(S(p + "_qd_ready"), 1)

        pool.wait_ge(S("ld_hmask"), 16)
        block_diagonal("a", 4, 2, 0)
        if upto >= 2:
            pool.wait_ge(S("ld_rows"), 16)
            for t in range(NT):
                written(pool, ("bg", t))
                g4 = b_g[:, t, :].rearrange("p (a n) -> p a n", a=4)
                pool.tensor_tensor(g4, g4, over(row("gn"), 4), ALU.mult).then_inc(S("b_gain"), 1)
        if upto >= 4:
            block_diagonal("d", 8, 4, 4)


def _bucket(rel, num_buckets=32, max_distance=128):
    nb = num_buckets // 2
    buckets = (rel > 0).astype(np.int32) * nb
    rel_abs = np.abs(rel)
    max_exact = nb // 2
    large = max_exact + (np.log(np.maximum(rel_abs, 1).astype(np.float32) / np.float32(max_exact))
                         / np.float32(np.log(max_distance / max_exact)) * (nb - max_exact)).astype(np.int32)
    return buckets + np.where(rel_abs < max_exact, rel_abs, np.minimum(large, nb - 1))


def kernel(**inputs):
    import concourse.bacc as _bacc
    from concourse.bass_utils import run_bass_kernel_spmd as _run

    I = {k: np.asarray(v) for k, v in inputs.items()}
    f32 = np.float32

    def kmajor(w):
        k, n = w.shape
        return np.ascontiguousarray(w.reshape(k // P, P, n).transpose(1, 0, 2))

    a = {}
    a["x"] = np.ascontiguousarray(I["x"].reshape(T, D))
    a["ctx"] = kmajor(I["ctx_1024"].reshape(NB * SK, D).T)
    a["mask"] = np.ascontiguousarray(I["mask_Bx1xSxS2_ff1"][:, 0].transpose(1, 0, 2))
    qkv, inp = I["L0_xattn_qkv_w"], I["L0_xattn_in_proj_w"]
    a["v_w"] = kmajor(qkv[512:].T)
    a["so_w"] = kmajor(I["L0_xattn_sa_out_w"].T)
    a["q_w"], a["k_w"], a["cv_w"] = (kmajor(inp[256 * i:256 * i + 256].T) for i in range(3))
    a["mo_w"] = kmajor(I["L0_xattn_mha_out_w"].T)
    a["lin1_w"] = kmajor(I["L0_xattn_lin1_w"].T)
    a["lin2_w"] = kmajor(I["L0_xattn_lin2_w"].T)
    swap = (np.arange(256) // 64) * 64 + (np.arange(256) % 64 + 32) % 64
    a["rq_w"], a["rk_w"] = kmajor(I["L0_attn_Wq"]), kmajor(I["L0_attn_Wk"])
    a["rqs_w"], a["rks_w"] = kmajor(I["L0_attn_Wq"][:, swap]), kmajor(I["L0_attn_Wk"][:, swap])
    a["rv_w"], a["rg_w"], a["ro_w"] = (kmajor(I["L0_attn_W" + n]) for n in "vgo")
    a["ffn_w1"], a["ffn_w2"] = kmajor(I["L0_ffn_W1"]), kmajor(I["L0_ffn_W2"])
    a["Wr"] = kmajor(I["L0_ffn_Wr"])
    for n in "qkv":
        a[f"x{n}_w"] = kmajor(I["L1_xattn_W" + n].transpose(1, 0, 2).reshape(D, D))
        a[f"e{n}_w"] = kmajor(I["L1_attn_W" + n].T)
    a["xo_w"] = kmajor(I["L1_xattn_Wo"])
    a["eo_w"] = kmajor(I["L1_attn_Wo"].T)
    a["gw"] = kmajor(I["L1_ffn_gate_w"].T)
    a["fw1"] = np.ascontiguousarray(I["L1_ffn_w1"].transpose(0, 2, 1).reshape(NE, 2, P, DFF).transpose(0, 2, 1, 3))
    a["fw2"] = np.ascontiguousarray(I["L1_ffn_w2"].transpose(0, 2, 1).reshape(NE, 4, P, D).transpose(0, 2, 1, 3))
    colv = {"v_b": I["L0_xattn_qkv_b"][512:], "q_b": I["L0_xattn_in_proj_b"][:256],
            "k_b": I["L0_xattn_in_proj_b"][256:512], "cv_b": I["L0_xattn_in_proj_b"][512:],
            "lin1_b": I["L0_xattn_lin1_b"], "ffn_b1": I["L0_ffn_b1"], "ffn_b2": I["L0_ffn_b2"],
            "xq_b": I["L1_xattn_bq"].reshape(-1), "xk_b": I["L1_xattn_bk"].reshape(-1),
            "xv_b": I["L1_xattn_bv"].reshape(-1)}
    a["cols"] = np.ascontiguousarray(np.concatenate([colv[n].reshape(-1, P).T for n in COLS], axis=1))
    rowv = {"so_b": I["L0_xattn_sa_out_b"], "ln1_g": I["L0_xattn_ln1_g"], "ln1_b": I["L0_xattn_ln1_b"],
            "mo_b": I["L0_xattn_mha_out_b"], "ln2_g": I["L0_xattn_ln2_g"], "ln2_b": I["L0_xattn_ln2_b"],
            "lin2_b": I["L0_xattn_lin2_b"], "ln3_g": I["L0_xattn_ln3_g"], "ln3_b": I["L0_xattn_ln3_b"],
            "gn": I["L0_attn_gn_weight"], "f_g": I["L0_ffn_ln_gamma"], "f_b": I["L0_ffn_ln_beta"],
            "ffn_b2": I["L0_ffn_b2"], "xo_b": I["L1_xattn_bo"], "br": I["L0_ffn_br"],
            "eb": I["L1_ffn_expert_bias"]}
    a["rows"] = np.ascontiguousarray(np.concatenate([rowv[n] for n in ROWS])[None, :])
    p = np.arange(P)
    a["ident"] = np.eye(P, dtype=f32)
    a["hmask"] = np.concatenate([p[:, None] // 32 == np.arange(4), p[:, None] // 16 == np.arange(8)], 1).astype(f32)
    inv_freq = f32(1.0) / np.power(f32(10000.0), np.arange(0, 64, 2, dtype=f32) / f32(64))
    ang = (np.arange(SQ, dtype=f32)[None, :] * inv_freq[p % 32][:, None]).astype(f32)
    sign = np.where(p % 64 < 32, -1.0, 1.0).astype(f32)[:, None]
    a["rot"] = np.ascontiguousarray(np.stack([np.cos(ang), np.sin(ang) * sign], 1).astype(f32))
    gamma = 1.0 - np.exp2(-5.0 - np.arange(4))
    j, i = (p % 64)[:, None, None], np.arange(SQ)[None, None, :]
    a["decay"] = np.where(i >= j, gamma[None, :, None] ** np.maximum(i - j, 0) / 8.0, 0.0).astype(f32)
    a["iota12"] = np.tile(np.arange(12, dtype=f32), (P, 1))
    ranks = []
    for size in (LIN * D, LIN * D, LIN, D):
        k = max(1, int(size * 0.1 / 2))
        ranks.append((size - k + 1, k))
    want = [ranks[0][0], ranks[1][0], ranks[0][1], ranks[1][1], ranks[2][0], ranks[3][0], ranks[2][1], ranks[3][1]]
    a["kwant"] = np.tile(np.array(want, f32), (P, 1))
    rel = np.arange(SQ)[:, None] - np.arange(SQ)[None, :]
    e = I["L1_attn_rel_emb"][_bucket(rel)]
    a["rbias"] = np.ascontiguousarray(e.reshape(SQ, SQ, 8, 2).transpose(3, 0, 2, 1).reshape(P, 8, SQ))
    a["causal"] = np.where(rel[p % 64] < 0, CAUSAL_NEG, 0.0).astype(f32)

    nc = _bacc.Bacc("TRN2", target_bir_lowering=False, num_devices=1)
    A = {n: nc.dram_tensor(f"in_{n}", v.shape, mybir.dt.from_np(v.dtype), kind="ExternalInput").ap()
         for n, v in a.items()}
    out = nc.dram_tensor("out_x", (T, D), F32, kind="ExternalOutput").ap()
    build(nc, A, out, UPTO)
    r = _run(nc, [{f"in_{n}": v for n, v in a.items()}], core_ids=[0])
    return r.results[0]["out_x"].reshape(NB, SQ, D)


UPTO = 6
```

```python
from contextlib import ExitStack

import numpy as np

import concourse.bass as bass
from concourse import mybir

F32 = mybir.dt.float32
F32R = mybir.dt.float32r
BF16 = mybir.dt.bfloat16
U16 = mybir.dt.uint16
I32 = mybir.dt.int32
U32 = mybir.dt.uint32
ALU = mybir.AluOpType
ACT = mybir.ActivationFunctionType
AX = mybir.AxisListType

P = 128
NB, SQ, SK, D = 8, 64, 256, 256
T = NB * SQ
NT = T // P
NH = 2
HT = T // NH
EPS = 1e-5
NE = 8
NSTEP1, NSTEP2 = 15, 16
N_SEARCH = NSTEP1 + NSTEP2
LIN, DFF = 1024, 512
NEG = -1.0e9
CAUSAL_NEG = -1.0e30

COLS = ["v_b", "q_b", "k_b", "cv_b", "lin1_b", "ffn_b1", "ffn_b2", "xq_b", "xk_b", "xv_b"]
COL_N = {"v_b": 2, "q_b": 2, "k_b": 2, "cv_b": 2, "lin1_b": 8, "ffn_b1": 8, "ffn_b2": 2, "xq_b": 2,
         "xk_b": 2, "xv_b": 2}
COL_AT = {n: sum(COL_N[m] for m in COLS[:i]) for i, n in enumerate(COLS)}
NCOL = sum(COL_N.values())
ROWS = ["so_b", "ln1_g", "ln1_b", "mo_b", "ln2_g", "ln2_b", "lin2_b", "ln3_g", "ln3_b", "gn", "f_g",
        "f_b", "ffn_b2", "xo_b", "br", "eb"]
ROW_N = {n: D for n in ROWS} | {"gn": 128, "br": 8, "eb": 12}
ROW_AT = {n: sum(ROW_N[m] for m in ROWS[:i]) for i, n in enumerate(ROWS)}
NROW = sum(ROW_N.values())


def long_batch(i):
    return i >= 4


def job_order():
    H = range(NH)
    out = []
    parts = [0]

    def search(n=1):
        for _ in range(n):
            s, summing = divmod(parts[0], 2)
            parts[0] += 1
            out.append(("tot" if summing else "cnt", s))

    def attention(p, n_s, steps):
        if p == "d":
            out.extend([("dK", 0), ("dV", 0)])
        for i in range(NB + 1):
            for s in range(n_s):
                if i < NB:
                    out.append((p + "S", i, s))
                if i > 0:
                    out.append((p + "PT", i - 1, s))
                if i < NB and s < 2:
                    search(steps)
            if i + 1 < NB:
                out.extend([(p + "K", i + 1), (p + "V", i + 1)])
            if i < NB and long_batch(i):
                search(steps)
            if i > 0:
                out.append((p + "O", i - 1))
            if i < NB and long_batch(i):
                search(steps)

    for n in ("aT0", "av", "aso", "aT1", "aq"):
        out.extend([(n, h) for h in H])
        if n == "aso":
            out.extend([("aK", 0), ("aV", 0)])
        if n in ("aT1", "aq"):
            search()
    attention("a", 2, 1)
    search()
    for n in ("amo", "aT2"):
        out.extend([(n, h) for h in H])
        search()
    for h in H:
        out.extend([("af1", 0, h, f) for f in range(4)])
        if h == 0:
            search()
    for h in H:
        out.extend([("af2", 0, h)])
        search()
    out.extend([("bT", h) for h in H])
    search()
    for h in H:
        for a in ("bq", "bqs", "bk", "bks"):
            out.append((a, h))
            search()
    for t in range(NT):
        out.extend([("bv", t), ("bg", t)])
        search()
    for t in range(NT + 1):
        if t < NT:
            out.extend([("bS", t, 0), ("bS", t, 1)])
        if t > 0:
            out.extend([("bO", t - 1, 0), ("bO", t - 1, 1)])
        if t < NT:
            search()
    out.extend([("bOT", t) for t in range(NT)])
    search()
    out.extend([("bwo", h) for h in H])
    search()
    out.extend([("cT", h) for h in H])
    search()
    for h in H:
        for f in range(4):
            out.append(("c1", 0, h, f))
            search()
        if h == 0:
            for n in ("cT2", "cr"):
                out.extend([(n, g) for g in H])
                search()
    out.extend([("c2", 0, h) for h in H])
    out.extend([("c1", 1, h, f) for h in H for f in range(4)])
    out.extend([("c2", 1, h) for h in H])
    out.extend([("dT", h) for h in H])
    out.extend([("dq", h) for h in H])
    attention("d", 4, 0)
    out.extend([("dmo", h) for h in H])
    def project(h):
        out.extend([("eT", h)] + [(n, h, c) for n in ("eq", "ek") for c in range(4)])

    def scores(h):
        out.extend([("eS", t, bp, hp) for t in (2 * h, 2 * h + 1) for bp in range(2) for hp in range(2)])

    def values(h):
        out.extend([("ev", t, n) for t in (2 * h, 2 * h + 1) for n in range(2)])

    def outputs(h):
        for t in (2 * h, 2 * h + 1):
            out.extend([("ePT", t, 0), ("ePT", t, 1), ("eO", t, 0), ("eO", t, 1)])

    project(0)
    scores(0)
    values(0)
    project(1)
    outputs(0)
    scores(1)
    out.append(("ewo", 0))
    values(1)
    outputs(1)
    out.append(("ewo", 1))
    out.extend([("fT", h) for h in H])
    out.extend([("fg", h) for h in H])
    for e in range(NE + 1):
        if e < NE:
            out.extend([("f1", e, f) for f in range(4)])
        if e > 0:
            out.extend([("f2", e - 1, h) for h in H])
    assert parts[0] == 2 * N_SEARCH
    return out


def build(nc, A, out):
    with ExitStack() as ctx:
        _build(nc, A, out, ctx)


def _build(nc, A, out, ctx):
    def sb(name, shape, dt=F32):
        return ctx.enter_context(nc.sbuf_tensor(name, shape, dt))

    sems = {}

    def S(name):
        if name not in sems:
            sems[name] = ctx.enter_context(nc.semaphore(name))
        return sems[name]

    JOBS = {name: (i % 8, i // 8) for i, name in enumerate(job_order())}
    psum = ctx.enter_context(nc.psum_tensor("psum", [P, 8, 512], F32))
    full = [S(f"bank{b}_full") for b in range(8)]
    free = [S(f"bank{b}_free") for b in range(8)]

    def region(stack, suffix, dt):
        def one(name, *shape):
            return stack.enter_context(nc.sbuf_tensor(name + suffix, [P, *shape], dt))
        return (one("FV", 2, T),
                one("FK", 2, T),
                one("BIG", 8192),
                one("RB", 5120),
                one("RC", 8192),
                one("CTX", 2, NB * SK))
    with ExitStack() as earlier:
        FV, FK, BIG, RB, RC, CTX = region(earlier, "", F32)
    FVr, FKr, BIGr, RBr, RCr, CTXr = region(ctx, "_r", F32R)
    X = sb("X", [P, NT, D])
    Z = sb("Z", [P, NT, D])
    Y = sb("Y", [P, NT, D])
    FT = sb("FT", [P, 2, T])
    RA = sb("RA", [P, 7168])
    KT = sb("KT", [P, 2, 2, SK])
    VB = sb("VB", [P, 2, 2, D])
    QD = sb("QD", [P, 2, 2, 8, SQ])
    PR = sb("PR", [P, 4, 512])
    PT = sb("PT", [P, 4, 512])
    rows = sb("rows", [P, NROW])
    cols = sb("cols", [P, NCOL])
    ident = sb("ident", [P, P])
    hmask = sb("hmask", [P, 16])
    rot = sb("rot", [P, 2, SQ])
    decay = sb("decay", [P, 4, SQ])
    iota12 = sb("iota12", [P, 12])
    Wr = sb("Wr", [P, 2, 8])
    gw = sb("gw", [P, 2, 12])
    kwant = sb("kwant", [P, 8])
    onesb = sb("onesb", [P, 1], BF16)
    onesf = sb("onesf", [P, P])
    st = sb("st", [P, NT, 6])
    mv = sb("mv", [P, NT, 2])
    lnv = sb("lnv", [P, NT])
    rstd = sb("rstd", [P, NT])
    nmx = sb("nmx", [P, 2, 8])
    sums = sb("sums", [P, 2, 8])
    rmx = sb("rmx", [P, 2, 8])
    rinv = sb("rinv", [P, 2, 8])
    ms = sb("ms", [P, NT, 4])
    eps = sb("eps", [P, 1])
    sm = sb("sm", [P, 256])
    cnt = sb("cnt", [P, 8])
    cur = sb("cur", [P, 8])
    cand = sb("cand", [P, 8])
    kleft = sb("kleft", [P, 8])
    base = sb("base", [P, 8])
    totals = sb("totals", [P, 8])
    fewer = sb("fewer", [P, 8])
    thr = sb("thr", [P, 2, 8])
    bkey = sb("bkey", [P, 4, 8], U16)
    below = sb("below", [P, 4, 8])
    nbias = sb("nbias", [P, 1])
    signs = sb("signs", [P, 1])
    bound = sb("bound", [P, 8])
    lgt = sb("lgt", [P, 4, 12])
    m8 = sb("m8", [P, 4, 8])
    i8 = sb("i8", [P, 4, 8], U32)
    i8f = sb("i8f", [P, 4, 8])
    wgt = sb("wgt", [P, 4, 12])
    rany = sb("rany", [P, NB])
    bp_row = sb("bp_row", [P, D])
    bp_col = sb("bp_col", [P, 8])

    def part(region, at, *shape):
        n = int(np.prod(shape))
        v = region[:, at:at + n]
        if len(shape) == 2:
            v = v.rearrange("p (a b) -> p a b", a=shape[0])
        if len(shape) == 3:
            v = v.rearrange("p (a b c) -> p a b c", a=shape[0], b=shape[1])
        return v

    a_wv, a_so, a_wq, a_wk, a_wcv, a_mo = (part(RA, 512 * i, 2, 256) for i in range(6))
    a_l1 = part(RA, 3072, 2, 1024)
    a_l2 = part(RA, 5120, 8, 256)
    b_wq, b_wqs, b_wk, b_wks = (part(RB, 512 * i, 2, 256) for i in range(4))
    b_wv, b_wg = part(RB, 2048, 2, 512), part(RB, 3072, 2, 512)
    b_wo = part(RB, 4096, 4, 256)
    c_w1 = [part(RC, 0, 2, 1024), part(RC, 4096, 2, 1024)]
    c_w2 = [part(RC, 2048, 8, 256), part(RC, 6144, 8, 256)]
    d_wq, d_wk, d_wv, d_wo = (part(RA, 512 * i, 2, 256) for i in range(4))
    d_mask = part(RB, 0, NB, SK)
    e_raw = [RC[:, 2048 * i:2048 * i + 2048] for i in range(4)]
    ctx_r = CTXr[:].rearrange("p k n -> p (k n)")
    e_high = [BIGr[:, 6144:8192], RBr[:, 2624:4672], ctx_r[:, 0:2048], RBr[:, 0:2048]]
    e_low = [RCr[:, 2048 * i:2048 * i + 2048] for i in range(4)]
    e_wq, e_wk, e_wv = ([w.rearrange("p (k n) -> p k n", k=2) for w in (e_high[i], e_low[i])] for i in range(3))
    e_wo = [w.rearrange("p (k n) -> p k n", k=8) for w in (e_high[3], e_low[3])]
    x_split = [FVr[:], FKr[:]]
    e_out = [part(BIGr, 0, 8, HT), part(BIGr, 2048, 8, HT)]
    e_bias = part(RB, 2048, 8, SQ)
    e_causal = part(RB, 2560, SQ)
    f_raw = [RA[:, 2048 + 2048 * i:4096 + 2048 * i] for i in range(2)]
    f_slot = [ctx_r, RCr[:, 0:4096], RBr[:, 0:4096]]
    f_split = [[r[:, 2048 * i:2048 * i + 2048] for i in range(2)] for r in f_slot]
    f_w1 = [[w[:, 0:1024].rearrange("p (k n) -> p k n", k=2) for w in r] for r in f_split]
    f_w2 = [[w[:, 1024:2048].rearrange("p (k n) -> p k n", k=4) for w in r] for r in f_split]
    f_act = [part(RC, 4096 + 2048 * i, 4, T) for i in range(2)]
    a_hid = part(BIG, 0, 8, T)
    b_v, b_g = part(BIG, 0, NT, 512), part(BIG, 2048, NT, 512)
    b_sq = QD[:].rearrange("p a c h n -> p (a c h n)").rearrange("p (t n) -> p t n", t=NT)
    b_o, b_ot = part(RA, 2048, NT, 512), part(RA, 4608, 4, T)
    c_hid = [part(BIG, 0, 8, T), part(BIG, 4096, 8, T)]
    e_q = [part(BIG, 0, 8, HT), part(CTX[:].rearrange("p k n -> p (k n)"), 2048, 8, HT)]
    e_k = [part(BIG, 2048, 8, HT), part(RA, 0, 8, HT)]
    e_v = part(BIG, 4096, 2, 1024)
    f_hid = [[part(BIGr, 4096 * i + 2048 * j, 4, T) for j in range(2)] for i in range(2)]
    inv_diag = {"a": FK[:].rearrange("p k n -> p (k n)").rearrange("p (a j n) -> p a j n", a=2, j=4),
                "d": BIG[:, 0:2048].rearrange("p (a j n) -> p a j n", a=2, j=8)}
    KEY = BIG[:, 4096:8192].bitcast(U16).rearrange("p (q n) -> p q n", q=4)
    low_half = KEY[:, 2:4, :]
    smask = RC[:, 4096:8192].bitcast(BF16).rearrange("p (q n) -> p q n", q=4)

    def row(name, n=None):
        return rows[:, ROW_AT[name]:ROW_AT[name] + (n or ROW_N[name])]

    def col(name, i):
        return cols[:, COL_AT[name] + i:COL_AT[name] + i + 1]

    def bank(name):
        return psum[:, JOBS[name][0], :]

    def over(ap, n):
        return ap.unsqueeze(1).to_broadcast([ap.shape[0], n, ap.shape[1]])

    def each(ap, n):
        return ap.unsqueeze(2).to_broadcast([ap.shape[0], ap.shape[1], n])

    block = ctx.enter_context(nc.Block())

    def claim(pe, name):
        b, u = JOBS[name]
        if u:
            pe.wait_ge(free[b], u)
        return psum[:, b, :]

    def filled(name):
        return full[JOBS[name][0]]

    def taken(name):
        return free[JOBS[name][0]]

    def finished(eng, name):
        b, u = JOBS[name]
        eng.wait_ge(full[b], u + 1)
        return psum[:, b, :]

    def written(eng, name):
        b, u = JOBS[name]
        eng.wait_ge(free[b], u + 1)

    half = [slice(h * HT, (h + 1) * HT) for h in range(NH)]
    tiles = [slice(2 * h, 2 * h + 2) for h in range(NH)]

    @block.sync
    def _(sp):
        def load(dst, name, src=None):
            sp.dma_start(dst, A[name] if src is None else src).then_inc(S("ld_" + name), 16)

        for t in range(NT):
            sp.dma_start(X[:, t, :], A["x"][t * P:(t + 1) * P, :]).then_inc(S(f"ld_x{t // 2}"), 16)
        load(ident[:], "ident")
        load(cols[:], "cols")
        load(a_wv, "v_w")
        load(rows[:], "rows", A["rows"].to_broadcast([P, NROW]))
        load(a_so, "so_w")
        load(a_wk, "k_w")
        load(a_wcv, "cv_w")
        load(CTX[:, :, 0:SK], "ctx0", A["ctx"][:, :, 0:SK])
        load(c_w1[0], "ffn_w1")
        load(c_w2[0], "ffn_w2")
        load(kwant[:], "kwant")
        load(a_wq, "q_w")
        load(CTX[:, :, SK:], "ctx", A["ctx"][:, :, SK:])
        load(hmask[:], "hmask")
        load(a_mo, "mo_w")
        load(a_l1, "lin1_w")
        load(a_l2, "lin2_w")
        load(b_wq, "rq_w")
        load(b_wqs, "rqs_w")
        load(b_wk, "rk_w")
        load(b_wks, "rks_w")
        load(b_wv, "rv_w")
        load(b_wg, "rg_w")
        load(b_wo, "ro_w")
        load(rot[:], "rot")
        load(decay[:], "decay")
        load(Wr[:], "Wr")
        load(gw[:], "gw")
        load(iota12[:], "iota12")
        finished(sp, ("af2", 0, 1))
        load(d_wq, "xq_w")
        load(d_wk, "xk_w")
        load(d_wv, "xv_w")
        load(d_wo, "xo_w")
        finished(sp, ("bwo", 1))
        for hp in range(2):
            sp.dma_start(d_mask[hp * 64:hp * 64 + 64], A["mask"]).then_inc(S("ld_mask"), 16)
        load(e_bias, "rbias")
        load(e_causal, "causal")
        finished(sp, ("c2", 1, 1))
        for i, name in enumerate(("eq_w", "ek_w", "ev_w", "eo_w")):
            load(e_raw[i], name, A[name].rearrange("p k n -> p (k n)"))
        for e in range(NE):
            if e >= 2:
                sp.wait_ge(S("f_w_low"), e - 1)
            sp.dma_start(f_raw[e % 2], A["fw"][e]).then_inc(S(f"ld_f{e % 2}"), 16)
        for h in range(NH):
            written(sp, ("f2", NE - 1, h))
            for t in (2 * h, 2 * h + 1):
                sp.dma_start(out[t * P:(t + 1) * P, :], X[:, t, :]).then_inc(S("stored"), 16)
        sp.wait_ge(S("stored"), 16 * NT)

    @block.tensor
    def _(pe):
        parts = [0]

        def loaded(*names):
            for n in names:
                pe.wait_ge(S("ld_" + n), 16)

        def to_fm(name, h, src, nk=2):
            ps = claim(pe, (name, h)).rearrange("p (c n) -> p c n", c=2)
            for t in (2 * h, 2 * h + 1):
                for c in range(2):
                    ins = pe.transpose(ps[:, c, (t % 2) * P:(t % 2 + 1) * P], src[:, t, c * P:(c + 1) * P],
                                       ident[:])
            ins.then_inc(filled((name, h)), 1)

        def fm(name, w, c0, src, tok):
            ps = claim(pe, name).rearrange("p (c n) -> p c n", c=2)
            for c in range(2):
                for k in range(2):
                    ins = pe.matmul(ps[:, c, :], w[:, k, (c0 + c) * P:(c0 + c + 1) * P], src[:, k, tok],
                                    start=(k == 0), stop=(k == 1))
            ins.then_inc(filled(name), 1)

        def tm(name, src, h, w, nk, n=256, t0=None):
            ps = claim(pe, name).rearrange("p (c n) -> p c n", c=2)
            for j in range(2):
                at = ((2 * h + j) if t0 is None else j) * P
                for k in range(nk):
                    ins = pe.matmul(ps[:, j, :n], src[:, k, at:at + P], w[:, k, :n],
                                    start=(k == 0), stop=(k == nk - 1))
            ins.then_inc(filled(name), 1)

        PASSES = ((0, 0), (0, 1), (1, 0))

        def split_matmul(dst, lhs, rhs, first=True, last=True):
            for n, (a, b) in enumerate(PASSES):
                ins = pe.matmul(dst, lhs(a), rhs(b), start=(first and n == 0), stop=(last and n == 2))
            return ins

        def search():
            s, summing = divmod(parts[0], 2)
            parts[0] += 1
            if not summing:
                ps = claim(pe, ("cnt", s))
                for q in range(1, 4):
                    pe.wait_ge(S("smask_ready"), 3 * s + q)
                    for i in range(16):
                        ins = pe.matmul(ps[:, q:q + 1], smask[:, q, i * P:(i + 1) * P], onesb[:],
                                        start=(i == 0), stop=(i == 15))
                ins.then_inc(filled(("cnt", s)), 1)
            else:
                ps = claim(pe, ("tot", s))
                written(pe, ("cnt", s))
                pe.matmul(ps[:, 0:8], onesf[:], cnt[:], start=True, stop=True).then_inc(filled(("tot", s)), 1)

        def keys_values(p, wk, wv, i):
            fm((p + "K", i), wk, 0, CTX, slice(i * SK, (i + 1) * SK))
            ps = claim(pe, (p + "V", i)).rearrange("p (c n) -> p c n", c=2)
            for kt in range(2):
                for k in range(2):
                    at = i * SK + kt * P
                    ins = pe.matmul(ps[:, kt, :], CTX[:, k, at:at + P], wv[:, k, :],
                                    start=(k == 0), stop=(k == 1))
            ins.then_inc(filled((p + "V", i)), 1)

        def attention(p, wk, wv, n_s, steps):
            w = D // (4 * n_s) * 2
            per = 2 if n_s == 2 else 4

            def pv(b):
                ps = claim(pe, (p + "O", b))
                in_chunk = P // w
                for c in range(2):
                    for kc in range(2):
                        for jj in range(in_chunk):
                            j = in_chunk * c + jj
                            s, pr = j // 2, j % 2
                            ins = pe.matmul(ps[jj * w:(jj + 1) * w, c * P:(c + 1) * P],
                                            VB[:, b % 2, kc, j * w:(j + 1) * w],
                                            PT[:, (n_s * b + s) % 4, pr * 256 + kc * P:pr * 256 + (kc + 1) * P],
                                            start=(kc == 0), stop=(kc == 1))
                ins.then_inc(filled((p + "O", b)), 1)

            def p_transpose(b, s):
                ps = claim(pe, (p + "PT", b, s))
                pe.wait_ge(S(p + "_diag"), n_s * b + s + 1)
                for pr in range(2):
                    for kc in range(2):
                        at = pr * 256 + kc * P
                        ins = pe.matmul(ps[:, at:at + P], PR[:, (n_s * b + s) % 4, at:at + P],
                                        inv_diag[p][:, b % 2, 2 * s + pr, :], start=True, stop=True)
                ins.then_inc(filled((p + "PT", b, s)), 1)

            if p == "d":
                keys_values(p, wk, wv, 0)
            for i in range(NB + 1):
                if i < NB:
                    pe.wait_ge(S(p + "_qd_ready"), i + 1)
                    written(pe, (p + "K", i))
                for s in range(n_s):
                    if i < NB:
                        ps = claim(pe, (p + "S", i, s))
                        for pr in range(2):
                            j = 2 * s + pr
                            c, jj = j // per, j % per
                            ins = pe.matmul(ps[:, pr * 256:(pr + 1) * 256], QD[:, i % 2, c, 2 * jj:2 * jj + 2, :],
                                            KT[:, i % 2, c, :], start=True, stop=True)
                        ins.then_inc(filled((p + "S", i, s)), 1)
                    if i > 0:
                        p_transpose(i - 1, s)
                    if steps and i < NB and s < 2:
                        search()
                if i + 1 < NB:
                    keys_values(p, wk, wv, i + 1)
                if steps and i < NB and long_batch(i):
                    search()
                if i > 0:
                    for s in range(n_s):
                        written(pe, (p + "PT", i - 1, s))
                    written(pe, (p + "V", i - 1))
                    pv(i - 1)
                if steps and i < NB and long_batch(i):
                    search()

        def ffn_in(name, w1, h):
            fm(name, w1, 2 * name[-1], FT, half[h])

        def ffn_out(one, two, e, h, n_f, hid, w2):
            for f in range(n_f):
                written(pe, (one, e, h, f))
            tm((two, e, h), hid, h, w2, 2 * n_f)

        loaded("ident", "v_w")
        pe.wait_ge(S("ones_ready"), 2)
        for h in range(NH):
            pe.wait_ge(S("a_z0"), h + 1)
            to_fm("aT0", h, Z)
        for h in range(NH):
            written(pe, ("aT0", h))
            fm(("av", h), a_wv, 0, FT, half[h])
        loaded("so_w")
        for h in range(NH):
            written(pe, ("av", h))
            tm(("aso", h), FV, h, a_so, 2)
        loaded("k_w", "cv_w", "ctx0")
        keys_values("a", a_wk, a_wcv, 0)
        for h in range(NH):
            pe.wait_ge(S("a_z1"), h + 1)
            to_fm("aT1", h, Z)
        search()
        loaded("q_w")
        for h in range(NH):
            written(pe, ("aT1", h))
            fm(("aq", h), a_wq, 0, FT, half[h])
        search()
        loaded("ctx")
        attention("a", a_wk, a_wcv, 2, 1)
        search()
        loaded("mo_w")
        for h in range(NH):
            written(pe, ("aO", 4 * h + 3))
            tm(("amo", h), FT, h, a_mo, 2)
        search()
        for h in range(NH):
            pe.wait_ge(S("a_z2"), h + 1)
            to_fm("aT2", h, Z)
        search()
        loaded("lin1_w", "lin2_w")
        for h in range(NH):
            written(pe, ("aT2", h))
            for f in range(4):
                ffn_in(("af1", 0, h, f), a_l1, h)
            if h == 0:
                search()
        for h in range(NH):
            ffn_out("af1", "af2", 0, h, 4, a_hid, a_l2)
            search()

        for h in range(NH):
            pe.wait_ge(S("b_z"), h + 1)
            to_fm("bT", h, Z)
        search()
        loaded("rq_w", "rqs_w", "rk_w", "rks_w")
        for h in range(NH):
            written(pe, ("bT", h))
            for n, w in (("bq", b_wq), ("bqs", b_wqs), ("bk", b_wk), ("bks", b_wks)):
                fm((n, h), w, 0, FT, half[h])
                search()
        loaded("rv_w", "rg_w")
        for t in range(NT):
            for n, w in (("bv", b_wv), ("bg", b_wg)):
                ps = claim(pe, (n, t))
                for k in range(2):
                    ins = pe.matmul(ps, FT[:, k, t * P:(t + 1) * P], w[:, k, :], start=(k == 0), stop=(k == 1))
                ins.then_inc(filled((n, t)), 1)
            search()
        for t in range(NT + 1):
            if t < NT:
                if t % 2 == 0:
                    pe.wait_ge(S("b_qk"), 2 * (t // 2 + 1))
                for hp in range(2):
                    claim(pe, ("bS", t, hp))
                for bp, c in ((0, 0), (0, 1), (1, 0), (1, 1)):
                    tok = slice(t * P + bp * 64, t * P + bp * 64 + 64)
                    for hp in range(2):
                        ps = bank(("bS", t, hp)).rearrange("p (c n) -> p c n", n=SQ)
                        ins = pe.matmul(ps[bp * 64:bp * 64 + 64, c, :], FK[hp * 64:hp * 64 + 64, c, tok],
                                        FV[hp * 64:hp * 64 + 64, c, tok], start=True, stop=True)
                        if (bp, c) == (1, 1):
                            ins.then_inc(filled(("bS", t, hp)), 1)
            if t > 0:
                for hp in range(2):
                    written(pe, ("bS", t - 1, hp))
                written(pe, ("bv", t - 1))
                for bp in range(2):
                    claim(pe, ("bO", t - 1, bp))
                for hd in range(4):
                    for bp in range(2):
                        at = slice(bp * 64, bp * 64 + 64)
                        ps = bank(("bO", t - 1, bp))
                        ins = pe.matmul(ps[at, hd * P:(hd + 1) * P], PR[at, t - 1, hd * SQ:(hd + 1) * SQ],
                                        b_v[at, t - 1, hd * P:(hd + 1) * P], start=True, stop=True)
                        if hd == 3:
                            ins.then_inc(filled(("bO", t - 1, bp)), 1)
            if t < NT:
                search()
        for t in range(NT):
            ps = claim(pe, ("bOT", t))
            pe.wait_ge(S("b_gated"), t + 1)
            for c in range(4):
                ins = pe.transpose(ps[:, c * P:(c + 1) * P], b_o[:, t, c * P:(c + 1) * P], ident[:])
            ins.then_inc(filled(("bOT", t)), 1)
        search()
        loaded("ro_w")
        for h in range(NH):
            for t in (2 * h, 2 * h + 1):
                written(pe, ("bOT", t))
            tm(("bwo", h), b_ot, h, b_wo, 4)
        search()

        for h in range(NH):
            pe.wait_ge(S("c_z"), h + 1)
            to_fm("cT", h, Z)
        search()
        loaded("Wr", "ffn_w1", "ffn_w2")
        for h in range(NH):
            written(pe, ("cT", h))
            for f in range(4):
                ffn_in(("c1", 0, h, f), c_w1[0], h)
                search()
            if h == 0:
                for g in range(NH):
                    pe.wait_ge(S("c_y"), g + 1)
                    to_fm("cT2", g, Y)
                search()
                for g in range(NH):
                    written(pe, ("cT2", g))
                    tm(("cr", g), FV, g, Wr, 2, 8)
                search()
        for h in range(NH):
            ffn_out("c1", "c2", 0, h, 4, c_hid[0], c_w2[0])
        pe.wait_ge(S("perturbed"), 1)
        for h in range(NH):
            for f in range(4):
                ffn_in(("c1", 1, h, f), c_w1[1], h)
        pe.wait_ge(S("perturbed"), 4)
        for h in range(NH):
            ffn_out("c1", "c2", 1, h, 4, c_hid[1], c_w2[1])

        for h in range(NH):
            pe.wait_ge(S("d_z"), h + 1)
            to_fm("dT", h, Z)
        loaded("xq_w", "xk_w", "xv_w")
        for h in range(NH):
            written(pe, ("dT", h))
            fm(("dq", h), d_wq, 0, FT, half[h])
        attention("d", d_wk, d_wv, 4, 0)
        loaded("xo_w")
        for h in range(NH):
            written(pe, ("dO", 4 * h + 3))
            tm(("dmo", h), FT, h, d_wo, 2)

        def project(h):
            pe.wait_ge(S("e_z"), h + 1)
            to_fm("eT", h, Z)
            written(pe, ("eT", h))
            for i, (n, w) in enumerate((("eq", e_wq), ("ek", e_wk))):
                pe.wait_ge(S("e_w_low"), i + 1)
                for f in range(4):
                    ps = claim(pe, (n, h, f)).rearrange("p (c n) -> p c n", c=2)
                    for c in range(2):
                        out_at = slice((2 * f + c) * P, (2 * f + c + 1) * P)
                        for k in range(2):
                            ins = split_matmul(ps[:, c, :], lambda a: w[a][:, k, out_at],
                                               lambda b: x_split[b][:, k, half[h]], k == 0, k == 1)
                    ins.then_inc(filled((n, h, f)), 1)

        def scores(h):
            for c in range(4):
                written(pe, ("eq", h, c))
                written(pe, ("ek", h, c))
            for t in (2 * h, 2 * h + 1):
                for bp in range(2):
                    tok = slice((t % 2) * P + bp * 64, (t % 2) * P + bp * 64 + 64)
                    for hp in range(2):
                        claim(pe, ("eS", t, bp, hp))
                    for pr in range(8):
                        for hp in range(2):
                            at = slice(hp * 64, hp * 64 + 64)
                            ps = bank(("eS", t, bp, hp)).rearrange("p (c n) -> p c n", n=SQ)
                            ins = pe.matmul(ps[at, pr, :], e_q[h][at, pr, tok], e_k[h][at, pr, tok],
                                            start=True, stop=True)
                            if pr == 7:
                                ins.then_inc(filled(("eS", t, bp, hp)), 1)

        def values(h):
            pe.wait_ge(S("e_w_low"), 3)
            for t in (2 * h, 2 * h + 1):
                for n in range(2):
                    ps = claim(pe, ("ev", t, n))
                    for k in range(2):
                        ins = split_matmul(ps, lambda a: x_split[a][:, k, t * P:(t + 1) * P],
                                           lambda b: e_wv[b][:, k, n * 512:(n + 1) * 512], k == 0, k == 1)
                    ins.then_inc(filled(("ev", t, n)), 1)

        def outputs(h):
            for t in (2 * h, 2 * h + 1):
                pe.wait_ge(S("e_p"), t + 1)
                for s in range(2):
                    ps = claim(pe, ("ePT", t, s))
                    for i in range(4):
                        pr = 4 * s + i
                        src = PR[:, 2 * (t % 2):2 * (t % 2) + 2, :].rearrange("p a n -> p (a n)")
                        ins = pe.transpose(ps[:, i * P:(i + 1) * P], src[:, pr * P:(pr + 1) * P], ident[:])
                    ins.then_inc(filled(("ePT", t, s)), 1)
                for n in range(2):
                    written(pe, ("ev", t, n))
                    written(pe, ("ePT", t, n))
                for bp in range(2):
                    claim(pe, ("eO", t, bp))
                for hd in range(16):
                    pr, hp = hd // 2, hd % 2
                    for bp in range(2):
                        at = slice(bp * 64, bp * 64 + 64)
                        probs = PT[at, 2 * (t % 2) + pr // 4, (pr % 4) * P + hp * 64:(pr % 4) * P + hp * 64 + 64]
                        ins = pe.matmul(bank(("eO", t, bp))[hp * 64:hp * 64 + 64, pr * SQ:(pr + 1) * SQ],
                                        e_v[at, t % 2, hd * SQ:(hd + 1) * SQ], probs, start=True, stop=True)
                        if hd == 15:
                            ins.then_inc(filled(("eO", t, bp)), 1)

        def out_project(h):
            for t in (2 * h, 2 * h + 1):
                for bp in range(2):
                    written(pe, ("eO", t, bp))
            pe.wait_ge(S("e_w_low"), 4)
            ps = claim(pe, ("ewo", h)).rearrange("p (c n) -> p c n", c=2)
            for j in range(2):
                for k in range(8):
                    ins = split_matmul(ps[:, j, :], lambda a: e_out[a][:, k, j * P:(j + 1) * P],
                                       lambda b: e_wo[b][:, k, :], k == 0, k == 7)
            ins.then_inc(filled(("ewo", h)), 1)

        project(0)
        scores(0)
        values(0)
        project(1)
        outputs(0)
        scores(1)
        out_project(0)
        values(1)
        outputs(1)
        out_project(1)

        for h in range(NH):
            pe.wait_ge(S("f_z"), h + 1)
            to_fm("fT", h, Z)
        loaded("gw")
        for h in range(NH):
            written(pe, ("fT", h))
            tm(("fg", h), FT, h, gw, 2, 12)
        for e in range(NE + 1):
            if e < NE:
                pe.wait_ge(S("f_w_low"), e + 1)
                if e == 0:
                    pe.wait_ge(S("f_x_low"), 2)
                for f in range(4):
                    ps = claim(pe, ("f1", e, f))
                    for k in range(2):
                        ins = split_matmul(ps, lambda a: f_w1[e % 3][a][:, k, f * P:(f + 1) * P],
                                           lambda b: x_split[b][:, k, :], k == 0, k == 1)
                    ins.then_inc(filled(("f1", e, f)), 1)
            if e > 0:
                o = e - 1
                pe.wait_ge(S("f_low"), 4 * e)
                for h in range(NH):
                    ps = claim(pe, ("f2", o, h)).rearrange("p (c n) -> p c n", c=2)
                    for j in range(2):
                        at = (2 * h + j) * P
                        for k in range(4):
                            ins = split_matmul(ps[:, j, :], lambda a: f_hid[o % 2][a][:, k, at:at + P],
                                               lambda b: f_w2[o % 3][b][:, k, :], k == 0, k == 3)
                    ins.then_inc(filled(("f2", o, h)), 1)

    @block.scalar
    def _(act):
        chain = [0]
        steps_done = [0]
        norms = [0]

        def link(ins):
            chain[0] += 1
            ins.then_inc(S("act_chain"), 1)
            act.wait_ge(S("act_chain"), chain[0])

        def norm(h):
            norms[0] += 1
            act.wait_ge(S("var_ready"), norms[0])
            t = tiles[h]
            link(act.activation(lnv[:, t], mv[:, t, 1], ACT.Ln, bias=eps[:]))
            act.activation(rstd[:, t], lnv[:, t], ACT.Exp, scale=-0.5).then_inc(S("rstd_ready"), 1)

        def copy_fm(name, dst, bias=None, scale=1.0, func=ACT.Identity):
            ps = finished(act, name).rearrange("p (c n) -> p c n", c=2)
            if bias is None:
                act.activation(dst, ps, ACT.Copy, scale=scale).then_inc(taken(name), 1)
                return
            for c in range(2):
                ins = act.activation(dst[:, c, :], ps[:, c, :], func, bias=bias[c])
            ins.then_inc(taken(name), 1)

        def search():
            s = steps_done[0]
            steps_done[0] += 1
            act.wait_ge(S("cand_ready"), s + 1)
            act.activation(smask[:, 0, :], KEY[:, 0, :], ACT.Sign, bias=nbias[:], accum_out=signs[:])\
               .then_inc(S("signs_ready"), 1)

        def bias2(name, at=0):
            return [col(name, at), col(name, at + 1)]

        def keys_values(p, kb, n_s, b):
            if b >= 2:
                finished(act, (p + "S", b - 2, n_s - 1))
            copy_fm((p + "K", b), KT[:, b % 2], bias2(kb))
            if p == "a" and b and long_batch(b - 1):
                search()
            if b >= 2:
                finished(act, (p + "O", b - 2))
            copy_fm((p + "V", b), VB[:, b % 2])

        def attention(p, n_s, kb):
            if p == "d":
                keys_values(p, kb, n_s, 0)
            for b in range(NB):
                for s in range(n_s):
                    n = n_s * b + s
                    r = n % 4
                    if p == "a" and s == 0:
                        search()
                    act.wait_ge(S(p + "_max"), n + 1)
                    if b >= 2:
                        act.wait_ge(S(p + "_rinv"), n_s * (b - 1))
                    if p == "a":
                        ps = finished(act, ("aS", b, s))
                        if n >= 4:
                            finished(act, ("aPT", *divmod(n - 4, n_s)))
                    else:
                        ps = PR[:, r, :]
                    for pr in range(2):
                        j = 2 * s + pr
                        ins = act.activation(PR[:, r, pr * 256:(pr + 1) * 256], ps[:, pr * 256:(pr + 1) * 256],
                                             ACT.Exp, bias=nmx[:, b % 2, j:j + 1],
                                             accum_out=sums[:, b % 2, j:j + 1])
                    ins.then_inc(taken(("aS", b, s)) if p == "a" else S("d_p"), 1)
                if b + 1 < NB:
                    keys_values(p, kb, n_s, b + 1)
                elif p == "a":
                    search()

        TABLE = "natural_log_exp_and_others"
        act.preload_act_table_set(TABLE)
        act.wait_ge(S("eps_ready"), 1)
        act.wait_ge(S("ld_cols"), 16)
        norm(0)
        norm(1)
        for h in range(NH):
            copy_fm(("aT0", h), FT[:, :, half[h]])
        for h in range(NH):
            copy_fm(("av", h), FV[:, :, half[h]], bias2("v_b"))
        norm(0)
        norm(1)
        for h in range(NH):
            copy_fm(("aT1", h), FT[:, :, half[h]])
        keys_values("a", "k_b", 2, 0)
        search()
        attention("a", 2, "k_b")
        search()
        norm(0)
        norm(1)
        for h in range(NH):
            copy_fm(("aT2", h), FT[:, :, half[h]])
        search()
        for h in range(NH):
            for f in range(4):
                copy_fm(("af1", 0, h, f), a_hid[:, 2 * f:2 * f + 2, half[h]], bias2("lin1_b", 2 * f), func=ACT.Relu)
        search()
        norm(0)
        norm(0)
        norm(1)

        norm(1)
        for h in range(NH):
            copy_fm(("bT", h), FT[:, :, half[h]])
        for _ in range(5):
            search()
        for t in range(NT):
            act.activation(b_v[:, t, :], finished(act, ("bv", t)), ACT.Copy).then_inc(taken(("bv", t)), 1)
            act.activation(b_g[:, t, :], finished(act, ("bg", t)), ACT.Silu).then_inc(taken(("bg", t)), 1)
            if t % 2 == 1:
                search()
        act.preload_act_table_set(TABLE)
        search()
        search()

        def root(t):
            act.wait_ge(S("b_ms"), t + 1)
            link(act.activation(ms[:, t, :], ms[:, t, :], ACT.Ln, bias=eps[:], scale=1.0 / 128))
            act.activation(ms[:, t, :], ms[:, t, :], ACT.Exp, scale=-0.5).then_inc(S("b_rms"), 1)

        for t in range(NT):
            for bp in range(2):
                at = slice(bp * 64, bp * 64 + 64)
                ps = finished(act, ("bO", t, bp))
                act.activation(b_sq[at, t, :], ps[at, :], ACT.Square)
                act.activation(b_o[at, t, :], ps[at, :], ACT.Copy).then_inc(taken(("bO", t, bp)), 1)
            if t > 0:
                root(t - 1)
        root(NT - 1)
        for t in range(NT):
            ps = finished(act, ("bOT", t)).rearrange("p (c n) -> p c n", c=4)
            act.activation(b_ot[:, :, t * P:(t + 1) * P], ps, ACT.Copy).then_inc(taken(("bOT", t)), 1)
        search()

        norm(0)
        norm(1)
        for h in range(NH):
            copy_fm(("cT", h), FT[:, :, half[h]])
        norm(0)
        norm(1)
        BIASES = [lambda f: bias2("ffn_b1", 2 * f),
                  lambda f: [bp_col[:, 2 * f:2 * f + 1], bp_col[:, 2 * f + 1:2 * f + 2]]]

        def gelu(e, h, f):
            copy_fm(("c1", e, h, f), c_hid[e][:, 2 * f:2 * f + 2, half[h]], BIASES[e](f), func=ACT.Gelu_apprx_tanh)

        for h in range(NH):
            for f in range(4):
                gelu(0, h, f)
                if f % 2 == 0:
                    search()
            if h == 0:
                for g in range(NH):
                    copy_fm(("cT2", g), FV[:, :, half[g]])
                search()
        act.wait_ge(S("c_shifted"), 1)
        act.activation(lgt[:, :, 0:8], lgt[:, :, 0:8], ACT.Exp).then_inc(S("c_exp"), 1)
        act.wait_ge(S("perturbed"), 2)
        for h in range(NH):
            for f in range(4):
                gelu(1, h, f)
        act.preload_act_table_set(TABLE)

        norm(0)
        norm(1)
        for h in range(NH):
            copy_fm(("dT", h), FT[:, :, half[h]])
        attention("d", 4, "xk_b")

        def project(h):
            ps = finished(act, ("eT", h)).rearrange("p (c n) -> p c n", c=2)
            act.activation(x_split[0][:, :, half[h]], ps, ACT.Copy).then_inc(S("e_x_high"), 1)
            if h == 0:
                norm(1)
            for c in range(4):
                copy_fm(("eq", h, c), e_q[h][:, 2 * c:2 * c + 2, :], scale=0.125)
            for c in range(4):
                copy_fm(("ek", h, c), e_k[h][:, 2 * c:2 * c + 2, :])

        def probs_values(h):
            for t in (2 * h, 2 * h + 1):
                act.wait_ge(S("e_shifted"), t + 1)
                p2 = PR[:, 2 * (t % 2):2 * (t % 2) + 2, :]
                act.activation(p2, p2, ACT.Exp).then_inc(S("e_exp"), 1)
                for n in range(2):
                    ps = finished(act, ("ev", t, n))
                    act.activation(e_v[:, t % 2, n * 512:(n + 1) * 512], ps, ACT.Copy)\
                       .then_inc(taken(("ev", t, n)), 1)

        def outputs(h):
            if h:
                finished(act, ("ewo", h - 1))
            for t in (2 * h, 2 * h + 1):
                for bp in range(2):
                    ps = finished(act, ("eO", t, bp)).rearrange("p (c n) -> p c n", c=8)
                    at = (t % 2) * P + bp * SQ
                    act.activation(e_out[0][:, :, at:at + SQ], ps, ACT.Copy).then_inc(S("e_out_high"), 1)

        norm(0)
        project(0)
        probs_values(0)
        project(1)
        outputs(0)
        probs_values(1)
        norm(0)
        outputs(1)
        norm(1)

        for h in range(NH):
            ps = finished(act, ("fT", h)).rearrange("p (c n) -> p c n", c=2)
            act.activation(FT[:, :, half[h]], ps, ACT.Copy)
            act.activation(x_split[0][:, :, half[h]], ps, ACT.Copy).then_inc(taken(("fT", h)), 1)
        act.wait_ge(S("f_gap"), 1)
        act.activation(sm[:, 0:4], sm[:, 0:4], ACT.Exp).then_inc(S("f_exp"), 1)
        for e in range(NE):
            for f in range(4):
                ps = finished(act, ("f1", e, f))
                if e >= 2:
                    act.wait_ge(S("f_low"), 4 * e - 7 + f)
                    finished(act, ("f2", e - 2, 1))
                act.activation(f_act[e % 2][:, f, :], ps, ACT.Silu).then_inc(taken(("f1", e, f)), 1)
                written(act, ("f1", e, f))
                act.activation(f_hid[e % 2][0][:, f, :], f_act[e % 2][:, f, :], ACT.Copy)\
                   .then_inc(S("f_high"), 1)

    @block.vector
    def _(dve):
        chain = [0]
        norms = [0]
        parts = [0]
        perturbed = [0]
        scratch = [QD[:].rearrange("p a c h n -> p (a c h n)"), PT[:].rearrange("p a n -> p (a n)")]

        def link(ins):
            chain[0] += 1
            ins.then_inc(S("dve_chain"), 1)
            dve.wait_ge(S("dve_chain"), chain[0])

        def statistics(h, src):
            for t in (2 * h, 2 * h + 1):
                ins = dve.bn_stats(st[:, t, :], src[:, t, :])
            link(ins)
            for t in (2 * h, 2 * h + 1):
                ins = dve.bn_aggr(mv[:, t, :], st[:, t, :])
            norms[0] += 1
            ins.then_inc(S("var_ready"), 1)

        def normalise(h, src, dst, n, signal, gain=None, shift=None):
            dve.wait_ge(S("rstd_ready"), n)
            for t in (2 * h, 2 * h + 1):
                if gain is None:
                    ins = dve.tensor_scalar(dst[:, t, :], src[:, t, :], mv[:, t, 0:1], rstd[:, t:t + 1],
                                            ALU.subtract, ALU.mult)
                else:
                    link(dve.scalar_tensor_tensor(out=Y[:, t, :], in0=src[:, t, :], scalar=mv[:, t, 0:1],
                                                  in1=row(gain), op0=ALU.subtract, op1=ALU.mult))
                    ins = dve.scalar_tensor_tensor(out=dst[:, t, :], in0=Y[:, t, :], scalar=rstd[:, t:t + 1],
                                                   in1=row(shift), op0=ALU.mult, op1=ALU.add)
            if signal is None:
                link(ins)
            else:
                ins.then_inc(S(signal), 1)

        def norm_half(h, signal, src=X, dst=Z, gain=None, shift=None):
            statistics(h, src)
            normalise(h, src, dst, norms[0], signal, gain, shift)

        def plain_norm(signal, src=X, dst=Z, gain=None, shift=None):
            for h in range(NH):
                norm_half(h, signal, src, dst, gain, shift)

        def add_norm(name, h, signal, gain, shift):
            job = (*name, h)
            ps = finished(dve, job).rearrange("p (c n) -> p c n", c=2)
            y = Y[:, tiles[h], :]
            dve.tensor_tensor(y, ps, y, ALU.add).then_inc(taken(job), 1)
            written(dve, job)
            norm_half(h, signal, Y, Z, gain, shift)

        def add_bias(bias, signal):
            dve.wait_ge(S(signal), 2)
            link(dve.tensor_tensor(Y[:], Z[:], over(row(bias), 4), ALU.add))

        def split_weights(e):
            dve.wait_ge(S(f"ld_f{e % 2}"), 16 * (e // 2 + 1))
            if e >= 3:
                finished(dve, ("f2", e - 3, 1))
            dve.tensor_copy(f_split[e % 3][0], f_raw[e % 2]).then_inc(S("f_w_high"), 1)

        w1f, w2f = RC[:, 0:2048], RC[:, 2048:4096]
        b1c = cols[:, COL_AT["ffn_b1"]:COL_AT["ffn_b1"] + 8]
        b2c = cols[:, COL_AT["ffn_b2"]:COL_AT["ffn_b2"] + 2]
        srcs = [w1f, w2f, w1f, w2f, b1c, b2c, b1c, b2c]

        def key(q, phase):
            if q >= 4:
                return bkey[:, q - 4, 0:srcs[q].shape[1]]
            return KEY[:, q if phase else q % 2, :]

        def keys_high():
            for n in ("ffn_w1", "ffn_w2", "kwant"):
                dve.wait_ge(S("ld_" + n), 16)
            dve.wait_ge(S("ld_cols"), 16)
            link(dve.memset(bkey[:], 65535))
            for q in (0, 1, 4, 5, 6, 7):
                ins = dve.tensor_scalar(key(q, 0), srcs[q].bitcast(U16)[:, 1::2], 0x7FFF, None, ALU.bitwise_and)
            link(ins)
            dve.memset(cur[:], 0.0)
            dve.memset(base[:], 0.0)
            link(dve.tensor_copy(kleft[:], kwant[:]))

        def keys_low():
            dve.tensor_copy(thr[:, 0, :], cur[:])
            link(dve.tensor_tensor(kleft[:], kleft[:], base[:], ALU.subtract))
            dve.wait_ge(S("low_halves"), 2)
            other = RC[:, 5120:7168].bitcast(U16).rearrange("p (q n) -> p q n", q=2)
            for q in range(2):
                dve.tensor_scalar(other[:, q, :], KEY[:, q, :], cur[:, q + 2:q + 3], 65535.0, ALU.not_equal, ALU.mult)
                link(dve.tensor_scalar(KEY[:, q, :], KEY[:, q, :], cur[:, q:q + 1], 65535.0, ALU.not_equal, ALU.mult))
                link(dve.tensor_tensor(KEY[:, q, :], KEY[:, q, :], low_half[:, q, :], ALU.max))
                link(dve.tensor_tensor(KEY[:, q + 2, :], low_half[:, q, :], other[:, q, :], ALU.max))
            for q in range(4, 8):
                link(dve.tensor_scalar(key(q, 1), key(q, 0), cur[:, q:q + 1], 65535.0, ALU.not_equal, ALU.mult))
                link(dve.tensor_tensor(key(q, 1), key(q, 1), srcs[q].bitcast(U16)[:, 0::2], ALU.max))
            link(dve.memset(cur[:], 0.0))

        def bit(s):
            return float(1 << (NSTEP1 - 1 - s if s < NSTEP1 else N_SEARCH - 1 - s))

        def compare(s):
            if s == 0:
                keys_high()
            if s == NSTEP1:
                keys_low()
            phase = int(s >= NSTEP1)
            dve.tensor_scalar(cand[:], cur[:], bit(s), None, ALU.add)
            dve.tensor_scalar(nbias[:], cur[:, 0:1], -1.0, 0.5 - bit(s), ALU.mult, ALU.add).then_inc(S("cand_ready"), 1)
            dve.wait_ge(S("cand_ready"), s + 1)
            for q in range(1, 4):
                dve.tensor_scalar(smask[:, q, :], key(q, phase), cand[:, q:q + 1], None, ALU.is_lt)\
                   .then_inc(S("smask_ready"), 1)
            link(dve.tensor_tensor(below[:], bkey[:], each(cand[:, 4:8], 8), ALU.is_lt))
            dve.tensor_reduce(cnt[:, 4:8], below[:], AX.X, ALU.add)

        def search():
            s, summing = divmod(parts[0], 2)
            parts[0] += 1
            if not summing:
                dve.wait_ge(S("signs_ready"), s + 1)
                dve.tensor_scalar(cnt[:, 0:1], signs[:], -0.5, LIN * D / P / 2, ALU.mult, ALU.add)
                ps = finished(dve, ("cnt", s))
                dve.tensor_copy(cnt[:, 1:4], ps[:, 1:4]).then_inc(taken(("cnt", s)), 1)
                return
            ps = finished(dve, ("tot", s))
            dve.tensor_tensor(fewer[:], ps[:, 0:8], kleft[:], ALU.is_lt)
            dve.tensor_copy(totals[:], ps[:, 0:8]).then_inc(taken(("tot", s)), 1)
            written(dve, ("tot", s))
            link(dve.scalar_tensor_tensor(out=cur[:], in0=fewer[:], scalar=bit(s), in1=cur[:],
                                          op0=ALU.mult, op1=ALU.add))
            if s < NSTEP1:
                link(dve.tensor_tensor(totals[:], totals[:], base[:], ALU.subtract))
                link(dve.tensor_tensor(totals[:], totals[:], fewer[:], ALU.mult))
                link(dve.tensor_tensor(base[:], base[:], totals[:], ALU.add))
            if s + 1 < N_SEARCH:
                compare(s + 1)

        def bounds():
            link(dve.tensor_copy(thr[:, 1, :], cur[:]))
            hi, lo = bound[:].bitcast(I32), sm[:, 208:216].bitcast(I32)
            dve.tensor_copy(hi, thr[:, 0, :])
            link(dve.tensor_copy(lo, thr[:, 1, :]))
            link(dve.tensor_scalar(hi, hi, 16, None, ALU.logical_shift_left))
            link(dve.tensor_tensor(hi, hi, lo, ALU.bitwise_or))
            for a in (0, 4):
                low, apart = bound[:, a + 2:a + 4], sm[:, 216:218]
                link(dve.tensor_tensor(apart, bound[:, a:a + 2], low, ALU.is_gt))
                link(dve.tensor_tensor(low, low, apart, ALU.mult))
                link(dve.scalar_tensor_tensor(out=low, in0=apart, scalar=-1.0, in1=low, op0=ALU.add, op1=ALU.add))

        def perturb(src, dst, q):
            n = src.shape[1]
            t1, t2 = scratch[0][:, 0:n], scratch[1][:, 0:n]
            link(dve.tensor_scalar(t1.bitcast(I32), src.bitcast(I32), 0x7FFFFFFF, None, ALU.bitwise_and))
            link(dve.tensor_scalar(t2, t1, bound[:, q:q + 1], None, ALU.is_ge))
            link(dve.scalar_tensor_tensor(out=t2, in0=t1, scalar=bound[:, q + 2:q + 3], in1=t2,
                                          op0=ALU.is_le, op1=ALU.subtract))
            link(dve.scalar_tensor_tensor(out=t2, in0=t2, scalar=0.8, in1=src, op0=ALU.mult, op1=ALU.mult))
            dve.tensor_tensor(dst, src, t2, ALU.add).then_inc(S("perturbed"), 1)
            perturbed[0] += 1
            dve.wait_ge(S("perturbed"), perturbed[0])

        def attention(p, n_s, even, vb):

            def transposed(b, s):
                n = n_s * b + s
                ps = finished(dve, (p + "PT", b, s))
                if n >= 4:
                    finished(dve, (p + "O", (n - 4) // n_s))
                dve.tensor_copy(PT[:, n % 4, :], ps).then_inc(taken((p + "PT", b, s)), 1)

            def invert(b, s):
                if b >= 2:
                    dve.wait_ge(S(p + "_diag"), n_s * (b - 1))
                if p == "a":
                    written(dve, ("aS", b, s))
                else:
                    dve.wait_ge(S("d_p"), n_s * b + s + 1)
                dve.reciprocal(rinv[:, b % 2, 2 * s:2 * s + 2], sums[:, b % 2, 2 * s:2 * s + 2])\
                   .then_inc(S(p + "_rinv"), 1)

            for i in range(NB + 1):
                for s in range(n_s):
                    if i < NB:
                        n = n_s * i + s
                        ps = finished(dve, (p + "S", i, s)).rearrange("p (c n) -> p c n", c=2)
                        if p == "a":
                            if i >= 2:
                                written(dve, ("aS", i - 2, n_s - 1))
                            dve.tensor_reduce(nmx[:, i % 2, 2 * s:2 * s + 2], ps, AX.X, ALU.max, negate=True)\
                               .then_inc(S("a_max"), 1)
                        else:
                            if n >= 4:
                                finished(dve, ("dPT", *divmod(n - 4, n_s)))
                            for pr in range(2):
                                j = 2 * s + pr
                                ins = dve.tensor_tensor_reduce(
                                    PR[:, n % 4, pr * 256:(pr + 1) * 256], ps[:, pr, :], d_mask[:, i, :],
                                    rany[:, i:i + 1], -3.0e38, ALU.add, ALU.max, rmx[:, i % 2, j:j + 1])
                            ins.then_inc(taken(("dS", i, s)), 1)
                            written(dve, ("dS", i, s))
                            dve.tensor_scalar(nmx[:, i % 2, 2 * s:2 * s + 2], rmx[:, i % 2, 2 * s:2 * s + 2], -1.0,
                                              None, ALU.mult).then_inc(S("d_max"), 1)
                    if i < NB and s > 0:
                        invert(i, s - 1)
                    if i > 0:
                        transposed(i - 1, s)
                    if p == "a" and i < NB:
                        search()
                if i < NB:
                    invert(i, n_s - 1)
                if p == "a" and i < NB and long_batch(i):
                    search()
                if i > 0:
                    b = i - 1
                    ps = finished(dve, (p + "O", b)).rearrange("p (c g n) -> p c g n", c=4, g=2)
                    tok = slice(b * SQ, (b + 1) * SQ)
                    for c in range(2):
                        ins = dve.tensor_scalar(FT[:, c, tok], ps[:, c, 0, :], hmask[:, even:even + 1], col(vb, c),
                                                ALU.mult, ALU.add)
                    link(ins)
                    ins = dve.scalar_tensor_tensor(out=FT[:, :, tok], in0=ps[:, 0:2, 1, :],
                                                   scalar=hmask[:, even + 1:even + 2], in1=FT[:, :, tok],
                                                   op0=ALU.mult, op1=ALU.add)
                    ins.then_inc(taken((p + "O", b)), 1)
                if p == "a" and i < NB and long_batch(i):
                    search()
                if p == "d" and i in (1, 2):
                    high_part(i - 1)

        def high_part(i):
            if i == 2:
                finished(dve, ("dV", NB - 1))
            dve.wait_ge(S(("ld_eq_w", "ld_ek_w", "ld_ev_w", "ld_eo_w")[i]), 16)
            dve.tensor_copy(e_high[i], e_raw[i]).then_inc(S("e_w_high"), 1)

        def low_stream(h):
            dve.wait_ge(S("e_x_high"), h + 1)
            ps = finished(dve, ("eT", h)).rearrange("p (c n) -> p c n", c=2)
            dve.tensor_tensor(x_split[1][:, :, half[h]], ps, x_split[0][:, :, half[h]], ALU.subtract)\
               .then_inc(taken(("eT", h)), 1)

        dve.memset(eps[:], EPS).then_inc(S("eps_ready"), 1)
        dve.memset(onesb[:], 1.0).then_inc(S("ones_ready"), 1)
        dve.memset(onesf[:], 1.0).then_inc(S("ones_ready"), 1)

        for h in range(NH):
            dve.wait_ge(S(f"ld_x{h}"), 32)
            statistics(h, X)
        for h in range(NH):
            normalise(h, X, Z, h + 1, "a_z0")
        dve.wait_ge(S("ld_rows"), 16)
        add_bias("so_b", "a_z0")
        for h in range(NH):
            add_norm(("aso",), h, "a_z1", "ln1_g", "ln1_b")
        compare(0)
        search()
        dve.wait_ge(S("ld_cols"), 16)
        for h in range(NH):
            ps = finished(dve, ("aq", h)).rearrange("p (c n) -> p c n", c=2)
            for c in range(2):
                ins = dve.tensor_scalar(FV[:, c, half[h]], ps[:, c, :], col("q_b", c), 32.0 ** -0.5, ALU.add, ALU.mult)
            ins.then_inc(taken(("aq", h)), 1)
        search()
        add_bias("mo_b", "a_z1")
        dve.wait_ge(S("ld_hmask"), 16)
        attention("a", 2, 12, "cv_b")
        search()
        for h in range(NH):
            add_norm(("amo",), h, "a_z2", "ln2_g", "ln2_b")
        search()
        add_bias("lin2_b", "a_z2")
        for _ in range(3):
            search()
        for h in range(NH):
            add_norm(("af2", 0), h, None, "ln3_g", "ln3_b")
            ins = dve.tensor_tensor(X[:, tiles[h], :], X[:, tiles[h], :], Z[:, tiles[h], :], ALU.add)
            link(ins)
            norm_half(h, "b_z")
        search()

        dve.wait_ge(S("b_z"), 2)
        search()
        for n in ("rot", "decay"):
            dve.wait_ge(S("ld_" + n), 16)
        for h in range(NH):
            for a, b, dst, turned in (("bq", "bqs", FV, Y), ("bk", "bks", FK, Z)):
                ps = finished(dve, (a, h)).rearrange("p (c m s) -> p c m s", c=2, s=SQ)
                for c in range(2):
                    ins = dve.tensor_tensor(dst[:, c, half[h]].rearrange("p (m s) -> p m s", s=SQ), ps[:, c],
                                            over(rot[:, 0, :], 4), ALU.mult)
                ins.then_inc(taken((a, h)), 1)
                search()
                ps = finished(dve, (b, h)).rearrange("p (m s) -> p m s", s=SQ)
                y = turned[:, tiles[h], :].rearrange("p t (m s) -> p (t m) s", s=SQ)
                dve.tensor_tensor(y, ps, over(rot[:, 1, :], 8), ALU.mult).then_inc(taken((b, h)), 1)
                search()
        for t in range(NT):
            search()
        for t in range(NT):
            for hp in range(2):
                ps = finished(dve, ("bS", t, hp)).rearrange("p (c n) -> p c n", n=SQ)
                dst = PR[:, t, 0:256].rearrange("p (c g n) -> p c g n", c=2, g=2)[:, :, hp, :]
                dec = decay[:].rearrange("p (c g) n -> p c g n", g=2)[:, :, hp, :]
                dve.tensor_tensor(dst, ps[:, 0:2, :], dec, ALU.mult).then_inc(taken(("bS", t, hp)), 1)
            search()
        def squares(t):
            for bp in range(2):
                written(dve, ("bO", t, bp))
            dve.tensor_reduce(ms[:, t, :], b_sq[:, t, :].rearrange("p (a n) -> p a n", a=4), AX.X, ALU.add)\
               .then_inc(S("b_ms"), 1)

        squares(0)
        for t in range(NT):
            if t + 1 < NT:
                squares(t + 1)
            o4 = b_o[:, t, :].rearrange("p (a n) -> p a n", a=4)
            dve.wait_ge(S("b_rms"), t + 1)
            link(dve.tensor_tensor(o4, o4, each(ms[:, t, :], 128), ALU.mult))
            dve.wait_ge(S("b_gain"), t + 1)
            dve.tensor_tensor(b_o[:, t, :], b_o[:, t, :], b_g[:, t, :], ALU.mult).then_inc(S("b_gated"), 1)
        search()
        for h in range(NH):
            ps = finished(dve, ("bwo", h)).rearrange("p (c n) -> p c n", c=2)
            dve.tensor_tensor(X[:, tiles[h], :], X[:, tiles[h], :], ps, ALU.add).then_inc(taken(("bwo", h)), 1)
            written(dve, ("bwo", h))
            norm_half(h, "c_z")
        search()

        dve.wait_ge(S("c_z"), 2)
        plain_norm("c_y", Z, Y, "f_g", "f_b")
        for _ in range(6):
            search()
        for h in range(NH):
            ps = finished(dve, ("cr", h)).rearrange("p (c n) -> p c n", c=2)
            dve.tensor_tensor(lgt[:, tiles[h], 0:8], ps[:, :, 0:8], over(row("br"), 2), ALU.add)\
               .then_inc(taken(("cr", h)), 1)
            written(dve, ("cr", h))
        lg = lgt[:, :, 0:8]
        link(dve.tensor_reduce(sm[:, 16:20], lg, AX.X, ALU.max))
        dve.tensor_tensor(lg, lg, each(sm[:, 16:20], 8), ALU.subtract).then_inc(S("c_shifted"), 1)
        for _ in range(5):
            search()
        dve.wait_ge(S("c_exp"), 1)
        dve.tensor_reduce(sm[:, 20:24], lg, AX.X, ALU.add)
        link(dve.tensor_reduce(sm[:, 24:28], lgt[:, :, 1:8], AX.X, ALU.add))
        link(dve.reciprocal(sm[:, 20:24], sm[:, 20:24]))
        w_clean, w_others = sm[:, 32:36], sm[:, 36:40]
        dve.tensor_tensor(w_clean, lgt[:, :, 0], sm[:, 20:24], ALU.mult)
        link(dve.tensor_tensor(w_others, sm[:, 24:28], sm[:, 20:24], ALU.mult))
        bounds()
        perturb(w1f, RC[:, 4096:6144], 0)
        perturb(b1c, bp_col[:], 4)
        perturb(row("ffn_b2"), bp_row[:], 5)

        def add_expert(e, weight, b2):
            for t in range(NT):
                ins = dve.scalar_tensor_tensor(out=X[:, t, :], in0=b2, scalar=weight[:, t:t + 1], in1=X[:, t, :],
                                               op0=ALU.mult, op1=ALU.add)
            link(ins)
            for h in range(NH):
                ps = finished(dve, ("c2", e, h)).rearrange("p (c n) -> p c n", c=2)
                for t in (2 * h, 2 * h + 1):
                    ins = dve.scalar_tensor_tensor(out=X[:, t, :], in0=ps[:, t % 2, :],
                                                   scalar=weight[:, t:t + 1],
                                                   in1=X[:, t, :], op0=ALU.mult, op1=ALU.add)
                ins.then_inc(taken(("c2", e, h)), 1)
                written(dve, ("c2", e, h))
                if e:
                    norm_half(h, "d_z")

        add_expert(0, w_clean, row("ffn_b2"))
        perturb(w2f, RC[:, 6144:8192], 1)
        add_expert(1, w_others, bp_row[:])

        dve.wait_ge(S("d_z"), 2)
        link(dve.tensor_tensor(X[:], X[:], over(row("xo_b"), 4), ALU.add))
        dve.wait_ge(S("ld_mask"), 32)
        link(dve.tensor_scalar(d_mask, d_mask, 0.0, NEG, ALU.is_equal, ALU.mult))
        link(dve.tensor_reduce(rany[:], d_mask, AX.X, ALU.max))
        link(dve.tensor_scalar(rany[:], rany[:], 0.0, None, ALU.is_ge))
        for h in range(NH):
            ps = finished(dve, ("dq", h)).rearrange("p (c n) -> p c n", c=2)
            for c in range(2):
                ins = dve.tensor_scalar(FV[:, c, half[h]], ps[:, c, :], col("xq_b", c), 0.25, ALU.add, ALU.mult)
            ins.then_inc(taken(("dq", h)), 1)
        attention("d", 4, 14, "xv_b")
        for h in range(NH):
            ps = finished(dve, ("dmo", h)).rearrange("p (c n) -> p c n", c=2)
            xs = X[:, tiles[h], :]
            dve.tensor_tensor(xs, xs, ps, ALU.add).then_inc(taken(("dmo", h)), 1)
            written(dve, ("dmo", h))
            norm_half(h, "e_z")
            if h == 0:
                low_stream(0)

        dve.wait_ge(S("ld_rbias"), 16)
        dve.wait_ge(S("ld_causal"), 16)
        link(dve.tensor_tensor(e_bias, e_bias, over(e_causal, 8), ALU.add))
        def shift(h):
            for t in (2 * h, 2 * h + 1):
                p2 = PR[:, 2 * (t % 2):2 * (t % 2) + 2, :].rearrange("p a n -> p (a n)")
                if t >= 2:
                    finished(dve, ("ePT", t - 2, 1))
                for bp in range(2):
                    for hp in range(2):
                        at = slice(hp * 64, hp * 64 + 64)
                        ps = finished(dve, ("eS", t, bp, hp)).rearrange("p (c n) -> p c n", n=SQ)
                        dst = p2.rearrange("p (c g n) -> p c g n", c=8, g=2)[at, :, bp, :]
                        dve.tensor_tensor(dst, ps[at], e_bias[at], ALU.add).then_inc(taken(("eS", t, bp, hp)), 1)
                        written(dve, ("eS", t, bp, hp))
                pv = p2.rearrange("p (c n) -> p c n", n=SQ)
                mx = sm[:, 64 + 16 * (t % 2):80 + 16 * (t % 2)]
                link(dve.tensor_reduce(mx, pv, AX.X, ALU.max))
                dve.tensor_tensor(pv, pv, each(mx, SQ), ALU.subtract).then_inc(S("e_shifted"), 1)

        def normalised(h):
            for t in (2 * h, 2 * h + 1):
                p2 = PR[:, 2 * (t % 2):2 * (t % 2) + 2, :].rearrange("p a n -> p (a n)")
                pv = p2.rearrange("p (c n) -> p c n", n=SQ)
                mx = sm[:, 64 + 16 * (t % 2):80 + 16 * (t % 2)]
                dve.wait_ge(S("e_exp"), t + 1)
                link(dve.tensor_reduce(mx, pv, AX.X, ALU.add))
                link(dve.reciprocal(mx, mx))
                dve.tensor_tensor(pv, pv, each(mx, SQ), ALU.mult).then_inc(S("e_p"), 1)

        def transposed(h):
            for t in (2 * h, 2 * h + 1):
                for s in range(2):
                    ps = finished(dve, ("ePT", t, s))
                    if t >= 2:
                        finished(dve, ("eO", t - 2, 1))
                    dve.tensor_copy(PT[:, 2 * (t % 2) + s, :], ps).then_inc(taken(("ePT", t, s)), 1)

        def low_outputs(h):
            for t in (2 * h, 2 * h + 1):
                for bp in range(2):
                    dve.wait_ge(S("e_out_high"), 2 * t + bp + 1)
                    ps = finished(dve, ("eO", t, bp)).rearrange("p (c n) -> p c n", c=8)
                    at = slice((t % 2) * P + bp * SQ, (t % 2) * P + bp * SQ + SQ)
                    dve.tensor_tensor(e_out[1][:, :, at], ps, e_out[0][:, :, at], ALU.subtract)\
                       .then_inc(taken(("eO", t, bp)), 1)

        def add_outputs(h):
            ps = finished(dve, ("ewo", h)).rearrange("p (c n) -> p c n", c=2)
            dve.tensor_tensor(X[:, tiles[h], :], X[:, tiles[h], :], ps, ALU.add).then_inc(taken(("ewo", h)), 1)
            written(dve, ("ewo", h))

        high_part(2)
        high_part(3)
        shift(0)
        low_stream(1)
        normalised(0)
        transposed(0)
        low_outputs(0)
        shift(1)
        add_outputs(0)
        normalised(1)
        transposed(1)
        norm_half(0, "f_z")
        low_outputs(1)
        finished(dve, ("ev", 3, 1))
        split_weights(0)
        add_outputs(1)
        norm_half(1, "f_z")

        dve.wait_ge(S("f_z"), 2)
        split_weights(1)
        dve.wait_ge(S("ld_iota12"), 16)
        for h in range(NH):
            written(dve, ("fT", h))
            dve.tensor_tensor(x_split[1][:, :, half[h]], FT[:, :, half[h]], x_split[0][:, :, half[h]], ALU.subtract)\
               .then_inc(S("f_x_low"), 1)
        for h in range(NH):
            ps = finished(dve, ("fg", h)).rearrange("p (c n) -> p c n", c=2)
            dve.tensor_tensor(lgt[:, tiles[h], :], ps[:, :, 0:12], over(row("eb"), 2), ALU.add)\
               .then_inc(taken(("fg", h)), 1)
            written(dve, ("fg", h))
        for t in range(NT):
            link(dve.max(m8[:, t, :], lgt[:, t, :]))
            link(dve.max_index(i8[:, t, :], m8[:, t, :], lgt[:, t, :]))
        dve.tensor_tensor(sm[:, 0:4], m8[:, :, 1], m8[:, :, 0], ALU.subtract).then_inc(S("f_gap"), 1)
        link(dve.tensor_copy(i8f[:, :, 0:2], i8[:, :, 0:2]))
        dve.wait_ge(S("f_exp"), 1)
        link(dve.tensor_scalar(sm[:, 4:8], sm[:, 0:4], 1.0, None, ALU.add))
        link(dve.reciprocal(sm[:, 8:12], sm[:, 4:8]))
        link(dve.tensor_tensor(sm[:, 12:16], sm[:, 0:4], sm[:, 8:12], ALU.mult))
        for t in range(NT):
            dve.tensor_scalar(wgt[:, t, :], iota12[:], i8f[:, t, 0:1], sm[:, 8 + t:9 + t], ALU.is_equal, ALU.mult)
            link(dve.tensor_scalar(lgt[:, t, :], iota12[:], i8f[:, t, 1:2], sm[:, 12 + t:13 + t], ALU.is_equal,
                                   ALU.mult))
        link(dve.tensor_tensor(wgt[:], wgt[:], lgt[:], ALU.add))
        link(dve.tensor_reduce(sm[:, 16:20], wgt[:, :, 8:12], AX.X, ALU.add))
        for t in range(NT):
            ins = dve.scalar_tensor_tensor(out=X[:, t, :], in0=Z[:, t, :], scalar=sm[:, 16 + t:17 + t],
                                           in1=X[:, t, :], op0=ALU.mult, op1=ALU.add)
        link(ins)
        for e in range(NE + 1):
            if e < NE:
                if e >= 2:
                    finished(dve, ("f2", e - 2, 1))
                for f in range(4):
                    dve.wait_ge(S("f_high"), 4 * e + f + 1)
                    dve.tensor_tensor(f_hid[e % 2][1][:, f, :], f_act[e % 2][:, f, :],
                                      f_hid[e % 2][0][:, f, :], ALU.subtract).then_inc(S("f_low"), 1)
            if e > 0:
                for h in range(NH):
                    name = ("f2", e - 1, h)
                    ps = finished(dve, name).rearrange("p (c n) -> p c n", c=2)
                    for t in (2 * h, 2 * h + 1):
                        ins = dve.scalar_tensor_tensor(out=X[:, t, :], in0=ps[:, t % 2, :],
                                                       scalar=wgt[:, t, e - 1:e],
                                                       in1=X[:, t, :], op0=ALU.mult, op1=ALU.add)
                    ins.then_inc(taken(name), 1)
                    written(dve, name)
            if e + 2 < NE:
                split_weights(e + 2)

    @block.gpsimd
    def _(pool):
        def attention(p, n_h, n_s, m0):
            def block_diagonal(b):
                if b >= 2:
                    finished(pool, (p + "S", b - 2, n_s - 1))
                if b % 4 == 0:
                    written(pool, (p + "q", b // 4))
                tok = slice(b * SQ, (b + 1) * SQ)
                for c in range(2):
                    ins = pool.tensor_tensor(QD[:, b % 2, c, 0:n_h, :], over(FV[:, c, tok], n_h),
                                             each(hmask[:, m0:m0 + n_h], SQ), ALU.mult)
                ins.then_inc(S(p + "_qd_ready"), 1)

            def divisors(b):
                for s in range(n_s):
                    if b >= 2:
                        finished(pool, (p + "PT", b - 2, s))
                    pool.wait_ge(S(p + "_rinv"), n_s * b + s + 1)
                    for j in (2 * s, 2 * s + 1):
                        ins = pool.tensor_scalar(inv_diag[p][:, b % 2, j, :], ident[:], rinv[:, b % 2, j:j + 1], None,
                                                 ALU.mult)
                    ins.then_inc(S(p + "_diag"), 1)

            block_diagonal(0)
            for b in range(1, NB):
                block_diagonal(b)
                divisors(b - 1)
                if p == "d" and b in (3, 5):
                    low_part((b - 3) // 2)
            divisors(NB - 1)

        def low_part(i):
            pool.wait_ge(S("e_w_high"), i + 1)
            pool.tensor_tensor(e_low[i], e_raw[i], e_high[i], ALU.subtract).then_inc(S("e_w_low"), 1)

        for q, name in ((0, "ffn_w1"), (1, "ffn_w2")):
            pool.wait_ge(S("ld_" + name), 16)
            src = RC[:, 2048 * q:2048 * q + 2048].bitcast(U16)[:, 0::2]
            pool.tensor_copy(low_half[:, q, :], src).then_inc(S("low_halves"), 1)
        pool.wait_ge(S("ld_hmask"), 16)
        pool.wait_ge(S("ld_ident"), 16)
        attention("a", 4, 2, 0)
        for h in range(NH):
            for b, dst, turned in (("bqs", FV, Y), ("bks", FK, Z)):
                written(pool, (b, h))
                d = dst[:, :, half[h]]
                pool.tensor_tensor(d, d, turned[:, tiles[h], :], ALU.add)\
                    .then_inc(S("b_qk"), 1)
        pool.wait_ge(S("ld_rows"), 16)
        for t in range(NT):
            written(pool, ("bg", t))
            g4 = b_g[:, t, :].rearrange("p (a n) -> p a n", a=4)
            pool.tensor_tensor(g4, g4, over(row("gn"), 4), ALU.mult).then_inc(S("b_gain"), 1)
        attention("d", 8, 4, 4)
        for i in (2, 3):
            low_part(i)
        for e in range(NE):
            pool.wait_ge(S("f_w_high"), e + 1)
            pool.tensor_tensor(f_split[e % 3][1], f_raw[e % 2], f_split[e % 3][0], ALU.subtract)\
                .then_inc(S("f_w_low"), 1)


def _bucket(rel, num_buckets=32, max_distance=128):
    nb = num_buckets // 2
    buckets = (rel > 0).astype(np.int32) * nb
    rel_abs = np.abs(rel)
    max_exact = nb // 2
    large = max_exact + (np.log(np.maximum(rel_abs, 1).astype(np.float32) / np.float32(max_exact))
                         / np.float32(np.log(max_distance / max_exact)) * (nb - max_exact)).astype(np.int32)
    return buckets + np.where(rel_abs < max_exact, rel_abs, np.minimum(large, nb - 1))


def kernel(**inputs):
    import concourse.bacc as _bacc
    from concourse.bass_utils import run_bass_kernel_spmd as _run

    I = {k: np.asarray(v) for k, v in inputs.items()}
    f32 = np.float32

    def kmajor(w):
        k, n = w.shape
        return np.ascontiguousarray(w.reshape(k // P, P, n).transpose(1, 0, 2))

    a = {}
    a["x"] = np.ascontiguousarray(I["x"].reshape(T, D))
    a["ctx"] = kmajor(I["ctx_1024"].reshape(NB * SK, D).T)
    a["mask"] = np.ascontiguousarray(I["mask_Bx1xSxS2_ff1"][:, 0].transpose(1, 0, 2))
    qkv, inp = I["L0_xattn_qkv_w"], I["L0_xattn_in_proj_w"]
    a["v_w"] = kmajor(qkv[512:].T)
    a["so_w"] = kmajor(I["L0_xattn_sa_out_w"].T)
    a["q_w"], a["k_w"], a["cv_w"] = (kmajor(inp[256 * i:256 * i + 256].T) for i in range(3))
    a["mo_w"] = kmajor(I["L0_xattn_mha_out_w"].T)
    a["lin1_w"] = kmajor(I["L0_xattn_lin1_w"].T)
    a["lin2_w"] = kmajor(I["L0_xattn_lin2_w"].T)
    swap = (np.arange(256) // 64) * 64 + (np.arange(256) % 64 + 32) % 64
    a["rq_w"], a["rk_w"] = kmajor(I["L0_attn_Wq"]), kmajor(I["L0_attn_Wk"])
    a["rqs_w"], a["rks_w"] = kmajor(I["L0_attn_Wq"][:, swap]), kmajor(I["L0_attn_Wk"][:, swap])
    a["rv_w"], a["rg_w"], a["ro_w"] = (kmajor(I["L0_attn_W" + n]) for n in "vgo")
    a["ffn_w1"], a["ffn_w2"] = kmajor(I["L0_ffn_W1"]), kmajor(I["L0_ffn_W2"])
    a["Wr"] = kmajor(I["L0_ffn_Wr"])
    for n in "qkv":
        a[f"x{n}_w"] = kmajor(I["L1_xattn_W" + n].transpose(1, 0, 2).reshape(D, D))
        a[f"e{n}_w"] = kmajor(I["L1_attn_W" + n].T)
    a["xo_w"] = kmajor(I["L1_xattn_Wo"])
    a["eo_w"] = kmajor(I["L1_attn_Wo"].T)
    a["gw"] = kmajor(I["L1_ffn_gate_w"].T)
    fw1 = I["L1_ffn_w1"].transpose(0, 2, 1).reshape(NE, 2, P, DFF).transpose(0, 2, 1, 3)
    fw2 = I["L1_ffn_w2"].transpose(0, 2, 1).reshape(NE, 4, P, D).transpose(0, 2, 1, 3)
    a["fw"] = np.concatenate([fw1.reshape(NE, P, -1), fw2.reshape(NE, P, -1)], axis=2)
    colv = {"v_b": I["L0_xattn_qkv_b"][512:], "q_b": I["L0_xattn_in_proj_b"][:256],
            "k_b": I["L0_xattn_in_proj_b"][256:512], "cv_b": I["L0_xattn_in_proj_b"][512:],
            "lin1_b": I["L0_xattn_lin1_b"], "ffn_b1": I["L0_ffn_b1"], "ffn_b2": I["L0_ffn_b2"],
            "xq_b": I["L1_xattn_bq"].reshape(-1), "xk_b": I["L1_xattn_bk"].reshape(-1),
            "xv_b": I["L1_xattn_bv"].reshape(-1)}
    a["cols"] = np.ascontiguousarray(np.concatenate([colv[n].reshape(-1, P).T for n in COLS], axis=1))
    rowv = {"so_b": I["L0_xattn_sa_out_b"], "ln1_g": I["L0_xattn_ln1_g"], "ln1_b": I["L0_xattn_ln1_b"],
            "mo_b": I["L0_xattn_mha_out_b"], "ln2_g": I["L0_xattn_ln2_g"], "ln2_b": I["L0_xattn_ln2_b"],
            "lin2_b": I["L0_xattn_lin2_b"], "ln3_g": I["L0_xattn_ln3_g"], "ln3_b": I["L0_xattn_ln3_b"],
            "gn": I["L0_attn_gn_weight"], "f_g": I["L0_ffn_ln_gamma"], "f_b": I["L0_ffn_ln_beta"],
            "ffn_b2": I["L0_ffn_b2"], "xo_b": I["L1_xattn_bo"], "br": I["L0_ffn_br"],
            "eb": I["L1_ffn_expert_bias"]}
    a["rows"] = np.ascontiguousarray(np.concatenate([rowv[n] for n in ROWS])[None, :])
    p = np.arange(P)
    a["ident"] = np.eye(P, dtype=f32)
    a["hmask"] = np.concatenate([p[:, None] // 32 == np.arange(4), p[:, None] // 16 == np.arange(8),
                                 p[:, None] // 32 % 2 == np.arange(2), p[:, None] // 16 % 2 == np.arange(2)],
                                1).astype(f32)
    inv_freq = f32(1.0) / np.power(f32(10000.0), np.arange(0, 64, 2, dtype=f32) / f32(64))
    ang = (np.arange(SQ, dtype=f32)[None, :] * inv_freq[p % 32][:, None]).astype(f32)
    sign = np.where(p % 64 < 32, -1.0, 1.0).astype(f32)[:, None]
    a["rot"] = np.ascontiguousarray(np.stack([np.cos(ang), np.sin(ang) * sign], 1).astype(f32))
    gamma = 1.0 - np.exp2(-5.0 - np.arange(4))
    j, i = (p % 64)[:, None, None], np.arange(SQ)[None, None, :]
    a["decay"] = np.where(i >= j, gamma[None, :, None] ** np.maximum(i - j, 0) / 8.0, 0.0).astype(f32)
    a["iota12"] = np.tile(np.arange(12, dtype=f32), (P, 1))
    ranks = []
    for size in (LIN * D, LIN * D, LIN, D):
        k = max(1, int(size * 0.1 / 2))
        ranks.append((size - k + 1, k))
    want = [ranks[0][0], ranks[1][0], ranks[0][1], ranks[1][1], ranks[2][0], ranks[3][0], ranks[2][1], ranks[3][1]]
    a["kwant"] = np.tile(np.array(want, f32), (P, 1))
    rel = np.arange(SQ)[:, None] - np.arange(SQ)[None, :]
    e = I["L1_attn_rel_emb"][_bucket(rel)]
    a["rbias"] = np.ascontiguousarray(e.reshape(SQ, SQ, 8, 2).transpose(3, 0, 2, 1).reshape(P, 8, SQ))
    a["causal"] = np.where(rel[p % 64] < 0, CAUSAL_NEG, 0.0).astype(f32)

    nc = _bacc.Bacc("TRN2", target_bir_lowering=False, num_devices=1)
    A = {n: nc.dram_tensor(f"in_{n}", v.shape, mybir.dt.from_np(v.dtype), kind="ExternalInput").ap()
         for n, v in a.items()}
    out = nc.dram_tensor("out_x", (T, D), F32, kind="ExternalOutput").ap()
    build(nc, A, out)
    r = _run(nc, [{f"in_{n}": v for n, v in a.items()}], core_ids=[0])
    return r.results[0]["out_x"].reshape(NB, SQ, D)
```
